# Optimizing a Trainium2 kernel written in Bass

```python
import numpy as np
import jax
import jax.numpy as jnp

def _softmax(x, axis=-1):
    return jax.nn.softmax(x, axis=axis)

def _gelu(x):
    return jax.nn.gelu(x, approximate=True)

def _silu(x):
    return jax.nn.silu(x)

def _sigmoid(x):
    return jax.nn.sigmoid(x)

def _layernorm(x, axis=-1, eps=1e-05):
    m = jnp.mean(x, axis=axis, keepdims=True)
    v = jnp.var(x, axis=axis, keepdims=True)
    return (x - m) / jnp.sqrt(v + eps)

def _scatter_add(tgt, idx, src, axis=0):
    return tgt.at[idx].add(src)

def _segment_sum(src, seg, n):
    return jax.ops.segment_sum(src, seg, n)
kernel_name = 'mk_gnn_preln_d4_gnn_r64_c21e0c'

def setup_inputs(seed: int=0):
    np.random.seed(seed)
    _w = jnp.asarray

    def _rec_inputs():
        import jax
        import jax.numpy as jnp
        _gk = jax.random.key(seed)
        x = -0.0004402 + 1 * jax.random.normal(jax.random.fold_in(_gk, 1), (100000, 16), jnp.float32)
        src = jax.random.randint(jax.random.fold_in(_gk, 2), (50000,), 0, 100000, jnp.int32)
        dst = jax.random.randint(jax.random.fold_in(_gk, 3), (50000,), 0, 100000, jnp.int32)
        _o = jnp.argsort(dst, stable=True)
        src = src[_o]
        dst = dst[_o]
        edge_attr_16 = -3.57403e-05 + 0.999761 * jax.random.normal(jax.random.fold_in(_gk, 12), (50000, 16), jnp.float32)
        edge_attr_8 = -0.00010739 + 0.99994 * jax.random.normal(jax.random.fold_in(_gk, 13), (50000, 8), jnp.float32)
        edge_weight = jax.random.uniform(jax.random.fold_in(_gk, 15), (50000,), jnp.float32, 0.0, 1)
        return (x, src, dst, edge_attr_16, edge_attr_8, edge_weight)
    x, src, dst, edge_attr_16, edge_attr_8, edge_weight = _rec_inputs()

    def _L0_gnn_setup():
        import jax, jax.numpy as jnp
        import numpy as np
        N_NODES = 30000
        N_EDGES = 300000
        IN_FEATS = 16
        OUT_FEATS = 16
        EDGE_DIM = 16
        key = jax.random.key(seed)
        ks = jax.random.split(key, 8)
        feat = jax.random.normal(ks[0], (N_NODES, IN_FEATS), dtype=jnp.float32)
        efeat = jax.random.normal(ks[1], (N_EDGES, EDGE_DIM), dtype=jnp.float32)
        W_msg = jax.random.normal(ks[2], (EDGE_DIM, IN_FEATS * OUT_FEATS), dtype=jnp.float32) * 0.1
        b_msg = jnp.zeros((IN_FEATS * OUT_FEATS,), dtype=jnp.float32)
        W_attn = jax.random.normal(ks[3], (EDGE_DIM, IN_FEATS * OUT_FEATS), dtype=jnp.float32) * 0.1
        b_attn = jnp.zeros((IN_FEATS * OUT_FEATS,), dtype=jnp.float32)
        src = jax.random.randint(ks[4], (N_EDGES,), 0, N_NODES, dtype=jnp.int32)
        dst = jax.random.randint(ks[5], (N_EDGES,), 0, N_NODES, dtype=jnp.int32)
        return {'feat': feat, 'efeat': efeat, 'W_msg': W_msg, 'b_msg': b_msg, 'W_attn': W_attn, 'b_attn': b_attn, 'src': src, 'dst': dst}
    _L0_gnn_all = _L0_gnn_setup()
    _L0_gnn_in = {k: v for k, v in _L0_gnn_all.items() if k in ('W_msg', 'b_msg', 'W_attn', 'b_attn')}
    del _L0_gnn_all

    def _L1_gnn_setup():
        import jax, jax.numpy as jnp
        import numpy as np
        N_NODES = 100000
        N_EDGES = 50000
        DIM = 16
        B, K, C, D, E, H = (0.1, 5.0, 1.0, 5.0, 0.9, 0.1)
        E_ = E
        key = jax.random.key(seed)
        k1, k2, k3, k4 = jax.random.split(key, 4)
        x = jax.random.uniform(k1, (N_NODES, DIM), dtype=jnp.float32)
        edge_src = jax.random.randint(k2, (N_EDGES,), 0, N_NODES, dtype=jnp.int32)
        edge_dst = jax.random.randint(k3, (N_EDGES,), 0, N_NODES, dtype=jnp.int32)
        edge_vals = jax.random.uniform(k4, (N_EDGES,), dtype=jnp.float32)
        return {'x': x, 'edge_src': edge_src, 'edge_dst': edge_dst, 'edge_vals': edge_vals}
    _L1_gnn_all = _L1_gnn_setup()
    _L1_gnn_in = {k: v for k, v in _L1_gnn_all.items() if k in ()}
    del _L1_gnn_all

    def _L2_gnn_setup():
        import jax, jax.numpy as jnp
        import numpy as np
        N_NODES = 100000
        N_EDGES = 25000
        IN_DIM = 16
        OUT_DIM = 16
        EDGE_DIM = 8
        key = jax.random.key(seed)
        ks = jax.random.split(key, 7)
        x = jax.random.normal(ks[0], (N_NODES, IN_DIM), dtype=jnp.float32)
        edge_attr = jax.random.normal(ks[1], (N_EDGES, EDGE_DIM), dtype=jnp.float32)
        root_w = jax.random.normal(ks[2], (IN_DIM, OUT_DIM), dtype=jnp.float32) * 0.1
        root_b = jax.random.normal(ks[3], (OUT_DIM,), dtype=jnp.float32) * 0.1
        edge_w = jax.random.normal(ks[4], (EDGE_DIM, OUT_DIM * IN_DIM), dtype=jnp.float32) * 0.1
        edge_b = jax.random.normal(ks[5], (OUT_DIM * IN_DIM,), dtype=jnp.float32) * 0.1
        edge_index = jax.random.randint(ks[6], (2, N_EDGES), 0, N_NODES, dtype=jnp.int64)
        return {'x': x, 'edge_attr': edge_attr, 'root_w': root_w, 'root_b': root_b, 'edge_w': edge_w, 'edge_b': edge_b, 'edge_index': edge_index}
    _L2_gnn_all = _L2_gnn_setup()
    _L2_gnn_in = {k: v for k, v in _L2_gnn_all.items() if k in ('root_w', 'root_b', 'edge_w', 'edge_b')}
    del _L2_gnn_all

    def _L3_gnn_setup():
        import jax, jax.numpy as jnp
        import numpy as np
        N_NODES = 50000
        N_EDGES = 12500
        D_IN = 16

        def gcn_conv(x, edge_index, W, b, n_nodes):
            h = x @ W
            src = jnp.concatenate([edge_index[0], jnp.arange(n_nodes)])
            dst = jnp.concatenate([edge_index[1], jnp.arange(n_nodes)])
            deg = jax.ops.segment_sum(jnp.ones_like(dst, dtype=h.dtype), dst, num_segments=n_nodes)
            deg_inv_sqrt = jnp.where(deg > 0, jax.lax.rsqrt(deg), 0.0)
            norm = deg_inv_sqrt[src] * deg_inv_sqrt[dst]
            msg = h[src] * norm[:, None]
            out = jax.ops.segment_sum(msg, dst, num_segments=n_nodes)
            return out + b
        key = jax.random.key(seed)
        ks = jax.random.split(key, 16)
        d = D_IN
        x = jax.random.normal(ks[0], (N_NODES, d), dtype=jnp.float32)
        edge_index = jax.random.randint(ks[1], (2, N_EDGES), 0, N_NODES, dtype=jnp.int64)

        def glorot(k, fan_in, fan_out):
            s = (6.0 / (fan_in + fan_out)) ** 0.5
            return jax.random.uniform(k, (fan_in, fan_out), jnp.float32, -s, s)
        return {'x': x, 'edge_index': edge_index, 'W1': glorot(ks[2], d, 2 * d), 'b1': jnp.zeros((2 * d,), jnp.float32), 'W2': glorot(ks[3], 2 * d, 4 * d), 'b2': jnp.zeros((4 * d,), jnp.float32), 'W3': glorot(ks[4], 4 * d, 8 * d), 'b3': jnp.zeros((8 * d,), jnp.float32), 'Wl1': glorot(ks[5], 8 * d, 4 * d), 'bl1': jnp.zeros((4 * d,), jnp.float32), 'Wl2': glorot(ks[6], 4 * d, 2 * d), 'bl2': jnp.zeros((2 * d,), jnp.float32), 'Wl3': glorot(ks[7], 2 * d, d), 'bl3': jnp.zeros((d,), jnp.float32)}
    _L3_gnn_all = _L3_gnn_setup()
    _L3_gnn_in = {k: v for k, v in _L3_gnn_all.items() if k in ('W1', 'b1', 'W2', 'b2', 'W3', 'b3', 'Wl1', 'bl1', 'Wl2', 'bl2', 'Wl3', 'bl3')}
    del _L3_gnn_all
    return {'x': x, 'src': src, 'dst': dst, 'edge_attr_16': edge_attr_16, 'edge_attr_8': edge_attr_8, 'edge_weight': edge_weight, 'L0_gnn_W_msg': _L0_gnn_in['W_msg'], 'L0_gnn_b_msg': _L0_gnn_in['b_msg'], 'L0_gnn_W_attn': _L0_gnn_in['W_attn'], 'L0_gnn_b_attn': _L0_gnn_in['b_attn'], 'L2_gnn_root_w': _L2_gnn_in['root_w'], 'L2_gnn_root_b': _L2_gnn_in['root_b'], 'L2_gnn_edge_w': _L2_gnn_in['edge_w'], 'L2_gnn_edge_b': _L2_gnn_in['edge_b'], 'L3_gnn_W1': _L3_gnn_in['W1'], 'L3_gnn_b1': _L3_gnn_in['b1'], 'L3_gnn_W2': _L3_gnn_in['W2'], 'L3_gnn_b2': _L3_gnn_in['b2'], 'L3_gnn_W3': _L3_gnn_in['W3'], 'L3_gnn_b3': _L3_gnn_in['b3'], 'L3_gnn_Wl1': _L3_gnn_in['Wl1'], 'L3_gnn_bl1': _L3_gnn_in['bl1'], 'L3_gnn_Wl2': _L3_gnn_in['Wl2'], 'L3_gnn_bl2': _L3_gnn_in['bl2'], 'L3_gnn_Wl3': _L3_gnn_in['Wl3'], 'L3_gnn_bl3': _L3_gnn_in['bl3']}

def reference(x, src, dst, edge_attr_16, edge_attr_8, edge_weight, L0_gnn_W_msg, L0_gnn_b_msg, L0_gnn_W_attn, L0_gnn_b_attn, L2_gnn_root_w, L2_gnn_root_b, L2_gnn_edge_w, L2_gnn_edge_b, L3_gnn_W1, L3_gnn_b1, L3_gnn_W2, L3_gnn_b2, L3_gnn_W3, L3_gnn_b3, L3_gnn_Wl1, L3_gnn_bl1, L3_gnn_Wl2, L3_gnn_bl2, L3_gnn_Wl3, L3_gnn_bl3):
    import jax
    import jax.numpy as jnp

    def _L0_gnn_ref(feat, efeat, W_msg, b_msg, W_attn, b_attn, src, dst):
        import jax, jax.numpy as jnp
        import numpy as np
        N_NODES = 30000
        N_EDGES = 300000
        IN_FEATS = 16
        OUT_FEATS = 16
        EDGE_DIM = 16
        N, in_f = feat.shape
        E = efeat.shape[0]
        w_m = (efeat @ W_msg + b_msg).reshape(E, in_f, -1)
        w_a = (efeat @ W_attn + b_attn).reshape(E, in_f, -1)
        h_src = feat[src][:, :, None]
        e1 = w_m * h_src
        e2 = w_a * h_src
        seg_max = jax.ops.segment_max(e2, dst, num_segments=N)
        ex = jnp.exp(e2 - seg_max[dst])
        denom = jax.ops.segment_sum(ex, dst, num_segments=N)
        attn = ex / denom[dst]
        ft = jax.ops.segment_sum(e1 * attn, dst, num_segments=N)
        return ft.sum(axis=1)

    def _L1_gnn_ref(x, edge_src, edge_dst, edge_vals):
        import jax, jax.numpy as jnp
        import numpy as np
        N_NODES = 100000
        N_EDGES = 50000
        DIM = 16
        B, K, C, D, E, H = (0.1, 5.0, 1.0, 5.0, 0.9, 0.1)
        E_ = E
        n = x.shape[0]
        f = B + x * (1.0 - x / K) * (x / C - 1.0)
        xi = x[edge_src]
        xj = x[edge_dst]
        msg = edge_vals[:, None] * xi * xj / (D + E_ * xi + H * xj)
        f = f + jax.ops.segment_sum(msg, edge_src, num_segments=n)
        return f

    def _L2_gnn_ref(x, edge_attr, root_w, root_b, edge_w, edge_b, edge_index):
        import jax, jax.numpy as jnp
        import numpy as np
        N_NODES = 100000
        N_EDGES = 25000
        IN_DIM = 16
        OUT_DIM = 16
        EDGE_DIM = 8
        src = edge_index[0]
        dst = edge_index[1]
        weights = (edge_attr @ edge_w + edge_b).reshape(-1, OUT_DIM, IN_DIM)
        msg = jnp.einsum('eoi,ei->eo', weights, x[src])
        out = x @ root_w + root_b
        out = out.at[dst].add(msg)
        return out

    def _L3_gnn_ref(x, edge_index, W1, b1, W2, b2, W3, b3, Wl1, bl1, Wl2, bl2, Wl3, bl3):
        import jax, jax.numpy as jnp
        import numpy as np
        N_NODES = 50000
        N_EDGES = 12500
        D_IN = 16

        def gcn_conv(x, edge_index, W, b, n_nodes):
            h = x @ W
            src = jnp.concatenate([edge_index[0], jnp.arange(n_nodes)])
            dst = jnp.concatenate([edge_index[1], jnp.arange(n_nodes)])
            deg = jax.ops.segment_sum(jnp.ones_like(dst, dtype=h.dtype), dst, num_segments=n_nodes)
            deg_inv_sqrt = jnp.where(deg > 0, jax.lax.rsqrt(deg), 0.0)
            norm = deg_inv_sqrt[src] * deg_inv_sqrt[dst]
            msg = h[src] * norm[:, None]
            out = jax.ops.segment_sum(msg, dst, num_segments=n_nodes)
            return out + b
        n = x.shape[0]
        out = jax.nn.relu(gcn_conv(x, edge_index, W1, b1, n))
        out = jax.nn.relu(gcn_conv(out, edge_index, W2, b2, n))
        out = jax.nn.relu(gcn_conv(out, edge_index, W3, b3, n))
        out = jax.nn.relu(out @ Wl1 + bl1)
        out = jax.nn.relu(out @ Wl2 + bl2)
        out = jax.nn.relu(out @ Wl3 + bl3)
        return out
    edge_index = jnp.stack([src, dst])
    h = jnp.maximum(_layernorm(x, axis=-1), 0.0)
    x = x + _L0_gnn_ref(h, edge_attr_16, L0_gnn_W_msg, L0_gnn_b_msg, L0_gnn_W_attn, L0_gnn_b_attn, src, dst)
    h = jnp.maximum(_layernorm(x, axis=-1), 0.0)
    x = x + _L1_gnn_ref(h, src, dst, edge_weight)
    h = jnp.maximum(_layernorm(x, axis=-1), 0.0)
    x = x + _L2_gnn_ref(h, edge_attr_8, L2_gnn_root_w, L2_gnn_root_b, L2_gnn_edge_w, L2_gnn_edge_b, edge_index)
    h = jnp.maximum(_layernorm(x, axis=-1), 0.0)
    x = x + _L3_gnn_ref(h, edge_index, L3_gnn_W1, L3_gnn_b1, L3_gnn_W2, L3_gnn_b2, L3_gnn_W3, L3_gnn_b3, L3_gnn_Wl1, L3_gnn_bl1, L3_gnn_Wl2, L3_gnn_bl2, L3_gnn_Wl3, L3_gnn_bl3)
    return x

_drawn_inputs = setup_inputs


def setup_inputs(seed=0):
    import zlib

    import numpy as np

    out = dict(_drawn_inputs(seed))
    spreads = {'L0_gnn_b_msg': (0.0, 0.1),
     'L0_gnn_b_attn': (0.0, 0.632),
     'L3_gnn_b1': (0.0, 0.8),
     'L3_gnn_b2': (0.0, 0.8),
     'L3_gnn_b3': (0.0, 0.1),
     'L3_gnn_bl1': (0.0, 0.299),
     'L3_gnn_bl2': (0.0, 0.297),
     'L3_gnn_bl3': (0.0, 0.482)}
    factors = {'edge_weight': 4.368}
    for name, (base, spread) in spreads.items():
        noise = np.random.default_rng([zlib.crc32(name.encode()), seed]).standard_normal(out[name].shape)
        drawn = base * np.exp(spread * noise) if base else spread * noise
        out[name] = jnp.asarray(drawn.astype(out[name].dtype))
    for name, factor in factors.items():
        out[name] = (out[name] * factor).astype(out[name].dtype)
    return out
```

```python
from contextlib import ExitStack

import concourse.bass as bass
from concourse import mybir

ALU = mybir.AluOpType
ACT = mybir.ActivationFunctionType
AX = mybir.AxisListType
F32 = mybir.dt.float32
BF16 = mybir.dt.bfloat16
I32 = mybir.dt.int32

P = 128
D = 16
N, E = 100000, 50000
NT = -(-N // (P * 56)) * 56
ET = -(-E // (P * 28)) * 28
NP, EP = NT * P, ET * P
G = 14
EC = ET // G
HG = G // 2
TG = 7
KB = TG * D + 1
A0W = D + 2
FW = D + D + 2 * D + 4 * D
FAR = 1 << 20
PEN = -1.0e30
EPS = 1e-5
DMA = 16


class Steps:

    def __init__(self, eng, sem, per_pass=0):
        self.eng, self.sem, self.per_pass, self.base, self.k = eng, sem, per_pass, 0, 0

    def start_pass(self, i):
        self.base, self.k = i * self.per_pass, 0

    def end_pass(self):
        assert self.k == self.per_pass, f"{self.k} steps in a pass, not {self.per_pass}"

    def did(self, ins):
        ins.then_inc(self.sem, 1)
        self.k += 1

    def wait(self):
        self.eng.wait_ge(self.sem, self.base + self.k)


def passes(eng, n, last_apart=False):
    yield 0, False
    with eng.Fori(1, n - 1 if last_apart else n) as i:
        yield i, False
    if last_apart:
        yield n - 1, True


def settle(core, eng):
    eng.sem_inc(core.settled, 1)


def cols(start, n):
    return bass.ds(start, n)


def over(ap, w):
    return ap.rearrange("p (n o) -> p n o", o=1).to_broadcast([ap.shape[0], ap.shape[1], w])


def centre(nc, st, x, xc, sq, s, var, var_ready, x_read=None):
    v = nc.vector
    st.did(v.tensor_reduce(s, x, AX.X, ALU.add))
    st.wait()
    ins = v.scalar_tensor_tensor(xc, over(s, D), -1.0 / D, x, ALU.mult, ALU.add)
    if x_read:
        ins.then_inc(x_read[0], 1)
        st.eng.wait_ge(*x_read)
    else:
        st.did(ins)
        st.wait()
    st.did(v.tensor_tensor(sq, xc, xc, ALU.mult))
    st.wait()
    st.did(v.tensor_reduce(s, sq, AX.X, ALU.add))
    st.wait()
    v.tensor_scalar(var, s, 1.0 / D, EPS, ALU.mult, ALU.add).then_inc(var_ready, 1)


def scale_relu(nc, st, root, rs, xc, out):
    st.did(nc.vector.reciprocal(rs, root))
    st.wait()
    st.did(nc.vector.scalar_tensor_tensor(out, xc, 0.0, over(rs, D), ALU.max, ALU.mult))


class Lanes:

    def __init__(self, nc, sb, ident):
        self.nc, self.ident = nc, ident
        self.edge = sb("lane_edge", [P, 4 * D])
        self.turned = sb("lane_turned", [4 * D, P])
        self.chain = sb("lane_chain", [4 * D, P + 2])
        self.into = sb("lane_into", [P, 4 * D])
        self.head = sb("head", [P, ET])
        self.tail = sb("tail", [P, ET])
        self.no_start = sb("no_start", [4 * D, P])
        self.no_end = sb("no_end", [4 * D, P])

    def tensor(self, pe, W, forward, psum, lanes_ready, lanes_turned):
        nc = self.nc
        pe.wait_ge(lanes_ready, 1)
        nc.tensor.transpose(psum[0:W, 0:P], self.edge[:, 0:W], self.ident[:]).then_inc(lanes_turned, 1)
        pe.wait_ge(lanes_ready, 2)
        a = 0 if forward else 2
        nc.tensor.transpose(psum[:, P:P + W], self.chain[0:W, a:a + P],
                            self.ident[0:W, 0:W]).then_inc(lanes_turned, 1)

    def vector(self, st, sums, W, forward, psum, lanes_ready, lanes_turned, done):
        v, eng = self.nc.vector, st.eng
        st.wait()
        at = ET - 1 if forward else 0
        v.tensor_copy(self.edge[:, 0:W], sums[:, at, :]).then_inc(lanes_ready, 1)
        eng.wait_ge(lanes_turned, 1)
        st.did(v.tensor_copy(self.turned[0:W, :], psum[0:W, 0:P]))
        st.wait()
        if forward:
            ins = v.tensor_tensor_scan(self.chain[0:W, 1:P + 1], self.no_start[0:W, :], self.turned[0:W, :],
                                       0.0, ALU.mult, ALU.add)
        else:
            ins = v.tensor_tensor_scan(self.chain[0:W, P:0:-1], self.no_end[0:W, ::-1], self.turned[0:W, ::-1],
                                       0.0, ALU.mult, ALU.add)
        ins.then_inc(lanes_ready, 1)
        eng.wait_ge(lanes_turned, 2)
        st.did(v.tensor_copy(self.into[:, 0:W], psum[:, P:P + W]))
        st.wait()
        mask = self.head if forward else self.tail
        for w in range(W):
            v.scalar_tensor_tensor(sums[:, :, w], mask[:], self.into[:, w:w + 1], sums[:, :, w],
                                   ALU.mult, ALU.add).then_inc(done, 1)


class Core:

    def __init__(self, nc):
        self.nc, self.sems = nc, []
        self.settled = self.nc.alloc_semaphore(name="settled")

    def sem(self, name):
        self.sems.append(self.nc.alloc_semaphore(name=name))
        return self.sems[-1]

    def end_stage(self):
        self.nc.clear_and_free_semaphores(self.sems)
        self.nc.all_engine_barrier()
        self.sems = []


def stage(core):
    nc, ctx = core.nc, ExitStack()
    sb = lambda name, shape, dt=F32: ctx.enter_context(nc.sbuf_tensor(name, shape, dt))
    ps = lambda name, shape: ctx.enter_context(nc.psum_tensor(name, shape, F32))
    return ctx, sb, ps


def setup(core, io, d, lanes, m):
    nc, sem = core.nc, core.sem
    ctx, sb, ps = stage(core)
    Q = ET // 4
    ZW = 7168
    zeros = sb("zeros", [P, ZW])
    at_b, prev_b, next_b = sb("at_b", [P, ET], I32), sb("prev_b", [P, ET], I32), sb("next_b", [P, ET], I32)
    at_s, next_s = sb("at_s", [P, ET], I32), sb("next_s", [P, ET], I32)
    pos_b, pos1_s = sb("pos_b", [P, ET]), sb("pos1_s", [P, ET])
    starts, start_pos, first, cnt = sb("starts", [P, ET]), sb("start_pos", [P, ET]), sb("first", [P, ET]), sb("cnt", [P, ET])
    pen = sb("pen", [P, ET], BF16)
    cnt_rows = sb("cnt_rows", [Q, 4, P])
    lane_max, lane_from = sb("lane_max", [1, P]), sb("lane_from", [1, P + 2])
    bare = sb("bare", [P, 2])
    from_col = sb("from_col", [P, 1])
    p_rows, p_col, p_one = ps("p_rows", [4 * D, 2, P]), ps("p_col", [P, 512]), ps("p_one", [P, 512])
    p_cnt = ps("p_cnt", [P, 4, Q])
    loaded, zeros_in, filled, own = sem("setup_loaded"), sem("zeros_in"), sem("tables_filled"), sem("setup_own")
    max_in, from_in, bare_in = sem("lane_max_in"), sem("lane_from_in"), sem("bare_in")
    max_turned, from_turned, bare_turned, cnt_turned = sem("max_turned"), sem("from_turned"), sem("bare_turned"), sem("cnt_turned")
    pen_in, cnt_in, rows_out, cnt_back = sem("pen_in"), sem("cnt_in"), sem("rows_out"), sem("cnt_back")
    window = lambda k: io["dst_ext"][k:k + EP].rearrange("(p t) -> p t", p=P)
    loads = ((m["ident"][:], io["ident"]), (pos_b[:], io["pos_b"]), (pos1_s[:], io["pos1_s"]),
             (prev_b[:], window(0)), (at_b[:], window(1)), (next_b[:], window(2)),
             (at_s[:], io["dst_s"]), (next_s[:], io["next_s"]))
    fills = []
    for name in ("a0", "a1", "f"):
        flat = d[name].rearrange("(p r) w -> p (r w)", p=P)
        fills += [(flat[:, a:min(a + ZW, flat.shape[1])], min(ZW, flat.shape[1] - a)) for a in range(0, flat.shape[1], ZW)]
    for name in ("t2", "t3a", "t3b"):
        fills.append((d[name][0:1, :], d[name].shape[1]))

    with ctx, nc.Block() as block:
        @block.sync
        def _(sp):
            for dst, src in loads:
                sp.dma_start(dst, src).then_inc(loaded, DMA)
            sp.wait_ge(pen_in, 1)
            sp.dma_start(d["pen"].rearrange("(p t) -> p t", p=P), pen[:]).then_inc(rows_out, DMA)
            sp.wait_ge(cnt_in, 1)
            sp.dma_start(d["cnt"].rearrange("(p t) -> p t", p=P), cnt[:]).then_inc(rows_out, DMA)
            sp.wait_ge(rows_out, 2 * DMA)
            sp.dma_start(cnt_rows[:], d["cnt"].rearrange("(f q p) -> q f p", f=4, p=P)).then_inc(cnt_back, DMA)

        @block.scalar
        def _(act):
            act.wait_ge(zeros_in, 1)
            for dst, width in fills:
                act.dma_start(dst, zeros[0:dst.shape[0], 0:width]).then_inc(filled, DMA)
            act.wait_ge(filled, DMA * len(fills))

        @block.tensor
        def _(pe):
            pe.wait_ge(loaded, DMA * len(loads))
            pe.wait_ge(max_in, 1)
            nc.tensor.transpose(p_one[0:1, 0:P], first[:, ET - 1:ET], m["ident"][:]).then_inc(max_turned, 1)
            pe.wait_ge(from_in, 1)
            nc.tensor.transpose(p_col[:, 0:1], lane_from[:, 0:P], m["ident"][0:1, 0:1]).then_inc(from_turned, 1)
            pe.wait_ge(bare_in, 2)
            for k in range(2):
                nc.tensor.matmul(p_rows[:, k, :], bare[:, k:k + 1].to_broadcast([P, 4 * D]), m["ident"][:],
                                 start=True, stop=True).then_inc(bare_turned, 1)
            pe.wait_ge(cnt_back, DMA)
            for f in range(4):
                mm = nc.tensor.transpose(p_cnt[:, f, :], cnt_rows[:, f, :], m["ident"][0:Q, 0:Q])
            mm.then_inc(cnt_turned, 1)

        @block.vector
        def _(v):
            st = Steps(v, own)
            tt, ts, scan = nc.vector.tensor_tensor, nc.vector.tensor_scalar, nc.vector.tensor_tensor_scan
            nc.vector.memset(zeros[:], 0.0).then_inc(zeros_in, 1)
            st.did(nc.vector.memset(lanes.chain[:], 0.0))
            st.did(nc.vector.memset(lane_from[:], 0.0))
            v.wait_ge(loaded, DMA * len(loads))
            st.did(tt(starts[:], at_b[:], prev_b[:], ALU.not_equal))
            st.did(tt(m["ends"][:], at_b[:], next_b[:], ALU.not_equal))
            st.did(tt(m["starts_not"][:], at_b[:], prev_b[:], ALU.is_equal))
            st.did(tt(m["ends_not"][:], at_b[:], next_b[:], ALU.is_equal))
            st.did(tt(cnt[:], at_s[:], next_s[:], ALU.is_equal))
            st.wait()
            st.did(scan(lanes.head[:], m["starts_not"][:], m["starts_not"][:], 1.0, ALU.mult, ALU.min))
            st.did(scan(lanes.tail[:, ::-1], m["ends_not"][:, ::-1], m["ends_not"][:, ::-1], 1.0, ALU.mult, ALU.min))
            st.did(nc.vector.scalar_tensor_tensor(m["end_s"][:], cnt[:], float(FAR), at_s[:], ALU.mult, ALU.add))
            st.did(nc.vector.scalar_tensor_tensor(m["end_b"][:], m["ends_not"][:], float(FAR), at_b[:], ALU.mult, ALU.add))
            st.did(tt(start_pos[:], starts[:], pos_b[:], ALU.mult))
            ts(pen[:], starts[:], PEN, None, ALU.mult).then_inc(pen_in, 1)
            st.wait()
            nc.vector.tensor_copy(bare[:, 0:1], lanes.head[:, ET - 1:ET]).then_inc(bare_in, 1)
            nc.vector.tensor_copy(bare[:, 1:2], lanes.tail[:, 0:1]).then_inc(bare_in, 1)
            scan(first[:], start_pos[:], start_pos[:], 0.0, ALU.max, ALU.max).then_inc(max_in, 1)
            v.wait_ge(max_turned, 1)
            st.did(nc.vector.tensor_copy(lane_max[:], p_one[0:1, 0:P]))
            st.wait()
            scan(lane_from[:, 1:P + 1], lane_max[:], lane_max[:], 0.0, ALU.max, ALU.max).then_inc(from_in, 1)
            v.wait_ge(from_turned, 1)
            st.did(nc.vector.tensor_copy(from_col[:], p_col[:, 0:1]))
            st.wait()
            st.did(ts(first[:], first[:], from_col[:], None, ALU.max))
            st.wait()
            st.did(tt(cnt[:], pos_b[:], first[:], ALU.subtract))
            st.wait()
            ts(cnt[:], cnt[:], 1.0, None, ALU.add).then_inc(cnt_in, 1)
            v.wait_ge(bare_turned, 2)
            st.did(nc.vector.tensor_copy(lanes.no_start[:], p_rows[:, 0, :]))
            st.did(nc.vector.tensor_copy(lanes.no_end[:], p_rows[:, 1, :]))
            st.did(nc.vector.tensor_copy(m["cntpos_s"][:, :, 1], pos1_s[:]))
            v.wait_ge(cnt_turned, 1)
            st.did(nc.vector.tensor_copy(m["cntpos_s"][:, :, 0], p_cnt[:].rearrange("p f q -> p (f q)")))
            st.wait()


def gather_sources(core, io, d, h0):
    nc, sem = core.nc, core.sem
    ctx, sb, ps = stage(core)
    idx, rows = sb("src_idx", [P, 2, G], I32), sb("src_rows_x", [P, 2, G, D])
    xc, sq, s = sb("gs_xc", [P, G, D]), sb("gs_sq", [P, G, D]), sb("gs_s", [P, G])
    var, root, rs = sb("gs_var", [P, 2, G]), sb("gs_root", [P, 2, G]), sb("gs_rs", [P, G])
    idx_in, gathered, kept = [sem(f"gs_idx{k}") for k in range(2)], [sem(f"gs_rows{k}") for k in range(2)], [sem(f"gs_kept{k}") for k in range(2)]
    rows_read, var_ready, root_ready, own = sem("gs_read"), sem("gs_varr"), sem("gs_rootr"), sem("gs_own")
    xs = d["xs"].rearrange("(t p) w -> p t w", p=P)
    with ctx, nc.Block() as block:
        @block.sync
        def _(sp):
            for i, _ in passes(sp, EC // 2):
                for k in range(2):
                    sp.wait_ge(gathered[k], i * (DMA * G))
                    sp.dma_start(idx[:, k, :], io["src_s"][:, cols(i * (2 * G) + k * G, G)]).then_inc(idx_in[k], DMA)

        @block.gpsimd
        def _(pool):
            for i, _ in passes(pool, EC // 2):
                for k in range(2):
                    pool.wait_ge(idx_in[k], (i + 1) * DMA)
                    pool.wait_ge(rows_read, 2 * i + k + 1)
                    pool.wait_ge(kept[k], i * DMA)
                    settle(core, pool)
                    for t in range(G):
                        nc.gpsimd.indirect_dma_start(
                            out=rows[:, k, t, :], out_offset=None, in_=io["x"][:, :],
                            in_offset=bass.IndirectOffsetOnAxis(ap=idx[:, k, t:t + 1], axis=0)).then_inc(gathered[k], DMA)

        @block.scalar
        def _(act):
            for i, _ in passes(act, EC // 2):
                for k in range(2):
                    act.wait_ge(gathered[k], (i + 1) * (DMA * G))
                    act.dma_start(xs[:, cols(i * (2 * G) + k * G, G), :], rows[:, k]).then_inc(kept[k], DMA)
                    act.wait_ge(var_ready, 2 * i + k + 1)
                    nc.scalar.activation(root[:, k], var[:, k], ACT.Sqrt).then_inc(root_ready, 1)
            for k in range(2):
                act.wait_ge(kept[k], EC // 2 * DMA)

        @block.vector
        def _(v):
            st = Steps(v, own, 10)
            v.sem_inc(rows_read, 2)
            for i, _ in passes(v, EC // 2):
                st.start_pass(i)
                for k in range(2):
                    c = 2 * i + k
                    v.wait_ge(gathered[k], (i + 1) * (DMA * G))
                    centre(nc, st, rows[:, k], xc[:], sq[:], s[:], var[:, k], var_ready, (rows_read, c + 3))
                    v.wait_ge(root_ready, c + 1)
                    scale_relu(nc, st, root[:, k], rs[:], xc[:], h0[:, cols(i * (2 * G) + k * G, G), :])
                    st.wait()
                st.end_pass()


def attention(core, io, d, m, h0):
    nc, sem = core.nc, core.sem
    ctx, sb, ps = stage(core)
    C = 4
    W = C * P
    NCH = ET // C
    weights, sel = sb("att_w", [D + 1, 4 * P]), sb("att_sel", [P, D])
    ef, pen = sb("att_ef", [D + 1, 2, W]), sb("att_pen", [P, 2, W], BF16)
    hs, hb = sb("att_hs", [P, 2, C, D * D]), sb("att_hb", [P, 2, W])
    x, mp, arg, ab = sb("att_x", [P, 2, W]), sb("att_mp", [P, 2, W]), sb("att_arg", [P, 2, 2 * W]), sb("att_ab", [P, 2, 2 * W])
    top = sb("att_top", [P, 2, 2, W + 1])
    den, num = sb("att_den", [P, 2, 2, W]), sb("att_num", [P, 2, 2, W])
    v_in, part = sb("att_v", [P, 2, W]), sb("att_part", [P, 2, W])
    logd, inv, ratio = sb("att_log", [P, 2, W]), sb("att_inv", [P, 2, W]), sb("att_ratio", [P, 2, W])
    rows, end_idx = sb("att_rows", [P, 2, C, A0W]), sb("att_end", [P, 2, C], I32)
    t_rows = sb("att_trows", [P, 2, C, D])
    xd_idx, xd_rows = sb("att_xdi", [P, 2, C], I32), sb("att_xdr", [P, 2, C, D])
    p_hb, p_wa, p_wm = [ps(f"p_hb{u}", [P, W]) for u in range(2)], [ps(f"p_wa{u}", [P, W]) for u in range(2)], [ps(f"p_wm{u}", [P, W]) for u in range(2)]
    p_out = ps("p_att_out", [P, C, D])
    two = lambda name: [sem(f"{name}{k}") for k in range(2)]
    consts, ef_in, pen_in, xdi_in = sem("att_consts"), two("att_ef_in"), two("att_pen_in"), two("att_xdi_in")
    xd_got, xd_kept, t_kept, scattered = two("att_xd_got"), two("att_xd_kept"), two("att_t_kept"), two("att_scat")
    hs_in, projected, hb_in, args_in, exp_done = sem("att_hs_in"), sem("att_proj"), sem("att_hb_in"), sem("att_args_in"), sem("att_exp")
    v_done, den_in, inv_own, inv_in, ratio_in = sem("att_v_done"), sem("att_den_in"), sem("att_inv_own"), sem("att_inv_in"), sem("att_ratio_in")
    out_in, rows_in, trows_in, endi_in, own = sem("att_out_in"), sem("att_rows_in"), sem("att_trows_in"), sem("att_endi_in"), sem("att_own")
    x_done, part_done, pen_read = sem("att_x_done"), sem("att_part_done"), sem("att_pen_read")
    state_in = sem("att_state_in")
    AHEAD = 2
    at_b = io["dst_ext"][1:1 + EP].rearrange("(p t) -> p t", p=P)
    xd, t0 = d["xd"].rearrange("(p t) w -> p t w", p=P), d["t0"].rearrange("(t p) w -> p t w", p=P)
    LOOP = NCH // 2

    with ctx, nc.Block() as block:
        @block.sync
        def _(sp):
            sp.dma_start(weights[:], io["w_att"]).then_inc(consts, DMA)
            sp.dma_start(sel[:], io["sel"]).then_inc(consts, DMA)
            for i, _ in passes(sp, LOOP):
                for k in range(2):
                    sp.wait_ge(xd_got[k], i * (C * DMA))
                    sp.dma_start(xd_idx[:, k, :], at_b[:, cols(i * (2 * C) + k * C, C)]).then_inc(xdi_in[k], DMA)
                    sp.wait_ge(projected, 4 * i + 2 * k)
                    sp.dma_start(ef[:, k, :], io["ef_t"][:, cols(i * (2 * W) + k * W, W)]).then_inc(ef_in[k], DMA)
                    sp.wait_ge(pen_read, 2 * i + k + 1)
                    settle(core, sp)
                    sp.dma_start(pen[:, k, :], d["pen"].rearrange("(o e) -> o e", o=1)[:, cols(i * (2 * W) + k * W, W)]
                                 .to_broadcast([P, W])).then_inc(pen_in[k], DMA)

        @block.gpsimd
        def _(pool):
            for i, _ in passes(pool, LOOP):
                for k in range(2):
                    pool.wait_ge(xdi_in[k], (i + 1) * DMA)
                    pool.wait_ge(xd_kept[k], i * DMA)
                    settle(core, pool)
                    for t in range(C):
                        nc.gpsimd.indirect_dma_start(
                            out=xd_rows[:, k, t, :], out_offset=None, in_=io["x"][:, :],
                            in_offset=bass.IndirectOffsetOnAxis(ap=xd_idx[:, k, t:t + 1], axis=0)).then_inc(xd_got[k], DMA)
                    pool.wait_ge(endi_in, 2 * i + k + 1)
                    pool.wait_ge(rows_in, 2 * (2 * i + k + 1))
                    settle(core, pool)
                    for t in range(C):
                        nc.gpsimd.indirect_dma_start(
                            out=d["a0"][:, :], out_offset=bass.IndirectOffsetOnAxis(ap=end_idx[:, k, t:t + 1], axis=0),
                            in_=rows[:, k, t, :], in_offset=None, bounds_check=NP - 1,
                            oob_is_err=False).then_inc(scattered[k], DMA)

        @block.tensor
        def _(pe):
            def project(c, i, k):
                pe.wait_ge(hs_in, c + 1)
                pe.wait_ge(ef_in[k], (i + 1) * DMA)
                for u in range(2):
                    pe.wait_ge(hb_in, 2 * c + u + 1)
                    for t in range(C):
                        nc.tensor.matmul(p_hb[u][:, t * P:(t + 1) * P],
                                         hs[:, k, t, u * P:(u + 1) * P], m["ident"][:], start=True, stop=True)
                    pe.wait_ge(x_done, 2 * c + u + 1)
                    pe.wait_ge(v_done, 2 * c + u + 1)
                    nc.tensor.matmul(p_wa[u][:], weights[:, u * P:(u + 1) * P], ef[:, k, :], start=True, stop=True)
                    nc.tensor.matmul(p_wm[u][:], weights[:, (2 + u) * P:(3 + u) * P], ef[:, k, :],
                                     start=True, stop=True).then_inc(projected, 1)

            def sum_inputs(c, k):
                pe.wait_ge(rows_in, 2 * c)
                pe.wait_ge(ratio_in, 2 * c + 2)
                for t in range(C):
                    for u in range(2):
                        mm = nc.tensor.matmul(p_out[:, t, :], ratio[:, u, t * P:(t + 1) * P], sel[:],
                                              start=(u == 0), stop=(u == 1))
                mm.then_inc(out_in, 1)

            pe.sem_inc(projected, AHEAD)
            pe.wait_ge(consts, 2 * DMA)
            project(0, 0, 0)
            for i, last in passes(pe, LOOP, last_apart=True):
                project(2 * i + 1, i, 1)
                sum_inputs(2 * i, 0)
                if not last:
                    project(2 * i + 2, i + 1, 0)
                sum_inputs(2 * i + 1, 1)

        @block.scalar
        def _(act):
            def spread(c, i, k):
                act.wait_ge(projected, 2 * c)
                nc.scalar.copy(hs[:, k].rearrange("p t (w o) -> p (t w) o", o=D),
                               over(h0[:, cols(c * C, C), :].rearrange("p t w -> p (t w)"), D)).then_inc(hs_in, 1)
                for u in range(2):
                    act.wait_ge(projected, 2 * c + u + 1 + AHEAD)
                    act.wait_ge(v_done, 2 * c + u + 1)
                    nc.scalar.copy(hb[:, u], p_hb[u][:]).then_inc(hb_in, 1)

            act.sem_inc(hb_in, AHEAD)
            spread(0, 0, 0)
            for i, last in passes(act, LOOP, last_apart=True):
                for k in range(2):
                    c = 2 * i + k
                    for u in range(2):
                        act.wait_ge(args_in, 2 * c + u + 1)
                        nc.scalar.activation(ab[:, u], arg[:, u], ACT.Exp).then_inc(exp_done, 1)
                    if not (last and k):
                        spread(c + 1, i + 1 if k else i, 1 - k)
                    for u in range(2):
                        act.wait_ge(den_in, 2 * c + u + 1)
                        nc.scalar.activation(logd[:, u], den[:, u, k], ACT.Ln).then_inc(inv_own, 1)
                        act.wait_ge(inv_own, 2 * c + u + 1)
                        nc.scalar.activation(inv[:, u], logd[:, u], ACT.Exp, scale=-1.0).then_inc(inv_in, 1)
                    act.wait_ge(scattered[k], i * (C * DMA))
                    act.wait_ge(t_kept[k], i * DMA)
                    nc.scalar.copy(end_idx[:, k], m["end_s"][:, cols(c * C, C)]).then_inc(endi_in, 1)
                    nc.scalar.copy(rows[:, k, :, D:A0W], m["cntpos_s"][:, cols(c * C, C), :]).then_inc(rows_in, 1)
                    act.wait_ge(out_in, c + 1)
                    nc.scalar.copy(rows[:, k, :, 0:D], p_out[:]).then_inc(rows_in, 1)
                    act.wait_ge(rows_in, 2 * c + 2)
                    act.dma_start(t0[:, cols(c * C, C), :], rows[:, k, :, 0:D]).then_inc(t_kept[k], DMA)
                    act.wait_ge(xd_got[k], (i + 1) * (C * DMA))
                    act.dma_start(xd[:, cols(c * C, C), :], xd_rows[:, k]).then_inc(xd_kept[k], DMA)
            for k in range(2):
                act.wait_ge(scattered[k], LOOP * C * DMA)
                act.wait_ge(t_kept[k], LOOP * DMA)
                act.wait_ge(xd_kept[k], LOOP * DMA)

        @block.vector
        def _(v):
            tt, scan = nc.vector.tensor_tensor, nc.vector.tensor_tensor_scan
            st = Steps(v, own, 18)
            v.sem_inc(pen_read, 2)
            v.sem_inc(x_done, AHEAD)
            v.sem_inc(v_done, AHEAD)
            pre = [nc.vector.memset(a[:, u, 1, W - 1 + o:W + o], 0.0) for u in range(2) for a, o in ((top, 1), (den, 0), (num, 0))]
            pre[-1].then_inc(state_in, 1)
            v.wait_ge(state_in, 1)
            for i, _ in passes(v, LOOP):
                st.start_pass(i)
                for k in range(2):
                    c = 2 * i + k
                    for u in range(2):
                        was, now = top[:, u, 1 - k, W:W + 1], top[:, u, k]
                        v.wait_ge(hb_in, 2 * c + u + 1 + AHEAD)
                        v.wait_ge(projected, 2 * c + u + 1 + AHEAD)
                        tt(x[:, u], p_wa[u][:], hb[:, u], ALU.mult).then_inc(x_done, 1)
                        st.did(nc.vector.tensor_copy(now[:, 0:1], was))
                        v.wait_ge(x_done, 2 * c + u + 1 + AHEAD)
                        if u == 0:
                            v.wait_ge(pen_in[k], (i + 1) * DMA)
                        st.did(scan(now[:, 1:W + 1], pen[:, k], x[:, u], was, ALU.add, ALU.max))
                        st.wait()
                        if u == 0:
                            st.did(tt(mp[:, u], now[:, 0:W], pen[:, k], ALU.add))
                            st.wait()
                        else:
                            tt(mp[:, u], now[:, 0:W], pen[:, k], ALU.add).then_inc(pen_read, 1)
                            v.wait_ge(pen_read, c + 3)
                        st.did(tt(arg[:, u, 0:W], mp[:, u], now[:, 1:W + 1], ALU.subtract))
                        tt(arg[:, u, W:2 * W], x[:, u], now[:, 1:W + 1], ALU.subtract).then_inc(args_in, 1)
                    for u in range(2):
                        tt(v_in[:, u], p_wm[u][:], hb[:, u], ALU.mult).then_inc(v_done, 1)
                    for u in range(2):
                        v.wait_ge(exp_done, 2 * c + u + 1)
                        v.wait_ge(v_done, 2 * c + u + 1 + AHEAD)
                        tt(part[:, u], v_in[:, u], ab[:, u, W:2 * W], ALU.mult).then_inc(part_done, 1)
                        scan(den[:, u, k], ab[:, u, 0:W], ab[:, u, W:2 * W], den[:, u, 1 - k, W - 1:W],
                             ALU.mult, ALU.add).then_inc(den_in, 1)
                        v.wait_ge(part_done, 2 * c + u + 1)
                        st.did(scan(num[:, u, k], ab[:, u, 0:W], part[:, u], num[:, u, 1 - k, W - 1:W], ALU.mult, ALU.add))
                    v.wait_ge(out_in, c)
                    for u in range(2):
                        v.wait_ge(inv_in, 2 * c + u + 1)
                        if u == 0:
                            st.wait()
                        tt(ratio[:, u], num[:, u, k], inv[:, u], ALU.mult).then_inc(ratio_in, 1)
                st.end_pass()


def message_sum(core, io, d, m, lanes, base, qf, dinv, own_sum):
    nc, sem = core.nc, core.sem
    ctx, sb, ps = stage(core)
    GW = HG * P
    M = 3 * D + 1
    wgt, before, dump = sb("wgt", [P, ET]), sb("before", [P, HG, P], BF16), sb("dump", [P, HG])
    one_only = sb("one_only", [P, M], BF16)
    idx, a0r = sb("ms_idx", [P, 2, G], I32), sb("ms_a0", [P, 2, G, A0W])
    xs, xd, s_row = sb("ms_xs", [P, 2, G, D]), sb("ms_xd", [P, 2, G, D]), sb("ms_srow", [P, 2, G * P], I32)
    s_col = sb("ms_scol", [P, 2, G])
    xa, xb, ca, cb, sq = (sb(f"ms_{n}", [P, G, D]) for n in ("xa", "xb", "ca", "cb", "sq"))
    ha, hb, t1, t2, t3, msg = (sb(f"ms_{n}", [P, G, D]) for n in ("ha", "hb", "t1", "t2", "t3", "msg"))
    s = sb("ms_s", [P, G])
    var, root, rs = sb("ms_var", [P, 3, G]), sb("ms_root", [P, 3, G]), sb("ms_rs", [P, G])
    after, before_i = sb("ms_with_one", [P, 2, G, M], BF16), sb("ms_with_zero", [P, 2, G, M], BF16)
    same = sb("ms_same", [P, 2, HG * (GW + P)], BF16)
    same_before = sb("ms_same_before", [P, 2, HG, P], BF16)
    sums, total, to_idx = sb("ms_sums", [P, 2, HG, M]), sb("ms_total", [P, 2, HG, D]), sb("ms_to", [P, 2, HG], I32)
    u1, u2 = sb("ms_u1", [P, HG]), sb("ms_u2", [P, HG])
    p_sum, p_lane = [ps(f"p_ms{g}", [P, HG, M]) for g in range(2)], ps("p_lane_ms", [P, 512])
    two = lambda name: [sem(f"{name}{k}") for k in range(2)]
    consts, lanes_ready, lanes_turned, own_in = sem("ms_consts"), sem("ms_lanes_in"), sem("ms_lanes_turned"), sem("ms_own_in")
    idx_in, rows_in, got, added = two("ms_idx_in"), two("ms_rows_in"), two("ms_got"), sem("ms_added")
    used, var_in, root_in, own, once = sem("ms_used"), sem("ms_var_in"), sem("ms_root_in"), sem("ms_own"), sem("ms_once")
    same_in, summed, copied, total_in = sem("ms_same_in"), sem("ms_summed"), sem("ms_copied"), sem("ms_total_in")
    landed = sem("ms_landed")
    LOOP = EC // 2
    blk = lambda name: d[name].rearrange("(p t) w -> p t w", p=P)
    loads = ((own_sum[:], blk("t0")), (wgt[:], io["wgt"]), (before[:], io["before"]), (dump[:], io["dump"]), (one_only[:], io["one_only"]))

    with ctx, nc.Block() as block:
        @block.sync
        def _(sp):
            for dst, src in loads:
                sp.dma_start(dst, src).then_inc(consts, DMA)
            for i, _ in passes(sp, LOOP):
                for k in range(2):
                    a = i * (2 * G) + k * G
                    sp.wait_ge(got[k], i * (G * DMA))
                    sp.dma_start(idx[:, k, :], io["src_b"][:, cols(a, G)]).then_inc(idx_in[k], DMA)
                    sp.wait_ge(used, 2 * i + k + 1)
                    sp.dma_start(xs[:, k], blk("xs")[:, cols(a, G), :]).then_inc(rows_in[k], DMA)
                    sp.dma_start(xd[:, k], blk("xd")[:, cols(a, G), :]).then_inc(rows_in[k], DMA)
                    sp.dma_start(s_col[:, k], io["src_f"][:, cols(a, G)]).then_inc(rows_in[k], DMA)
                    sp.dma_start(s_row[:, k], io["src_rows"][:, cols(i * (2 * G * P) + k * G * P, G * P)]
                                 .to_broadcast([P, G * P])).then_inc(rows_in[k], DMA)

        @block.gpsimd
        def _(pool):
            def gather(i, k, c):
                pool.wait_ge(idx_in[k], (i + 1) * DMA)
                pool.wait_ge(used, c + 1)
                settle(core, pool)
                for t in range(G):
                    nc.gpsimd.indirect_dma_start(
                        out=a0r[:, k, t, :], out_offset=None, in_=d["a0"][:, :],
                        in_offset=bass.IndirectOffsetOnAxis(ap=idx[:, k, t:t + 1], axis=0)).then_inc(got[k], DMA)

            for k in range(2):
                gather(0, k, k)
            for i, last in passes(pool, LOOP, last_apart=True):
                for k in range(2):
                    for g in range(2):
                        n = 4 * i + 2 * k + g
                        pool.wait_ge(total_in, n + 1)
                        pool.wait_ge(added, n * (HG * DMA))
                        pool.sem_inc(landed, 1)
                        for t in range(HG):
                            nc.gpsimd.indirect_dma_start(
                                out=d["a1"][:, :], out_offset=bass.IndirectOffsetOnAxis(ap=to_idx[:, g, t:t + 1], axis=0),
                                in_=total[:, g, t, :], in_offset=None, compute_op=ALU.add).then_inc(added, DMA)
                    if not last:
                        gather(i + 1, k, 2 * i + 2 + k)
            pool.wait_ge(added, 2 * EC * HG * DMA)

        @block.scalar
        def _(act):
            for i, _ in passes(act, LOOP):
                for k in range(2):
                    for r in range(3):
                        act.wait_ge(var_in, 3 * (2 * i + k) + r + 1)
                        nc.scalar.activation(root[:, r], var[:, r], ACT.Sqrt).then_inc(root_in, 1)
                    for g in range(2):
                        n = 4 * i + 2 * k + g
                        act.wait_ge(summed, n + 1)
                        nc.scalar.copy(sums[:, g], p_sum[g][:]).then_inc(copied, 1)

        @block.tensor
        def _(pe):
            lanes.tensor(pe, D, False, p_lane, lanes_ready, lanes_turned)
            for i, _ in passes(pe, LOOP):
                for k in range(2):
                    for g in range(2):
                        n = 4 * i + 2 * k + g
                        pe.wait_ge(same_in, n + 1)
                        for t in range(HG):
                            o = p_sum[g][:, t, :]
                            nc.tensor.matmul(o, same_before[:, g, t, :], one_only[:], start=True, stop=False)
                            for j in range(HG):
                                parts = after if j < t else before_i
                                mm = nc.tensor.matmul(o, same[:, g, j * GW + t * P:j * GW + (t + 1) * P],
                                                      parts[:, k, g * HG + j, :], start=False, stop=(j == HG - 1))
                        mm.then_inc(summed, 1)

        @block.vector
        def _(v):
            tt, ts, stt = nc.vector.tensor_tensor, nc.vector.tensor_scalar, nc.vector.scalar_tensor_tensor
            first = Steps(v, once)
            v.wait_ge(consts, len(loads) * DMA)
            first.did(nc.vector.memset(after[:], 1.0))
            first.did(nc.vector.memset(before_i[:], 0.0))
            first.did(tt(own_sum[:], own_sum[:], over(m["ends"][:], D), ALU.mult))
            first.wait()
            for w in range(D):
                first.did(nc.vector.tensor_tensor_scan(own_sum[:, ::-1, w], m["ends_not"][:, ::-1],
                                                       own_sum[:, ::-1, w], 0.0, ALU.mult, ALU.add))
            lanes.vector(first, own_sum, D, False, p_lane, lanes_ready, lanes_turned, own_in)
            v.wait_ge(own_in, D)
            v.sem_inc(used, 2)
            st = Steps(v, own, STEPS_MS)
            for i, _ in passes(v, LOOP):
                st.start_pass(i)
                for k in range(2):
                    c, at = 2 * i + k, cols(i * (2 * G) + k * G, G)
                    v.wait_ge(got[k], (i + 1) * (G * DMA))
                    v.wait_ge(rows_in[k], (i + 1) * (4 * DMA))
                    st.did(tt(xa[:], xs[:, k], a0r[:, k, :, 0:D], ALU.add))
                    st.did(tt(xb[:], xd[:, k], own_sum[:, at, :], ALU.add))
                    st.wait()
                    centre(nc, st, xa[:], ca[:], sq[:], s[:], var[:, 0], var_in)
                    v.wait_ge(var_in, 3 * c + 1)
                    centre(nc, st, xb[:], cb[:], sq[:], s[:], var[:, 1], var_in)
                    ts(var[:, 2], a0r[:, k, :, D], 1.0, None, ALU.add).then_inc(var_in, 1)
                    st.did(nc.vector.tensor_copy(qf[:, at], a0r[:, k, :, D + 1]))
                    v.wait_ge(root_in, 3 * c + 1)
                    scale_relu(nc, st, root[:, 0], rs[:], ca[:], ha[:])
                    st.wait()
                    v.wait_ge(root_in, 3 * c + 2)
                    scale_relu(nc, st, root[:, 1], rs[:], cb[:], hb[:])
                    v.wait_ge(root_in, 3 * c + 3)
                    st.did(nc.vector.reciprocal(dinv[:, at], root[:, 2]))
                    st.did(ts(t1[:], ha[:], -0.2, 1.0, ALU.mult, ALU.add))
                    st.did(stt(t2[:], ha[:], -1.0, ha[:], ALU.add, ALU.mult))
                    st.wait()
                    st.did(tt(t3[:], t1[:], t2[:], ALU.mult))
                    st.wait()
                    st.did(stt(base[:, at, :], t3[:], 0.1, xa[:], ALU.add, ALU.add))
                    st.did(ts(t2[:], hb[:], 0.1, 5.0, ALU.mult, ALU.add))
                    st.did(tt(msg[:], ha[:], hb[:], ALU.mult))
                    st.wait()
                    st.did(stt(t1[:], ha[:], 0.9, t2[:], ALU.mult, ALU.add))
                    st.did(tt(t3[:], msg[:], over(wgt[:, at], D), ALU.mult))
                    st.wait()
                    st.did(nc.vector.reciprocal(t2[:], t1[:]))
                    st.wait()
                    st.did(tt(msg[:], t3[:], t2[:], ALU.mult))
                    st.wait()
                    v.wait_ge(summed, 4 * i + 2 * k)
                    hi, mid, lo = (after[:, k, :, 1 + D * q:1 + D * (q + 1)] for q in range(3))
                    st.did(nc.vector.tensor_copy(hi, msg[:]))
                    st.wait()
                    st.did(tt(t1[:], msg[:], hi, ALU.subtract))
                    st.wait()
                    st.did(nc.vector.tensor_copy(mid, t1[:]))
                    st.wait()
                    st.did(tt(t2[:], t1[:], mid, ALU.subtract))
                    st.wait()
                    st.did(nc.vector.tensor_copy(lo, t2[:]))
                    st.wait()
                    st.did(nc.vector.tensor_copy(before_i[:, k, :, 1:M], after[:, k, :, 1:M]))
                    for g in range(2):
                        n = 4 * i + 2 * k + g
                        for j in range(HG):
                            st.did(ts(same[:, g, j * GW:(j + 1) * GW], s_row[:, k, g * GW:(g + 1) * GW],
                                      s_col[:, k, g * HG + j:g * HG + j + 1], None, ALU.is_equal))
                        st.wait()
                        diagonal = same[:, g].rearrange("p (j x) -> p j x", x=GW + P)[:, :, 0:P]
                        tt(same_before[:, g], diagonal, before[:], ALU.mult).then_inc(same_in, 1)
                    for g in range(2):
                        n = 4 * i + 2 * k + g
                        v.wait_ge(copied, n + 1)
                        v.wait_ge(landed, n)
                        st.did(ts(u1[:], sums[:, g, :, 0], 0.0, None, ALU.is_equal))
                        st.did(tt(u2[:], s_col[:, k, g * HG:(g + 1) * HG], dump[:], ALU.subtract))
                        st.did(tt(total[:, g], sums[:, g, :, 1:1 + D], sums[:, g, :, 1 + D:1 + 2 * D], ALU.add))
                        st.wait()
                        st.did(tt(u2[:], u2[:], u1[:], ALU.mult))
                        st.did(tt(total[:, g], total[:, g], sums[:, g, :, 1 + 2 * D:M], ALU.add))
                        st.wait()
                        tt(to_idx[:, g], u2[:], dump[:], ALU.add).then_inc(total_in, 1)
                    v.wait_ge(total_in, 4 * i + 2 * k + 2)
                    v.sem_inc(used, 1)
                st.end_pass()


def edge_layer(core, io, d, m, lanes, base):
    nc, sem = core.nc, core.sem
    ctx, sb, ps = stage(core)
    WE = 2 * D * D
    msg = sb("el_msg", [P, ET, D])
    sums = sb("el_sums", [P, ET, D])
    idx, rows = sb("el_idx", [P, 2, G], I32), sb("el_rows", [P, 2, G, D])
    ea = sb("el_ea", [9, 2, G, P])
    edge_w, root_w = sb("el_edge_w", [9, D * D]), sb("el_root_w", [KB, TG * D])
    x2, xc, sq, h = sb("el_x2", [P, 2, G, D]), sb("el_xc", [P, G, D]), sb("el_sq", [P, G, D]), sb("el_h", [P, 2, G, D])
    s, var, root, rs = sb("el_s", [P, G]), sb("el_var", [P, 2, G]), sb("el_root", [P, 2, G]), sb("el_rs", [P, G])
    turned = sb("el_turned", [KB, 2, 2, P])
    prod = sb("el_prod", [P, 2, WE])
    p_turn, p_lin = ps("p_el_turn", [TG * D, 2, P]), ps("p_el_lin", [P, 2, TG * D])
    p_w = [ps(f"p_el_w{k}", [P, WE]) for k in range(3)]
    p_lane = ps("p_el_lane", [P, 512])
    two = lambda name: [sem(f"{name}{k}") for k in range(2)]
    consts, lanes_ready, lanes_turned, sums_in, stored = sem("el_consts"), sem("el_lanes_in"), sem("el_lanes_turned"), sem("el_sums_in"), sem("el_stored")
    idx_in, got, ea_in, used = two("el_idx_in"), two("el_got"), two("el_ea_in"), sem("el_used")
    var_in, root_in, own, h_in, turn_in, turned_in, lin_in = sem("el_var_in"), sem("el_root_in"), sem("el_own"), sem("el_h_in"), sem("el_turn_in"), sem("el_turned_in"), sem("el_lin_in")
    w_in, w_used, ones_in, end_own = sem("el_w_in"), sem("el_w_used"), sem("el_ones_in"), sem("el_end_own")
    LOOP = EC // 2
    NW = G // 2

    with ctx, nc.Block() as block:
        @block.sync
        def _(sp):
            sp.dma_start(edge_w[:], io["edge_w"]).then_inc(consts, DMA)
            sp.dma_start(root_w[:], io["root_w"]).then_inc(consts, DMA)
            for i, _ in passes(sp, LOOP):
                for k in range(2):
                    a = i * (2 * G) + k * G
                    sp.wait_ge(got[k], i * (G * DMA))
                    sp.dma_start(idx[:, k, :], io["src_b"][:, cols(a, G)]).then_inc(idx_in[k], DMA)
                    sp.wait_ge(w_in, (2 * i + k) * NW)
                    sp.dma_start(ea[:, k], io["ea_t"][:, cols(a, G), :]).then_inc(ea_in[k], DMA)
            sp.wait_ge(sums_in, D)
            sp.dma_start(d["t2"][1:EP + 1, :].rearrange("(p t) w -> p t w", p=P), sums[:]).then_inc(stored, DMA)
            sp.wait_ge(stored, DMA)

        @block.gpsimd
        def _(pool):
            for i, _ in passes(pool, LOOP):
                for k in range(2):
                    pool.wait_ge(idx_in[k], (i + 1) * DMA)
                    pool.wait_ge(used, 2 * i + k + 1)
                    settle(core, pool)
                    for t in range(G):
                        nc.gpsimd.indirect_dma_start(
                            out=rows[:, k, t, :], out_offset=None, in_=d["a1"][:, :],
                            in_offset=bass.IndirectOffsetOnAxis(ap=idx[:, k, t:t + 1], axis=0)).then_inc(got[k], DMA)

        @block.scalar
        def _(act):
            act.wait_ge(ones_in, 1)
            for i, _ in passes(act, LOOP):
                for k in range(2):
                    c = 2 * i + k
                    act.wait_ge(var_in, c + 1)
                    nc.scalar.activation(root[:, k], var[:, k], ACT.Sqrt).then_inc(root_in, 1)
                    act.wait_ge(turn_in, c + 1)
                    nc.scalar.copy(turned[0:TG * D, k], p_turn[:]).then_inc(turned_in, 1)

        @block.tensor
        def _(pe):
            pe.wait_ge(consts, 2 * DMA)
            pe.sem_inc(w_in, NW)
            for i, _ in passes(pe, LOOP):
                for k in range(2):
                    c = 2 * i + k
                    pe.wait_ge(h_in, c + 1)
                    for q in range(2):
                        mm = nc.tensor.transpose(p_turn[:, q, :], h[:, k, q * TG:(q + 1) * TG, :].rearrange("p t w -> p (t w)"), m["ident"][:])
                    mm.then_inc(turn_in, 1)
                    pe.wait_ge(ea_in[k], (i + 1) * DMA)
                    for q in range(NW):
                        n = c * NW + q
                        pe.wait_ge(w_used, n + 1)
                        for j in range(2):
                            mm = nc.tensor.matmul(p_w[q % 3][:, j * D * D:(j + 1) * D * D], ea[:, k, 2 * q + j, :], edge_w[:],
                                                  start=True, stop=True)
                        mm.then_inc(w_in, 1)
                    pe.wait_ge(turned_in, c + 1)
                    for q in range(2):
                        mm = nc.tensor.matmul(p_lin[:, q, :], turned[:, k, q, :], root_w[:], start=True, stop=True)
                    mm.then_inc(lin_in, 1)
            lanes.tensor(pe, D, True, p_lane, lanes_ready, lanes_turned)

        @block.vector
        def _(v):
            tt, stt = nc.vector.tensor_tensor, nc.vector.scalar_tensor_tensor
            nc.vector.memset(turned[:], 1.0).then_inc(ones_in, 1)
            v.sem_inc(used, 2)
            v.sem_inc(w_used, 3)
            st = Steps(v, own, STEPS_EL)
            for i, _ in passes(v, LOOP):
                st.start_pass(i)
                for k in range(2):
                    c, at = 2 * i + k, cols(i * (2 * G) + k * G, G)
                    v.wait_ge(got[k], (i + 1) * (G * DMA))
                    tt(x2[:, k], base[:, at, :], rows[:, k], ALU.add).then_inc(used, 1)
                    v.wait_ge(used, c + 3)
                    centre(nc, st, x2[:, k], xc[:], sq[:], s[:], var[:, k], var_in)
                    v.wait_ge(root_in, c + 1)
                    st.did(nc.vector.reciprocal(rs[:], root[:, k]))
                    st.wait()
                    stt(h[:, k], xc[:], 0.0, over(rs[:], D), ALU.max, ALU.mult).then_inc(h_in, 1)
                    v.wait_ge(h_in, c + 1)
                    for q in range(NW):
                        n = c * NW + q
                        v.wait_ge(w_in, n + 1 + NW)
                        hh = h[:, k, 2 * q:2 * q + 2, :].rearrange("p t (o w) -> p t o w", o=1).to_broadcast([P, 2, D, D])
                        tt(prod[:, q % 2].rearrange("p (t o w) -> p t o w", t=2, o=D), p_w[q % 3][:].rearrange("p (t o w) -> p t o w", t=2, o=D),
                           hh, ALU.mult).then_inc(w_used, 1)
                        v.wait_ge(w_used, n + 4)
                        st.did(nc.vector.tensor_reduce(msg[:, cols(i * (2 * G) + k * G + 2 * q, 2), :], prod[:, q % 2].rearrange("p (t o w) -> p t o w", t=2, o=D), AX.X, ALU.add))
                    v.wait_ge(lin_in, c + 1)
                    st.did(tt(base[:, at, :], x2[:, k], p_lin[:].rearrange("p q (t w) -> p (q t) w", w=D), ALU.add))
                    st.wait()
                st.end_pass()
            last = Steps(v, end_own)
            for w in range(D):
                last.did(nc.vector.tensor_tensor_scan(sums[:, :, w], m["starts_not"][:], msg[:, :, w], 0.0, ALU.mult, ALU.add))
            lanes.vector(last, sums, D, True, p_lane, lanes_ready, lanes_turned, sums_in)


def gcn_first(core, io, d, m, lanes, base, qf, dinv, y0):
    nc, sem = core.nc, core.sem
    ctx, sb, ps = stage(core)
    sums = sb("gf_sums", [P, ET, D])
    idx, rows = sb("gf_idx", [P, 2, G], I32), sb("gf_rows", [P, 2, G, D])
    x3, xc, sq, h = (sb(f"gf_{n}", [P, G, D]) for n in ("x3", "xc", "sq", "h"))
    s, var, root, rs = sb("gf_s", [P, G]), sb("gf_var", [P, 2, G]), sb("gf_root", [P, 2, G]), sb("gf_rs", [P, G])
    p_lane = ps("p_gf_lane", [P, 512])
    two = lambda name: [sem(f"{name}{k}") for k in range(2)]
    lanes_ready, lanes_turned, sums_in, stored = sem("gf_lanes_in"), sem("gf_lanes_turned"), sem("gf_sums_in"), sem("gf_stored")
    idx_in, got, used = sem("gf_idx_in"), two("gf_got"), sem("gf_used")
    var_in, root_in, own, end_own = sem("gf_var_in"), sem("gf_root_in"), sem("gf_own"), sem("gf_end_own")
    LOOP = EC // 2
    with ctx, nc.Block() as block:
        @block.sync
        def _(sp):
            sp.wait_ge(sums_in, D)
            sp.dma_start(d["t3a"][1:EP + 1, :].rearrange("(p t) w -> p t w", p=P), sums[:]).then_inc(stored, DMA)
            sp.wait_ge(stored, DMA)

        @block.gpsimd
        def _(pool):
            gather_rows(core, pool, d["t2"], idx, rows, idx_in, used, got)

        @block.scalar
        def _(act):
            for i, last in passes(act, LOOP):
                for k in range(2):
                    place_indices(nc, act, i, k, qf, idx, idx_in, got)
                    act.wait_ge(var_in, 2 * i + k + 1)
                    nc.scalar.activation(root[:, k], var[:, k], ACT.Sqrt).then_inc(root_in, 1)

        @block.tensor
        def _(pe):
            lanes.tensor(pe, D, True, p_lane, lanes_ready, lanes_turned)

        @block.vector
        def _(v):
            tt = nc.vector.tensor_tensor
            v.sem_inc(used, 2)
            st = Steps(v, own, STEPS_GF)
            for i, _ in passes(v, LOOP):
                st.start_pass(i)
                for k in range(2):
                    c, at = 2 * i + k, cols(i * (2 * G) + k * G, G)
                    v.wait_ge(got[k], (i + 1) * (G * DMA))
                    tt(x3[:], base[:, at, :], rows[:, k], ALU.add).then_inc(used, 1)
                    v.wait_ge(used, c + 3)
                    centre(nc, st, x3[:], xc[:], sq[:], s[:], var[:, k], var_in)
                    v.wait_ge(root_in, c + 1)
                    scale_relu(nc, st, root[:, k], rs[:], xc[:], h[:])
                    st.wait()
                    st.did(tt(y0[:, at, :], h[:], over(dinv[:, at], D), ALU.mult))
                    st.wait()
                st.end_pass()
            last = Steps(v, end_own)
            for w in range(D):
                last.did(nc.vector.tensor_tensor_scan(sums[:, :, w], m["starts_not"][:], y0[:, :, w], 0.0, ALU.mult, ALU.add))
            lanes.vector(last, sums, D, True, p_lane, lanes_ready, lanes_turned, sums_in)


def gather_rows(core, pool, table, idx, rows, idx_in, used, got):
    nc = core.nc
    for i, _ in passes(pool, EC // 2):
        for k in range(2):
            pool.wait_ge(idx_in, 2 * i + k + 1)
            pool.wait_ge(used, 2 * i + k + 1)
            settle(core, pool)
            for t in range(G):
                nc.gpsimd.indirect_dma_start(
                    out=rows[:, k, t, :], out_offset=None, in_=table[:, :],
                    in_offset=bass.IndirectOffsetOnAxis(ap=idx[:, k, t:t + 1], axis=0)).then_inc(got[k], DMA)


def place_indices(nc, act, i, k, qf, idx, idx_in, got):
    act.wait_ge(got[k], i * (G * DMA))
    nc.scalar.copy(idx[:, k, :], qf[:, cols(i * (2 * G) + k * G, G)]).then_inc(idx_in, 1)


def turn_groups(W):
    n = P // W if P // W < TG else TG
    return [(a, min(n, G - a)) for a in range(0, G, n)]


def gcn_next(core, io, d, m, lanes, W, weights, bias, table, sums_d, y, y_out, sums, qf, dinv):
    nc, sem = core.nc, core.sem
    ctx, sb, ps = stage(core)
    n_ = f"g{W}_"
    groups = turn_groups(W)
    n0 = groups[0][1]
    W2 = 2 * W
    idx, rows = sb(n_ + "idx", [P, 2, G], I32), sb(n_ + "rows", [P, 2, G, W])
    a, agg = sb(n_ + "a", [P, G, W]), sb(n_ + "agg", [P, 2, G, W])
    wt, bs, ones = sb(n_ + "w", [n0 * W, n0 * W2]), sb(n_ + "b", [1, n0 * W2]), sb(n_ + "ones", [1, P])
    turned = sb(n_ + "turned", [n0 * W, 2, len(groups), P])
    p_turn = ps(n_ + "p_turn", [n0 * W, len(groups), P])
    p_out = [ps(n_ + f"p_out{q}", [P, n0 * W2]) for q in range(len(groups))]
    p_lane = ps(n_ + "p_lane", [P, 512])
    two = lambda name: [sem(n_ + f"{name}{k}") for k in range(2)]
    consts, lanes_ready, lanes_turned, sums_in, stored = sem(n_ + "consts"), sem(n_ + "lanes_in"), sem(n_ + "lanes_turned"), sem(n_ + "sums_in"), sem(n_ + "stored")
    idx_in, got, used, own, end_own, ones_in = sem(n_ + "idx_in"), two("got"), sem(n_ + "used"), sem(n_ + "own"), sem(n_ + "end_own"), sem(n_ + "ones_in")
    agg_in, turn_in, turned_in, out_in, out_read = sem(n_ + "agg_in"), sem(n_ + "turn_in"), sem(n_ + "turned_in"), sem(n_ + "out_in"), sem(n_ + "out_read")
    LOOP = EC // 2
    NG = len(groups)
    with ctx, nc.Block() as block:
        @block.sync
        def _(sp):
            sp.dma_start(wt[:], weights).then_inc(consts, DMA)
            sp.dma_start(bs[:], bias).then_inc(consts, DMA)
            sp.wait_ge(sums_in, W2)
            sp.dma_start(sums_d[1:EP + 1, :].rearrange("(p t) w -> p t w", p=P), sums[:]).then_inc(stored, DMA)
            sp.wait_ge(stored, DMA)

        @block.gpsimd
        def _(pool):
            gather_rows(core, pool, table, idx, rows, idx_in, used, got)

        @block.scalar
        def _(act):
            for i, _ in passes(act, LOOP):
                for k in range(2):
                    place_indices(nc, act, i, k, qf, idx, idx_in, got)
                    act.wait_ge(turn_in, 2 * i + k + 1)
                    n_last = groups[-1][1]
                    if n_last == n0:
                        nc.scalar.copy(turned[:, k], p_turn[:]).then_inc(turned_in, 1)
                    else:
                        nc.scalar.copy(turned[:, k, 0:NG - 1], p_turn[:, 0:NG - 1, :])
                        nc.scalar.copy(turned[0:n_last * W, k, NG - 1], p_turn[0:n_last * W, NG - 1, :]).then_inc(turned_in, 1)

        @block.tensor
        def _(pe):
            pe.wait_ge(consts, 2 * DMA)
            pe.wait_ge(ones_in, 1)
            for i, _ in passes(pe, LOOP):
                for k in range(2):
                    c = 2 * i + k
                    pe.wait_ge(agg_in, c + 1)
                    for q, (t, n) in enumerate(groups):
                        mm = nc.tensor.transpose(p_turn[0:n * W, q, :], agg[:, k, t:t + n, :].rearrange("p t w -> p (t w)"), m["ident"][:])
                    mm.then_inc(turn_in, 1)
                    pe.wait_ge(out_read, c * NG)
                    pe.wait_ge(turned_in, c + 1)
                    for q, (t, n) in enumerate(groups):
                        nc.tensor.matmul(p_out[q][:, 0:n * W2], ones[:], bs[:, 0:n * W2], start=True, stop=False)
                        mm = nc.tensor.matmul(p_out[q][:, 0:n * W2], turned[0:n * W, k, q, :], wt[0:n * W, 0:n * W2],
                                              start=False, stop=True)
                    mm.then_inc(out_in, 1)
            lanes.tensor(pe, W2, True, p_lane, lanes_ready, lanes_turned)

        @block.vector
        def _(v):
            tt, stt = nc.vector.tensor_tensor, nc.vector.scalar_tensor_tensor
            nc.vector.memset(ones[:], 1.0).then_inc(ones_in, 1)
            v.sem_inc(used, 2)
            st = Steps(v, own)

            def aggregate(i, k, c):
                at = cols(i * (2 * G) + k * G, G)
                v.wait_ge(got[k], (i + 1) * (G * DMA))
                tt(a[:], rows[:, k], y[:, at, :], ALU.add).then_inc(used, 1)
                v.wait_ge(used, c + 3)
                tt(agg[:, k], a[:], over(dinv[:, at], W), ALU.mult).then_inc(agg_in, 1)

            def finish(i, k, c):
                v.wait_ge(out_in, c + 1)
                for q, (t, n) in enumerate(groups):
                    at = cols(i * (2 * G) + k * G + t, n)
                    stt(y_out[:, at, :], p_out[q][:, 0:n * W2].rearrange("p (t w) -> p t w", w=W2), 0.0,
                        over(dinv[:, at], W2), ALU.max, ALU.mult).then_inc(out_read, 1)

            aggregate(0, 0, 0)
            for i, last in passes(v, LOOP, last_apart=True):
                aggregate(i, 1, 2 * i + 1)
                finish(i, 0, 2 * i)
                if not last:
                    aggregate(i + 1, 0, 2 * i + 2)
                finish(i, 1, 2 * i + 1)
            v.wait_ge(out_read, EC * NG)
            last = Steps(v, end_own)
            for w in range(W2):
                last.did(nc.vector.tensor_tensor_scan(sums[:, :, w], m["starts_not"][:], y_out[:, :, w], 0.0, ALU.mult, ALU.add))
            lanes.vector(last, sums, W2, True, p_lane, lanes_ready, lanes_turned, sums_in)


def final_scatter(core, io, d, m):
    nc, sem = core.nc, core.sem
    ctx, sb, ps = stage(core)
    rows, idx = sb("fs_rows", [P, 2, G, FW]), sb("fs_idx", [P, 2, G], I32)
    two = lambda name: [sem(f"{name}{k}") for k in range(2)]
    rows_in, idx_in, sent = two("fs_rows_in"), sem("fs_idx_in"), two("fs_sent")
    LOOP = EC // 2
    parts = []
    at = 0
    for name in ("t2", "t3a", "t3b", "t3c"):
        w = d[name].shape[1]
        parts.append((d[name][1:EP + 1, :].rearrange("(p t) w -> p t w", p=P), at, w))
        at += w
    with ctx, nc.Block() as block:
        @block.sync
        def _(sp):
            for i, _ in passes(sp, LOOP):
                for k in range(2):
                    sp.wait_ge(sent[k], i * (G * DMA))
                    for src, a, w in parts:
                        sp.dma_start(rows[:, k, :, a:a + w], src[:, cols(i * (2 * G) + k * G, G), :]).then_inc(rows_in[k], DMA)

        @block.scalar
        def _(act):
            for i, _ in passes(act, LOOP):
                for k in range(2):
                    act.wait_ge(sent[k], i * (G * DMA))
                    nc.scalar.copy(idx[:, k, :], m["end_b"][:, cols(i * (2 * G) + k * G, G)]).then_inc(idx_in, 1)

        @block.gpsimd
        def _(pool):
            for i, _ in passes(pool, LOOP):
                for k in range(2):
                    pool.wait_ge(idx_in, 2 * i + k + 1)
                    pool.wait_ge(rows_in[k], (i + 1) * (4 * DMA))
                    settle(core, pool)
                    for t in range(G):
                        nc.gpsimd.indirect_dma_start(
                            out=d["f"][:, :], out_offset=bass.IndirectOffsetOnAxis(ap=idx[:, k, t:t + 1], axis=0),
                            in_=rows[:, k, t, :], in_offset=None, bounds_check=NP - 1, oob_is_err=False).then_inc(sent[k], DMA)
            for k in range(2):
                pool.wait_ge(sent[k], LOOP * G * DMA)


def node_base(core, io, d, m, nbase, ndinv):
    nc, sem = core.nc, core.sem
    ctx, sb, ps = stage(core)
    GN = 28
    NQ = GN // TG
    x, a0, a1 = sb("nb_x", [P, 2, GN, D]), sb("nb_a0", [P, 2, GN, A0W]), sb("nb_a1", [P, 2, GN, D])
    x1, xc, sq, h, t1, t2, t3, x2 = (sb(f"nb_{n}", [P, GN, D]) for n in ("x1", "xc", "sq", "h", "t1", "t2", "t3", "x2"))
    h2 = sb("nb_h2", [P, 2, GN, D])
    s, rs = sb("nb_s", [P, GN]), sb("nb_rs", [P, GN])
    var, root = sb("nb_var", [P, 3, GN]), sb("nb_root", [P, 3, GN])
    root_w, turned = sb("nb_root_w", [KB, TG * D]), sb("nb_turned", [KB, 2, NQ, P])
    p_turn = [ps(f"nb_p_turn{k}", [TG * D, NQ, P]) for k in range(2)]
    p_lin = [ps(f"nb_p_lin{k}", [P, NQ, TG * D]) for k in range(2)]
    two = lambda name: [sem(f"{name}{k}") for k in range(2)]
    consts, rows_in, used, var_in, root_in, own = sem("nb_consts"), two("nb_rows_in"), sem("nb_used"), sem("nb_var_in"), sem("nb_root_in"), sem("nb_own")
    h_in, turn_in, turned_in, lin_in, ones_in = sem("nb_h_in"), sem("nb_turn_in"), sem("nb_turned_in"), sem("nb_lin_in"), sem("nb_ones_in")
    LOOP = NT // GN // 2
    blk = lambda ap: ap[0:NP, :].rearrange("(p t) w -> p t w", p=P)
    with ctx, nc.Block() as block:
        @block.sync
        def _(sp):
            sp.dma_start(root_w[:], io["root_w"]).then_inc(consts, DMA)
            for i, _ in passes(sp, LOOP):
                for k in range(2):
                    at = cols(i * (2 * GN) + k * GN, GN)
                    sp.wait_ge(used, 2 * i + k + 1)
                    for dst, src in ((x, io["x"]), (a0, d["a0"]), (a1, d["a1"])):
                        sp.dma_start(dst[:, k], blk(src)[:, at, :]).then_inc(rows_in[k], DMA)

        @block.scalar
        def _(act):
            act.wait_ge(ones_in, 1)
            for i, _ in passes(act, LOOP):
                for k in range(2):
                    c = 2 * i + k
                    for r in range(3):
                        act.wait_ge(var_in, 3 * c + r + 1)
                        nc.scalar.activation(root[:, r], var[:, r], ACT.Sqrt).then_inc(root_in, 1)
                    act.wait_ge(turn_in, c + 1)
                    nc.scalar.copy(turned[0:TG * D, k], p_turn[k][:]).then_inc(turned_in, 1)

        @block.tensor
        def _(pe):
            pe.wait_ge(consts, DMA)
            for i, _ in passes(pe, LOOP):
                for k in range(2):
                    c = 2 * i + k
                    pe.wait_ge(h_in, c + 1)
                    for q in range(NQ):
                        mm = nc.tensor.transpose(p_turn[k][:, q, :], h2[:, k, q * TG:(q + 1) * TG, :].rearrange("p t w -> p (t w)"), m["ident"][:])
                    mm.then_inc(turn_in, 1)
                    pe.wait_ge(turned_in, c + 1)
                    for q in range(NQ):
                        mm = nc.tensor.matmul(p_lin[k][:, q, :], turned[:, k, q, :], root_w[:], start=True, stop=True)
                    mm.then_inc(lin_in, 1)

        @block.vector
        def _(v):
            tt, ts, stt = nc.vector.tensor_tensor, nc.vector.tensor_scalar, nc.vector.scalar_tensor_tensor
            nc.vector.memset(turned[:], 1.0).then_inc(ones_in, 1)
            v.sem_inc(used, 2)
            st = Steps(v, own, STEPS_NB)
            for i, _ in passes(v, LOOP):
                st.start_pass(i)
                for k in range(2):
                    c, at = 2 * i + k, cols(i * (2 * GN) + k * GN, GN)
                    v.wait_ge(rows_in[k], (i + 1) * (3 * DMA))
                    st.did(tt(x1[:], x[:, k], a0[:, k, :, 0:D], ALU.add))
                    ts(var[:, 0], a0[:, k, :, D], 1.0, None, ALU.add).then_inc(var_in, 1)
                    st.wait()
                    centre(nc, st, x1[:], xc[:], sq[:], s[:], var[:, 1], var_in)
                    v.wait_ge(root_in, 3 * c + 1)
                    st.did(nc.vector.reciprocal(ndinv[:, at], root[:, 0]))
                    v.wait_ge(root_in, 3 * c + 2)
                    scale_relu(nc, st, root[:, 1], rs[:], xc[:], h[:])
                    st.wait()
                    st.did(ts(t1[:], h[:], -0.2, 1.0, ALU.mult, ALU.add))
                    st.did(stt(t2[:], h[:], -1.0, h[:], ALU.add, ALU.mult))
                    st.did(stt(x2[:], x1[:], 0.1, a1[:, k], ALU.add, ALU.add))
                    st.wait()
                    st.did(tt(t3[:], t1[:], t2[:], ALU.mult))
                    st.wait()
                    tt(x2[:], x2[:], t3[:], ALU.add).then_inc(used, 1)
                    v.wait_ge(used, c + 3)
                    centre(nc, st, x2[:], xc[:], sq[:], s[:], var[:, 2], var_in)
                    v.wait_ge(root_in, 3 * c + 3)
                    st.did(nc.vector.reciprocal(rs[:], root[:, 2]))
                    st.wait()
                    stt(h2[:, k], xc[:], 0.0, over(rs[:], D), ALU.max, ALU.mult).then_inc(h_in, 1)
                    v.wait_ge(lin_in, c + 1)
                    st.did(tt(nbase[:, at, :], x2[:], p_lin[k][:].rearrange("p q (t w) -> p (q t) w", w=D), ALU.add))
                st.end_pass()


class Turn:

    def __init__(self, i, kk, whole):
        self.i, self.kk, self.whole = i, kk, whole

    def chunk(self, lag, n):
        o = self.kk - lag
        if not self.whole and not 0 <= 4 * self.i + o < n:
            return None
        return 4 * self.i + o, self.i + o // 4, o % 4, 2 * self.i + o // 2, o % 2


def pipeline(eng, n, lags, steps=None):
    total, first = n + lags, -(-lags // 4) + 1
    begun = 0
    for i in range(first):
        for kk in range(4):
            yield Turn(i, kk, False)
    if steps:
        begun = steps.k
    with eng.Fori(first, n // 4) as i:
        if steps:
            steps.base, steps.k = begun + (i - first) * steps.per_pass, 0
        for kk in range(4):
            yield Turn(i, kk, True)
        if steps:
            steps.end_pass()
    if steps:
        steps.base, steps.k = begun + (n // 4 - first) * steps.per_pass, 0
    for j in range(n, total):
        yield Turn(n // 4, j - n, False)


def node_gcn(core, io, d, m, nbase, ndinv, out):
    nc, sem = core.nc, core.sem
    ctx, sb, ps = stage(core)
    NC = NT // G
    D2, D4, D8 = 2 * D, 4 * D, 8 * D
    HALF = G * P // 4
    LB, LC, LT, LM, LO, LS = 1, 2, 2, 3, 4, 6
    groups1 = turn_groups(D2)
    n1 = groups1[0][1]
    f = sb("ng_f", [P, 4, G, FW])
    xc, sq, h, y0, a0 = (sb(f"ng_{n}", [P, G, D]) for n in ("xc", "sq", "h", "y0", "a0"))
    s, var, root, rs = sb("ng_s", [P, G]), sb("ng_var", [P, G]), sb("ng_root", [P, G]), sb("ng_rs", [P, G])
    agg0, y1, a1, agg1 = sb("ng_agg0", [P, G, D]), sb("ng_y1", [P, G, D2]), sb("ng_a1", [P, G, D2]), sb("ng_agg1", [P, G, D2])
    y2, a2, agg2 = sb("ng_y2", [P, G, D4]), sb("ng_a2", [P, G, D4]), sb("ng_agg2", [P, G, D4])
    tu0, tu1, tu2 = sb("ng_tu0", [TG * D, 2, P]), sb("ng_tu1", [P, 4, P]), sb("ng_tu2", [P, 2, HG * P])
    h3, h4, h5 = sb("ng_h3", [P, 2, 2, HALF]), sb("ng_h4", [P, 2, HALF]), sb("ng_h5", [D4 + 1, 2 * HALF])
    res = sb("ng_res", [P, 2, G, D])
    ones = sb("ng_ones", [1, P])
    w1, b1 = sb("ng_w1", [TG * D, TG * D2]), sb("ng_b1", [1, TG * D2])
    w2, b2, w3, b3 = sb("ng_w2", [P, 2 * P]), sb("ng_b2", [1, 2 * P]), sb("ng_w3", [P, D8]), sb("ng_b3", [P, 1])
    wl1, bl1, wl2, bl2, wl3 = sb("ng_wl1", [P, D4]), sb("ng_bl1", [P, 1]), sb("ng_wl2", [P, D4]), sb("ng_bl2", [D4, 1]), sb("ng_wl3", [D4 + 1, D2])
    p_ao = ps("ng_p_ao", [P, 512])
    p_t0, p_o = p_ao[0:TG * D, 0:2 * P].rearrange("p (q x) -> p q x", q=2), p_ao[:, 2 * P:2 * P + G * D]
    p_l1, p_t = ps("ng_p_l1", [P, 512]), ps("ng_p_t", [P, 4, P])
    p_l2 = [ps(f"ng_p_l2{q}", [P, 512]) for q in range(2)]
    p_c, p_d, p_e = ps("ng_p_c", [P, 512]), ps("ng_p_d", [P, 512]), ps("ng_p_e", [D4, 512])
    consts, f_in, res_out, used = sem("ng_consts"), [sem(f"ng_f_in{k}") for k in range(4)], [sem(f"ng_res_out{k}") for k in range(2)], sem("ng_used")
    var_in, root_in, own, ready = sem("ng_var_in"), sem("ng_root_in"), sem("ng_own"), sem("ng_ready")
    agg0_in, agg1_in, agg2_in, res_in, l1_read, l2_read = (sem(f"ng_{n}") for n in ("agg0_in", "agg1_in", "agg2_in", "res_in", "l1_read", "l2_read"))
    t0_in, t1_in, t2_in, l1_in, l2_in, c_in, d_in, e_in, o_in = (sem(f"ng_{n}") for n in ("t0_in", "t1_in", "t2_in", "l1_in", "l2_in", "c_in", "d_in", "e_in", "o_in"))
    tu0_in, tu1_in, tu2_in, h3_in, h4_in, h5_in = (sem(f"ng_{n}") for n in ("tu0_in", "tu1_in", "tu2_in", "h3_in", "h4_in", "h5_in"))
    loads = [(w1, "w1"), (b1, "b1"), (w2, "w2"), (b2, "b2"), (w3, "w3"), (b3, "b3"), (wl1, "wl1"), (bl1, "bl1"), (wl2, "wl2"), (bl2, "bl2"), (wl3, "wl3")]
    f_rows, out_rows = d["f"].rearrange("(p t) w -> p t w", p=P), out.rearrange("(p t) w -> p t w", p=P)
    tiles = lambda c: cols(c * G, G)

    with ctx, nc.Block() as block:
        @block.sync
        def _(sp):
            for dst, name in loads:
                sp.dma_start(dst[:], io[name]).then_inc(consts, DMA)
            for turn in pipeline(sp, NC, LS):
                if ch := turn.chunk(0, NC):
                    c, m4, k4, m2, k2 = ch
                    sp.wait_ge(used, c + 1)
                    sp.dma_start(f[:, k4], f_rows[:, tiles(c), :]).then_inc(f_in[k4], DMA)
                if ch := turn.chunk(LS, NC):
                    c, m4, k4, m2, k2 = ch
                    sp.wait_ge(res_in, c + 1)
                    sp.dma_start(out_rows[:, tiles(c), :], res[:, k2]).then_inc(res_out[k2], DMA)
            for k in range(2):
                sp.wait_ge(res_out[k], NC // 2 * DMA)

        @block.tensor
        def _(pe):
            mmul = nc.tensor.matmul
            pe.wait_ge(consts, len(loads) * DMA)
            pe.wait_ge(ready, 2)

            def first(g, par, half):
                c, m4, k4, m2, k2 = g
                n = 4 * c + 2 * half + par
                pe.wait_ge(h3_in, n)
                if par == 0 and half == 0:
                    pe.wait_ge(tu2_in, 2 * c + 2)
                r = slice(par * D4, (par + 1) * D4)
                mmul(p_c[:, 0:HALF], w3[r, :], tu2[r, k2, half * HALF:(half + 1) * HALF], start=True, stop=True).then_inc(c_in, 1)

            def second(g, par, half):
                c = g[0]
                if par == 0:
                    pe.wait_ge(h4_in, 2 * c + half)
                pe.wait_ge(h3_in, 4 * c + 2 * half + par + 1)
                mm = mmul(p_d[par * D4:(par + 1) * D4, 0:HALF], wl1[:], h3[:, par, half], start=True, stop=True)
                if par == 1:
                    mm.then_inc(d_in, 1)

            def third(g, half):
                c = g[0]
                pe.wait_ge(h4_in, 2 * c + half + 1)
                pe.wait_ge(h5_in, 2 * c + half)
                mmul(p_e[:, 0:HALF], wl2[:], h4[:, half], start=True, stop=True).then_inc(e_in, 1)

            def turn2(g, q):
                c = g[0]
                if q == 0:
                    pe.wait_ge(agg2_in, c + 1)
                    pe.wait_ge(tu1_in, c + 1)
                else:
                    pe.wait_ge(tu2_in, 2 * c + 1)
                for j in range(4 if q == 0 else 3):
                    t = 2 * (4 * q + j)
                    mm = nc.tensor.transpose(p_t[:, j, :], agg2[:, t:t + 2, :].rearrange("p t w -> p (t w)"), m["ident"][:])
                mm.then_inc(t2_in, 1)

            for turn in pipeline(pe, NC, LM):
                a, b, g2, g = turn.chunk(0, NC), turn.chunk(LB, NC), turn.chunk(LT, NC), turn.chunk(LM, NC)
                if g:
                    first(g, 0, 0)
                if g2:
                    turn2(g2, 0)
                if g:
                    first(g, 1, 0)
                    second(g, 0, 0)
                if g2:
                    turn2(g2, 1)
                if g:
                    second(g, 1, 0)
                    first(g, 0, 1)
                if b:
                    pe.wait_ge(agg1_in, b[0] + 1)
                    pe.wait_ge(tu2_in, 2 * b[0])
                    for q, (t, n) in enumerate(groups1):
                        mm = nc.tensor.transpose(p_t[0:n * D2, q, :], agg1[:, t:t + n, :].rearrange("p t w -> p (t w)"), m["ident"][:])
                    mm.then_inc(t1_in, 1)
                if g:
                    third(g, 0)
                    first(g, 1, 1)
                    second(g, 0, 1)
                if b:
                    pe.wait_ge(tu1_in, b[0] + 1)
                    pe.wait_ge(l2_read, 4 * b[0])
                    for q, (t, n) in enumerate(groups1):
                        o = p_l2[q // 2][:, (q % 2) * 2 * P:(q % 2) * 2 * P + n * D4]
                        mmul(o, ones[:], b2[:, 0:n * D4], start=True, stop=False)
                        mm = mmul(o, tu1[0:n * D2, q, :], w2[0:n * D2, 0:n * D4], start=False, stop=True)
                    mm.then_inc(l2_in, 1)
                if g:
                    second(g, 1, 1)
                if a:
                    pe.wait_ge(agg0_in, a[0] + 1)
                    pe.wait_ge(tu0_in, a[0])
                    if g:
                        pe.wait_ge(res_in, g[0])
                    for q in range(2):
                        mm = nc.tensor.transpose(p_t0[:, q, :], agg0[:, q * TG:(q + 1) * TG, :].rearrange("p t w -> p (t w)"), m["ident"][:])
                    mm.then_inc(t0_in, 1)
                if g:
                    third(g, 1)
                if a:
                    pe.wait_ge(tu0_in, a[0] + 1)
                    pe.wait_ge(l1_read, a[0])
                    for q in range(2):
                        o = p_l1[:, q * TG * D2:(q + 1) * TG * D2]
                        mmul(o, ones[:], b1[:], start=True, stop=False)
                        mm = mmul(o, tu0[:, q, :], w1[:], start=False, stop=True)
                    mm.then_inc(l1_in, 1)
                if g:
                    pe.wait_ge(h5_in, 2 * g[0] + 2)
                    pe.wait_ge(res_in, g[0])
                    if a:
                        pe.wait_ge(tu0_in, a[0] + 1)
                    for j in range(HG):
                        mm = mmul(p_o[:, j * D2:(j + 1) * D2], h5[:, j * P:(j + 1) * P], wl3[:], start=True, stop=True)
                    mm.then_inc(o_in, 1)

        @block.scalar
        def _(act):
            relu = lambda o, i, bias: nc.scalar.activation(o, i, ACT.Relu, bias=bias)
            act.wait_ge(consts, len(loads) * DMA)
            act.wait_ge(ready, 2)

            def out3(g, par, half):
                act.wait_ge(c_in, 4 * g[0] + 2 * half + par + 1)
                relu(h3[:, par, half], p_c[:, 0:HALF], b3[:]).then_inc(h3_in, 1)

            def out4(g, half):
                act.wait_ge(d_in, 2 * g[0] + half + 1)
                relu(h4[:, half], p_d[:, 0:HALF], bl1[:]).then_inc(h4_in, 1)

            def out5(g, half):
                act.wait_ge(e_in, 2 * g[0] + half + 1)
                relu(h5[0:D4, half * HALF:(half + 1) * HALF], p_e[:, 0:HALF], bl2[:]).then_inc(h5_in, 1)

            def copy2(g, q):
                c, m4, k4, m2, k2 = g
                n = 4 if q == 0 else 3
                act.wait_ge(t2_in, 2 * c + q + 1)
                nc.scalar.copy(tu2[:, k2, q * 4 * P:(q * 4 + n) * P], p_t[:, 0:n, :].rearrange("p j x -> p (j x)")).then_inc(tu2_in, 1)

            for turn in pipeline(act, NC, LM):
                a, b, g2, g = turn.chunk(0, NC), turn.chunk(LB, NC), turn.chunk(LT, NC), turn.chunk(LM, NC)
                if g:
                    out3(g, 0, 0)
                if g2:
                    copy2(g2, 0)
                if g:
                    out3(g, 1, 0)
                if g2:
                    copy2(g2, 1)
                if g:
                    out3(g, 0, 1)
                    out4(g, 0)
                if b:
                    act.wait_ge(t1_in, b[0] + 1)
                    nl = groups1[-1][1]
                    nc.scalar.copy(tu1[:, 0:3, :], p_t[:, 0:3, :])
                    nc.scalar.copy(tu1[0:nl * D2, 3, :], p_t[0:nl * D2, 3, :]).then_inc(tu1_in, 1)
                if a:
                    act.wait_ge(var_in, a[0] + 1)
                    nc.scalar.activation(root[:], var[:], ACT.Sqrt).then_inc(root_in, 1)
                if g:
                    out3(g, 1, 1)
                    out5(g, 0)
                    out4(g, 1)
                if a:
                    act.wait_ge(t0_in, a[0] + 1)
                    nc.scalar.copy(tu0[:], p_t0).then_inc(tu0_in, 1)
                if g:
                    out5(g, 1)

        @block.vector
        def _(v):
            tt, stt = nc.vector.tensor_tensor, nc.vector.scalar_tensor_tensor
            nc.vector.memset(ones[:], 1.0).then_inc(ready, 1)
            nc.vector.memset(h5[:], 1.0).then_inc(ready, 1)
            v.sem_inc(used, 4)
            st = Steps(v, own, STEPS_NG)
            for turn in pipeline(v, NC, LO, st):
                if ch := turn.chunk(LC, NC):
                    c, m4, k4, m2, k2 = ch
                    v.wait_ge(l2_in, c + 1)
                    for q, (t, n) in enumerate(groups1):
                        o = p_l2[q // 2][:, (q % 2) * 2 * P:(q % 2) * 2 * P + n * D4].rearrange("p (t w) -> p t w", w=D4)
                        stt(y2[:, t:t + n, :], o, 0.0, over(ndinv[:, cols(c * G + t, n)], D4), ALU.max, ALU.mult).then_inc(l2_read, 1)
                    v.wait_ge(l2_read, 4 * c + 4)
                    tt(a2[:], y2[:], f[:, k4, :, 4 * D:8 * D], ALU.add).then_inc(used, 1)
                    v.wait_ge(used, c + 5)
                    tt(agg2[:], a2[:], over(ndinv[:, tiles(c)], D4), ALU.mult).then_inc(agg2_in, 1)
                if ch := turn.chunk(LB, NC):
                    c, m4, k4, m2, k2 = ch
                    v.wait_ge(l1_in, c + 1)
                    stt(y1[:], p_l1[:, 0:G * D2].rearrange("p (t w) -> p t w", w=D2), 0.0, over(ndinv[:, tiles(c)], D2),
                        ALU.max, ALU.mult).then_inc(l1_read, 1)
                    v.wait_ge(l1_read, c + 1)
                    st.did(tt(a1[:], y1[:], f[:, k4, :, 2 * D:4 * D], ALU.add))
                    st.wait()
                    tt(agg1[:], a1[:], over(ndinv[:, tiles(c)], D2), ALU.mult).then_inc(agg1_in, 1)
                if ch := turn.chunk(0, NC):
                    c, m4, k4, m2, k2 = ch
                    x3 = nbase[:, tiles(c), :]
                    v.wait_ge(f_in[k4], (m4 + 1) * DMA)
                    st.did(tt(x3, nbase[:, tiles(c), :], f[:, k4, :, 0:D], ALU.add))
                    st.wait()
                    settle(core, v)
                    centre(nc, st, x3, xc[:], sq[:], s[:], var[:], var_in)
                    v.wait_ge(root_in, c + 1)
                    scale_relu(nc, st, root[:], rs[:], xc[:], h[:])
                    st.wait()
                    st.did(tt(y0[:], h[:], over(ndinv[:, tiles(c)], D), ALU.mult))
                    st.wait()
                    st.did(tt(a0[:], y0[:], f[:, k4, :, D:2 * D], ALU.add))
                    st.wait()
                    tt(agg0[:], a0[:], over(ndinv[:, tiles(c)], D), ALU.mult).then_inc(agg0_in, 1)
                if ch := turn.chunk(LO, NC):
                    c, m4, k4, m2, k2 = ch
                    v.wait_ge(o_in, c + 1)
                    v.wait_ge(res_out[k2], m2 * DMA)
                    stt(res[:, k2], p_o.rearrange("p (t w) -> p t w", w=D), 0.0, nbase[:, tiles(c), :], ALU.max, ALU.add).then_inc(res_in, 1)


STEPS_MS, STEPS_EL, STEPS_GF, STEPS_NB, STEPS_NG = 112, 26, 14, 36, 40

INPUTS = ("x", "src_s", "dst_s", "next_s", "src_b", "dst_ext", "src_rows", "src_f", "ef_t", "ea_t", "wgt", "w_att", "root_w",
          "edge_w", "w1", "b1", "w2", "b2", "w3", "b3", "wl1", "bl1", "wl2", "bl2", "wl3", "ident", "sel", "before",
          "one_only", "pos_b", "pos1_s", "dump")


def gnn(nc, io, out):
    dram = lambda name, shape, dt=F32: nc.dram_tensor(name, shape, dt).ap()
    d = dict(xs=dram("xs_rows", [EP, D]), xd=dram("xd_rows", [EP, D]), t0=dram("t0_rows", [EP, D]),
             pen=dram("pen_row", [EP], BF16), cnt=dram("cnt_row", [EP]),
             a0=dram("att_nodes", [NP, A0W]), a1=dram("l1_nodes", [NP + HG * P, D]), f=dram("final_nodes", [NP, FW]),
             t2=dram("t2_rows", [EP + 1, D]), t3a=dram("t3a_rows", [EP + 1, D]),
             t3b=dram("t3b_rows", [EP + 1, 2 * D]), t3c=dram("t3c_rows", [EP + 1, 4 * D]))
    with ExitStack() as top:
        core = Core(nc)
        sb = lambda name, shape, dt=F32, ctx=top: ctx.enter_context(nc.sbuf_tensor(name, shape, dt))
        m = dict(ident=sb("ident", [P, P]), starts_not=sb("starts_not", [P, ET]), ends=sb("ends", [P, ET]),
                 ends_not=sb("ends_not", [P, ET]), cntpos_s=sb("cntpos_s", [P, ET, 2]),
                 end_s=sb("end_s", [P, ET], I32), end_b=sb("end_b", [P, ET], I32))
        lanes = Lanes(nc, sb, m["ident"])
        setup(core, io, d, lanes, m)
        core.end_stage()
        with ExitStack() as ctx:
            h0 = sb("h0", [P, ET, D], ctx=ctx)
            gather_sources(core, io, d, h0)
            core.end_stage()
            attention(core, io, d, m, h0)
            core.end_stage()
        with ExitStack() as edge:
            qf, dinv = sb("qf", [P, ET], ctx=edge), sb("dinv", [P, ET], ctx=edge)
            y1 = sb("y1", [P, ET, 2 * D], ctx=edge)
            with ExitStack() as c0:
                y0 = sb("y0", [P, ET, D], ctx=c0)
                with ExitStack() as c1:
                    base = sb("base", [P, ET, D], ctx=c1)
                    message_sum(core, io, d, m, lanes, base, qf, dinv, y0)
                    core.end_stage()
                    edge_layer(core, io, d, m, lanes, base)
                    core.end_stage()
                    gcn_first(core, io, d, m, lanes, base, qf, dinv, y0)
                    core.end_stage()
                with ExitStack() as c2:
                    sums = sb("y1_sums", [P, ET, 2 * D], ctx=c2)
                    gcn_next(core, io, d, m, lanes, D, io["w1"], io["b1"], d["t3a"], d["t3b"], y0, y1, sums, qf, dinv)
                    core.end_stage()
            with ExitStack() as c3:
                y2 = sb("y2", [P, ET, 4 * D], ctx=c3)
                gcn_next(core, io, d, m, lanes, 2 * D, io["w2"], io["b2"], d["t3b"], d["t3c"], y1, y2, y2, qf, dinv)
                core.end_stage()
        final_scatter(core, io, d, m)
        core.end_stage()
        with ExitStack() as ctx:
            nbase, ndinv = sb("node_base", [P, NT, D], ctx=ctx), sb("node_dinv", [P, NT], ctx=ctx)
            node_base(core, io, d, m, nbase, ndinv)
            core.end_stage()
            node_gcn(core, io, d, m, nbase, ndinv, out)
            core.end_stage()


def kernel(**inputs):
    import numpy as _np
    import ml_dtypes as _ml
    import concourse.bacc as _bacc
    from concourse import mybir as _mybir
    from concourse.bass_utils import run_bass_kernel_spmd as _run

    a = {k: _np.asarray(v) for k, v in inputs.items()}

    def padded(x, n, value=0):
        out = _np.full((n,) + x.shape[1:], value, x.dtype)
        out[:x.shape[0]] = x
        return out

    def diagonal(w, n):
        out = _np.zeros((n * w.shape[0], n * w.shape[1]), w.dtype)
        for q in range(n):
            out[q * w.shape[0]:(q + 1) * w.shape[0], q * w.shape[1]:(q + 1) * w.shape[1]] = w
        return out

    strided = lambda x: x.reshape(ET, P).T
    blocked = lambda x: x.reshape((P, ET) + x.shape[1:])
    row = lambda x: x[None, :]
    src = padded(a["src"].astype(_np.int32), EP, N + 1)
    dst = padded(a["dst"].astype(_np.int32), EP, N)
    dst_ext = _np.concatenate([_np.full(1, -1, _np.int32), dst, _np.full(1, -1, _np.int32)])
    ones = _np.ones((1, EP), _np.float32)
    pos = _np.arange(EP, dtype=_np.float32)
    io = dict(
        x=padded(a["x"], NP), src_s=strided(src), dst_s=strided(dst), next_s=strided(dst_ext[2:]), src_b=blocked(src),
        dst_ext=dst_ext, src_rows=row(blocked(src).T.reshape(-1)), src_f=blocked(src).astype(_np.float32),
        ef_t=_np.concatenate([padded(a["edge_attr_16"], EP).T, ones]),
        ea_t=_np.concatenate([blocked(padded(a["edge_attr_8"], EP)).transpose(2, 1, 0), _np.ones((1, ET, P), _np.float32)]),
        wgt=blocked(padded(a["edge_weight"], EP)),
        w_att=_np.concatenate([_np.concatenate([a["L0_gnn_W_attn"], a["L0_gnn_W_msg"]], 1),
                               row(_np.concatenate([a["L0_gnn_b_attn"], a["L0_gnn_b_msg"]]))]),
        root_w=_np.concatenate([diagonal(a["L2_gnn_root_w"], TG), row(_np.tile(a["L2_gnn_root_b"], TG))]),
        edge_w=_np.concatenate([a["L2_gnn_edge_w"], row(a["L2_gnn_edge_b"])]),
        w1=diagonal(a["L3_gnn_W1"], TG), b1=row(_np.tile(a["L3_gnn_b1"], TG)),
        w2=diagonal(a["L3_gnn_W2"], 4), b2=row(_np.tile(a["L3_gnn_b2"], 4)),
        w3=_np.tile(a["L3_gnn_W3"], (2, 1)), b3=a["L3_gnn_b3"][:, None],
        wl1=a["L3_gnn_Wl1"], bl1=_np.tile(a["L3_gnn_bl1"], 2)[:, None],
        wl2=diagonal(a["L3_gnn_Wl2"], 2), bl2=_np.tile(a["L3_gnn_bl2"], 2)[:, None],
        wl3=_np.concatenate([diagonal(a["L3_gnn_Wl3"], 2), row(_np.tile(a["L3_gnn_bl3"], 2))]),
        ident=_np.eye(P, dtype=_np.float32), sel=_np.tile(_np.eye(D, dtype=_np.float32), (P // D, 1)),
        before=_np.repeat(_np.triu(_np.ones((P, P)), 1).astype(_ml.bfloat16)[:, None, :], HG, 1),
        one_only=_np.repeat(_np.eye(1, 3 * D + 1).astype(_ml.bfloat16), P, 0),
        pos_b=blocked(pos), pos1_s=strided(pos + 1),
        dump=(NP + _np.arange(HG)[None, :] * P + _np.arange(P)[:, None]).astype(_np.float32))
    nc = _bacc.Bacc("TRN2", target_bir_lowering=False, num_devices=1)
    arrays, aps = {}, {}
    for name in INPUTS:
        arr = _np.ascontiguousarray(io[name])
        arrays[f"in_{name}"] = arr
        aps[name] = nc.dram_tensor(f"in_{name}", arr.shape, _mybir.dt.from_np(arr.dtype), kind="ExternalInput").ap()
    out = nc.dram_tensor("out_rows", (NP, D), F32, kind="ExternalOutput").ap()
    gnn(nc, aps, out)
    r = _run(nc, [arrays], core_ids=[0])
    return r.results[0]["out_rows"][:N]
```

```python
from contextlib import ExitStack

import concourse.bass as bass
from concourse import mybir

ALU = mybir.AluOpType
ACT = mybir.ActivationFunctionType
AX = mybir.AxisListType
F32 = mybir.dt.float32
BF16 = mybir.dt.bfloat16
I32 = mybir.dt.int32

P = 128
D = 16
N, E = 100000, 50000
NT = -(-N // (P * 56)) * 56
ET = -(-E // (P * 28)) * 28
NP, EP = NT * P, ET * P
G = 14
EC = ET // G
HG = G // 2
TG = 7
KB = TG * D + 1
A0W = D + 2
FW = D + D + 2 * D + 4 * D
FAR = 1 << 20
PEN = -1.0e30
EPS = 1e-5
LN_EXP_SET = 6
DMA = 16


class Steps:

    def __init__(self, eng, sem, per_pass=0):
        self.eng, self.sem, self.per_pass, self.base, self.k = eng, sem, per_pass, 0, 0

    def start_pass(self, i):
        self.base, self.k = i * self.per_pass, 0

    def end_pass(self):
        assert self.k == self.per_pass, f"{self.k} steps in a pass, not {self.per_pass}"

    def did(self, ins):
        ins.then_inc(self.sem, 1)
        self.k += 1

    def wait(self):
        since(self.eng, self.sem, self.base + self.k)


def passes(eng, n, last_apart=False):
    yield 0, False
    with eng.Fori(1, n - 1 if last_apart else n) as i:
        yield i, False
    if last_apart:
        yield n - 1, True


def settle(core, eng):
    eng.sem_inc(core.settled, 1)


def since(eng, sem, value):
    if not isinstance(value, int) or value > 0:
        eng.wait_ge(sem, value)


def run_on(nc, st, sums, starts_not, c, W):
    at = cols(0, G) if isinstance(c, int) and c == 0 else cols(c * G - 1, G + 1)
    for w in range(W):
        st.did(nc.vector.tensor_tensor_scan(sums[:, at, w], starts_not[:, at], sums[:, at, w], 0.0, ALU.mult, ALU.add))


def cols(start, n):
    return bass.ds(start, n)


def over(ap, w):
    return ap.rearrange("p (n o) -> p n o", o=1).to_broadcast([ap.shape[0], ap.shape[1], w])


def centre(nc, st, x, xc, sq, s, var, var_ready, x_read=None):
    v = nc.vector
    st.did(v.tensor_reduce(s, x, AX.X, ALU.add))
    st.wait()
    ins = v.scalar_tensor_tensor(xc, over(s, D), -1.0 / D, x, ALU.mult, ALU.add)
    if x_read:
        ins.then_inc(x_read[0], 1)
        st.eng.wait_ge(*x_read)
    else:
        st.did(ins)
        st.wait()
    st.did(v.tensor_tensor(sq, xc, xc, ALU.mult))
    st.wait()
    st.did(v.tensor_reduce(s, sq, AX.X, ALU.add))
    st.wait()
    v.tensor_scalar(var, s, 1.0 / D, EPS, ALU.mult, ALU.add).then_inc(var_ready, 1)


def scale_relu(nc, st, root, rs, xc, out):
    st.did(nc.vector.reciprocal(rs, root))
    st.wait()
    st.did(nc.vector.scalar_tensor_tensor(out, xc, 0.0, over(rs, D), ALU.max, ALU.mult))


class Lanes:

    def __init__(self, nc, sb, ident):
        self.nc, self.ident = nc, ident
        self.edge = sb("lane_edge", [P, 4 * D])
        self.turned = sb("lane_turned", [4 * D, P])
        self.chain = sb("lane_chain", [4 * D, P + 2])
        self.into = sb("lane_into", [P, 4 * D])
        self.head = sb("head", [P, ET])
        self.tail = sb("tail", [P, ET])
        self.no_start = sb("no_start", [4 * D, P])
        self.no_end = sb("no_end", [4 * D, P])

    def tensor(self, pe, W, forward, psum, lanes_ready, lanes_turned):
        nc = self.nc
        pe.wait_ge(lanes_ready, 1)
        nc.tensor.transpose(psum[0:W, 0:P], self.edge[:, 0:W], self.ident[:]).then_inc(lanes_turned, 1)
        pe.wait_ge(lanes_ready, 2)
        a = 0 if forward else 2
        nc.tensor.transpose(psum[:, P:P + W], self.chain[0:W, a:a + P],
                            self.ident[0:W, 0:W]).then_inc(lanes_turned, 1)

    def vector(self, st, sums, W, forward, psum, lanes_ready, lanes_turned, done):
        v, eng = self.nc.vector, st.eng
        st.wait()
        at = ET - 1 if forward else 0
        v.tensor_copy(self.edge[:, 0:W], sums[:, at, :]).then_inc(lanes_ready, 1)
        eng.wait_ge(lanes_turned, 1)
        st.did(v.tensor_copy(self.turned[0:W, :], psum[0:W, 0:P]))
        st.wait()
        if forward:
            ins = v.tensor_tensor_scan(self.chain[0:W, 1:P + 1], self.no_start[0:W, :], self.turned[0:W, :],
                                       0.0, ALU.mult, ALU.add)
        else:
            ins = v.tensor_tensor_scan(self.chain[0:W, P:0:-1], self.no_end[0:W, ::-1], self.turned[0:W, ::-1],
                                       0.0, ALU.mult, ALU.add)
        ins.then_inc(lanes_ready, 1)
        eng.wait_ge(lanes_turned, 2)
        st.did(v.tensor_copy(self.into[:, 0:W], psum[:, P:P + W]))
        st.wait()
        mask = self.head if forward else self.tail
        for w in range(W):
            v.scalar_tensor_tensor(sums[:, :, w], mask[:], self.into[:, w:w + 1], sums[:, :, w],
                                   ALU.mult, ALU.add).then_inc(done, 1)


class Core:

    def __init__(self, nc):
        self.nc, self.sems = nc, []
        self.settled = self.nc.alloc_semaphore(name="settled")

    def sem(self, name):
        self.sems.append(self.nc.alloc_semaphore(name=name))
        return self.sems[-1]

    def end_stage(self):
        self.nc.clear_and_free_semaphores(self.sems)
        self.nc.all_engine_barrier()
        self.sems = []


def stage(core):
    nc, ctx = core.nc, ExitStack()
    sb = lambda name, shape, dt=F32: ctx.enter_context(nc.sbuf_tensor(name, shape, dt))
    ps = lambda name, shape: ctx.enter_context(nc.psum_tensor(name, shape, F32))
    return ctx, sb, ps


def setup(core, io, d, lanes, m):
    nc, sem = core.nc, core.sem
    ctx, sb, ps = stage(core)
    Q = ET // 4
    ZW = 7168
    zeros = sb("zeros", [P, ZW])
    at_b, prev_b, next_b = sb("at_b", [P, ET], I32), sb("prev_b", [P, ET], I32), sb("next_b", [P, ET], I32)
    at_s, next_s = sb("at_s", [P, ET], I32), sb("next_s", [P, ET], I32)
    pos_b, pos1_s = sb("pos_b", [P, ET]), sb("pos1_s", [P, ET])
    starts, start_pos, first, cnt = sb("starts", [P, ET]), sb("start_pos", [P, ET]), sb("first", [P, ET]), sb("cnt", [P, ET])
    pen = sb("pen", [P, ET], BF16)
    cnt_rows = sb("cnt_rows", [Q, 4, P])
    lane_max, lane_from = sb("lane_max", [1, P]), sb("lane_from", [1, P + 2])
    bare = sb("bare", [P, 2])
    from_col = sb("from_col", [P, 1])
    p_rows, p_col, p_one = ps("p_rows", [4 * D, 2, P]), ps("p_col", [P, 512]), ps("p_one", [P, 512])
    p_cnt = ps("p_cnt", [P, 4, Q])
    loaded, zeros_in, filled, own = sem("setup_loaded"), sem("zeros_in"), sem("tables_filled"), sem("setup_own")
    max_in, from_in, bare_in = sem("lane_max_in"), sem("lane_from_in"), sem("bare_in")
    max_turned, from_turned, bare_turned, cnt_turned = sem("max_turned"), sem("from_turned"), sem("bare_turned"), sem("cnt_turned")
    pen_in, cnt_in, rows_out, cnt_back = sem("pen_in"), sem("cnt_in"), sem("rows_out"), sem("cnt_back")
    window = lambda k: io["dst_ext"][k:k + EP].rearrange("(p t) -> p t", p=P)
    loads = ((m["ident"][:], io["ident"]), (pos_b[:], io["pos_b"]), (pos1_s[:], io["pos1_s"]),
             (prev_b[:], window(0)), (at_b[:], window(1)), (next_b[:], window(2)),
             (at_s[:], io["dst_s"]), (next_s[:], io["next_s"]))
    fills = []
    for name in ("a0",):
        flat = d[name].rearrange("(p r) w -> p (r w)", p=P)
        fills += [(flat[:, a:min(a + ZW, flat.shape[1])], min(ZW, flat.shape[1] - a)) for a in range(0, flat.shape[1], ZW)]
    for name in ("t2", "t3a", "t3b"):
        fills.append((d[name][0:1, :], d[name].shape[1]))

    with ctx, nc.Block() as block:
        @block.sync
        def _(sp):
            for dst, src in loads:
                sp.dma_start(dst, src).then_inc(loaded, DMA)
            sp.wait_ge(pen_in, 1)
            sp.dma_start(d["pen"].rearrange("(p t) -> p t", p=P), pen[:]).then_inc(rows_out, DMA)
            sp.wait_ge(cnt_in, 1)
            sp.dma_start(d["cnt"].rearrange("(p t) -> p t", p=P), cnt[:]).then_inc(rows_out, DMA)
            sp.wait_ge(rows_out, 2 * DMA)
            sp.dma_start(cnt_rows[:], d["cnt"].rearrange("(f q p) -> q f p", f=4, p=P)).then_inc(cnt_back, DMA)

        @block.scalar
        def _(act):
            act.wait_ge(zeros_in, 1)
            for dst, width in fills:
                act.dma_start(dst, zeros[0:dst.shape[0], 0:width]).then_inc(filled, DMA)
            act.wait_ge(filled, DMA * len(fills))

        @block.tensor
        def _(pe):
            pe.wait_ge(loaded, DMA * len(loads))
            pe.wait_ge(max_in, 1)
            nc.tensor.transpose(p_one[0:1, 0:P], first[:, ET - 1:ET], m["ident"][:]).then_inc(max_turned, 1)
            pe.wait_ge(from_in, 1)
            nc.tensor.transpose(p_col[:, 0:1], lane_from[:, 0:P], m["ident"][0:1, 0:1]).then_inc(from_turned, 1)
            pe.wait_ge(bare_in, 2)
            for k in range(2):
                nc.tensor.matmul(p_rows[:, k, :], bare[:, k:k + 1].to_broadcast([P, 4 * D]), m["ident"][:],
                                 start=True, stop=True).then_inc(bare_turned, 1)
            pe.wait_ge(cnt_back, DMA)
            for f in range(4):
                mm = nc.tensor.transpose(p_cnt[:, f, :], cnt_rows[:, f, :], m["ident"][0:Q, 0:Q])
            mm.then_inc(cnt_turned, 1)

        @block.vector
        def _(v):
            st = Steps(v, own)
            tt, ts, scan = nc.vector.tensor_tensor, nc.vector.tensor_scalar, nc.vector.tensor_tensor_scan
            nc.vector.memset(zeros[:], 0.0).then_inc(zeros_in, 1)
            st.did(nc.vector.memset(lanes.chain[:], 0.0))
            st.did(nc.vector.memset(lane_from[:], 0.0))
            v.wait_ge(loaded, DMA * len(loads))
            st.did(tt(starts[:], at_b[:], prev_b[:], ALU.not_equal))
            st.did(tt(m["ends"][:], at_b[:], next_b[:], ALU.not_equal))
            st.did(tt(m["starts_not"][:], at_b[:], prev_b[:], ALU.is_equal))
            st.did(tt(m["ends_not"][:], at_b[:], next_b[:], ALU.is_equal))
            st.did(tt(cnt[:], at_s[:], next_s[:], ALU.is_equal))
            st.wait()
            st.did(scan(lanes.head[:], m["starts_not"][:], m["starts_not"][:], 1.0, ALU.mult, ALU.min))
            st.did(scan(lanes.tail[:, ::-1], m["ends_not"][:, ::-1], m["ends_not"][:, ::-1], 1.0, ALU.mult, ALU.min))
            st.did(nc.vector.scalar_tensor_tensor(m["end_s"][:], cnt[:], float(FAR), at_s[:], ALU.mult, ALU.add))
            st.did(nc.vector.scalar_tensor_tensor(m["end_b"][:], m["ends_not"][:], float(FAR), at_b[:], ALU.mult, ALU.add))
            st.did(tt(start_pos[:], starts[:], pos_b[:], ALU.mult))
            ts(pen[:], starts[:], PEN, None, ALU.mult).then_inc(pen_in, 1)
            st.wait()
            nc.vector.tensor_copy(bare[:, 0:1], lanes.head[:, ET - 1:ET]).then_inc(bare_in, 1)
            nc.vector.tensor_copy(bare[:, 1:2], lanes.tail[:, 0:1]).then_inc(bare_in, 1)
            scan(first[:], start_pos[:], start_pos[:], 0.0, ALU.max, ALU.max).then_inc(max_in, 1)
            v.wait_ge(max_turned, 1)
            st.did(nc.vector.tensor_copy(lane_max[:], p_one[0:1, 0:P]))
            st.wait()
            scan(lane_from[:, 1:P + 1], lane_max[:], lane_max[:], 0.0, ALU.max, ALU.max).then_inc(from_in, 1)
            v.wait_ge(from_turned, 1)
            st.did(nc.vector.tensor_copy(from_col[:], p_col[:, 0:1]))
            st.wait()
            st.did(ts(first[:], first[:], from_col[:], None, ALU.max))
            st.wait()
            st.did(tt(cnt[:], pos_b[:], first[:], ALU.subtract))
            st.wait()
            ts(cnt[:], cnt[:], 1.0, None, ALU.add).then_inc(cnt_in, 1)
            v.wait_ge(bare_turned, 2)
            st.did(nc.vector.tensor_copy(lanes.no_start[:], p_rows[:, 0, :]))
            st.did(nc.vector.tensor_copy(lanes.no_end[:], p_rows[:, 1, :]))
            st.did(nc.vector.tensor_copy(m["cntpos_s"][:, :, 1], pos1_s[:]))
            v.wait_ge(cnt_turned, 1)
            st.did(nc.vector.tensor_copy(m["cntpos_s"][:, :, 0], p_cnt[:].rearrange("p f q -> p (f q)")))
            st.wait()


def features(core, io, d):
    nc, sem = core.nc, core.sem
    ctx, sb, ps = stage(core)
    GN = 56
    x, row = sb("ft_x", [P, 2, GN, D]), sb("ft_row", [P, 2, GN, 2 * D])
    xc, sq = sb("ft_xc", [P, 2, GN, D]), sb("ft_sq", [P, GN, D])
    s, var, root, rs = sb("ft_s", [P, GN]), sb("ft_var", [P, 2, GN]), sb("ft_root", [P, 2, GN]), sb("ft_rs", [P, GN])
    x_in, row_out = [sem(f"ft_x_in{k}") for k in range(2)], [sem(f"ft_row_out{k}") for k in range(2)]
    inv_in, x_read, x_copied, var_in, root_in, row_in, own = (sem(f"ft_{n}") for n in ("inv_in", "x_read", "x_copied", "var_in", "root_in", "row_in", "own"))
    blk = lambda ap: ap.rearrange("(p t) w -> p t w", p=P)
    LOOP = NT // GN // 2
    with ctx, nc.Block() as block:
        @block.sync
        def _(sp):
            for i, _ in passes(sp, LOOP):
                for k in range(2):
                    c = 2 * i + k
                    since(sp, x_read, c - 1)
                    since(sp, x_copied, c - 1)
                    sp.dma_start(x[:, k], blk(io["x"])[:, cols(c * GN, GN), :]).then_inc(x_in[k], DMA)

        @block.scalar
        def _(act):
            for i, _ in passes(act, LOOP):
                for k in range(2):
                    c = 2 * i + k
                    act.wait_ge(x_in[k], (i + 1) * DMA)
                    since(act, row_out[k], i * DMA)
                    nc.scalar.copy(row[:, k, :, 0:D], x[:, k]).then_inc(x_copied, 1)
                    act.wait_ge(var_in, c + 1)
                    nc.scalar.activation(root[:, k], var[:, k], ACT.Sqrt).then_inc(root_in, 1)
                    act.wait_ge(x_copied, c + 1)
                    act.wait_ge(row_in, c + 1)
                    act.dma_start(blk(d["xh"])[:, cols(c * GN, GN), :], row[:, k]).then_inc(row_out[k], DMA)
            for k in range(2):
                act.wait_ge(row_out[k], LOOP * DMA)

        @block.vector
        def _(v):
            st = Steps(v, own, STEPS_FT)

            def finish(i, k):
                c = 2 * i + k
                v.wait_ge(root_in, c + 1)
                since(v, row_out[k], i * DMA)
                since(v, row_in, c)
                nc.vector.reciprocal(rs[:], root[:, k]).then_inc(inv_in, 1)
                v.wait_ge(inv_in, c + 1)
                nc.vector.scalar_tensor_tensor(row[:, k, :, D:2 * D], xc[:, k], 0.0, over(rs[:], D),
                                               ALU.max, ALU.mult).then_inc(row_in, 1)

            for i, _ in passes(v, LOOP):
                st.start_pass(i)
                for k in range(2):
                    v.wait_ge(x_in[k], (i + 1) * DMA)
                    since(v, var_in, 2 * i + k)
                    since(v, row_in, 2 * i + k - 1)
                    centre(nc, st, x[:, k], xc[:, k], sq[:], s[:], var[:, k], var_in, (x_read, 2 * i + k + 1))
                    if k or not isinstance(i, int):
                        finish(i if k else i - 1, 1 - k)
                st.end_pass()
            finish(LOOP - 1, 1)


def attention(core, io, d, m):
    nc, sem = core.nc, core.sem
    ctx, sb, ps = stage(core)
    C = 4
    W = C * P
    NCH = ET // C
    LOOP = NCH // 2
    ZW = 7168
    zeros = sb("att_zeros", [P, ZW])
    weights, sel = sb("att_w", [D + 1, 4 * P]), sb("att_sel", [P, D])
    ef, pen = sb("att_ef", [D + 1, 2, W]), sb("att_pen", [P, 2, W], BF16)
    hs, hb = sb("att_hs", [P, 2, C, D * D]), sb("att_hb", [P, 2, W])
    mxv = sb("att_mxv", [P, 2, 3, W])
    arg, ab = sb("att_arg", [P, 2, 2, W]), sb("att_ab", [P, 2, 2, W])
    top = sb("att_top", [P, 2, 2, W + 1])
    den, num = sb("att_den", [P, 2, 2, W]), sb("att_num", [P, 2, 2, W])
    part, ratio = sb("att_part", [P, 2, W]), sb("att_ratio", [P, 2, W])
    logd, inv = sb("att_log", [P, 2, W]), sb("att_inv", [P, 2, W])
    rows, end_idx = sb("att_rows", [P, 2, C, A0W]), sb("att_end", [P, 2, C], I32)
    xs_idx, xs_rows = sb("att_xsi", [P, 2, C], I32), sb("att_xsr", [P, 2, C, 2 * D])
    xd_idx, xd_rows = sb("att_xdi", [P, 2, C], I32), sb("att_xdr", [P, 2, C, D])
    p_hb, p_w = [ps(f"p_hb{u}", [P, W]) for u in range(2)], [ps(f"p_w{u}", [P, 2, W]) for u in range(2)]
    p_out = ps("p_att_out", [P, C, D])
    two = lambda name: [sem(f"att_{name}{k}") for k in range(2)]
    ef_in, pen_in, xsi_in, xdi_in = two("ef_in"), two("pen_in"), two("xsi_in"), two("xdi_in")
    xs_got, xs_kept, xd_got, xd_kept, t_kept, scattered = two("xs_got"), two("xs_kept"), two("xd_got"), two("xd_kept"), two("t_kept"), two("scattered")
    one = lambda *names: (sem(f"att_{n}") for n in names)
    consts, state_in, zeros_in, filled, own = one("consts", "state_in", "zeros_in", "filled", "own")
    hs_in, hb_out, hb_in, w_out, x_done, pen_read = one("hs_in", "hb_out", "hb_in", "w_out", "x_done", "pen_read")
    args_in, exp_done, part_in, den_in, log_in, inv_in = one("args_in", "exp_done", "part_in", "den_in", "log_in", "inv_in")
    ratio_in, out_in, rows_in, endi_in = one("ratio_in", "out_in", "rows_in", "endi_in")
    at_b = io["dst_ext"][1:1 + EP].rearrange("(p t) -> p t", p=P)
    xs, t0 = (d[n].rearrange("(t p) w -> p t w", p=P) for n in ("xs", "t0"))
    xd = d["xd"].rearrange("(p t) w -> p t w", p=P)
    fills = []
    for name in ("a1",):
        flat = d[name].rearrange("(p r) w -> p (r w)", p=P)
        fills += [(flat[:, a:min(a + ZW, flat.shape[1])], min(ZW, flat.shape[1] - a)) for a in range(0, flat.shape[1], ZW)]

    f_flat = d["f"].rearrange("(p r) w -> p (r w)", p=P)
    FZ = f_flat.shape[1] // NCH

    def steps(eng):
        for i, last in passes(eng, LOOP, last_apart=True):
            for kk in range(2):
                def at(offset, i=i, kk=kk, last=last):
                    o = kk + offset
                    if (last and o > 1) or (isinstance(i, int) and 2 * i + o < 0):
                        return None
                    return 2 * i + o, i + o // 2, o % 2
                yield at

    with ctx, nc.Block() as block:
        @block.sync
        def _(sp):
            def source_idx(c, i, k):
                since(sp, xs_got[k], i * (C * DMA))
                sp.dma_start(xs_idx[:, k, :], io["src_s"][:, cols(c * C, C)]).then_inc(xsi_in[k], DMA)

            def loads(c, i, k):
                since(sp, xd_got[k], i * (C * DMA))
                sp.dma_start(xd_idx[:, k, :], at_b[:, cols(c * C, C)]).then_inc(xdi_in[k], DMA)
                since(sp, w_out, 2 * c - 2)
                sp.dma_start(ef[:, k, :], io["ef_t"][:, cols(c * W, W)]).then_inc(ef_in[k], DMA)
                since(sp, pen_read, c - 1)
                if not isinstance(c, int):
                    settle(core, sp)
                sp.dma_start(pen[:, k, :], d["pen"].rearrange("(o e) -> o e", o=1)[:, cols(c * W, W)]
                             .to_broadcast([P, W])).then_inc(pen_in[k], DMA)

            def keep_sources(c, i, k):
                sp.wait_ge(xs_got[k], (i + 1) * (C * DMA))
                sp.dma_start(xs[:, cols(c * C, C), :], xs_rows[:, k, :, 0:D]).then_inc(xs_kept[k], DMA)

            def keep_targets(c, i, k):
                sp.wait_ge(xd_got[k], (i + 1) * (C * DMA))
                sp.dma_start(xd[:, cols(c * C, C), :], xd_rows[:, k]).then_inc(xd_kept[k], DMA)

            source_idx(0, 0, 0)
            source_idx(1, 0, 1)
            sp.dma_start(weights[:], io["w_att"]).then_inc(consts, DMA)
            sp.dma_start(sel[:], io["sel"]).then_inc(consts, DMA)
            loads(0, 0, 0)
            keep_sources(0, 0, 0)
            sp.wait_ge(zeros_in, 1)
            for dst, width in fills:
                sp.dma_start(dst, zeros[0:dst.shape[0], 0:width]).then_inc(filled, DMA)
            for at in steps(sp):
                sp.dma_start(f_flat[:, cols(at(0)[0] * FZ, FZ)], zeros[:, 0:FZ]).then_inc(filled, DMA)
                for part_of, offset in ((source_idx, 2), (loads, 1), (keep_sources, 1), (keep_targets, -1)):
                    if at(offset):
                        part_of(*at(offset))
            keep_targets(NCH - 1, LOOP - 1, 1)
            for k in range(2):
                sp.wait_ge(xs_kept[k], LOOP * DMA)
                sp.wait_ge(xd_kept[k], LOOP * DMA)
            sp.wait_ge(filled, (len(fills) + NCH) * DMA)

        @block.gpsimd
        def _(pool):
            def gather_sources(c, i, k):
                pool.wait_ge(xsi_in[k], (i + 1) * DMA)
                since(pool, hs_in, c - 1)
                since(pool, xs_kept[k], i * DMA)
                settle(core, pool)
                for t in range(C):
                    nc.gpsimd.indirect_dma_start(
                        out=xs_rows[:, k, t, :], out_offset=None, in_=d["xh"][:, :],
                        in_offset=bass.IndirectOffsetOnAxis(ap=xs_idx[:, k, t:t + 1], axis=0)).then_inc(xs_got[k], DMA)

            def gather_targets(c, i, k):
                pool.wait_ge(xdi_in[k], (i + 1) * DMA)
                since(pool, xd_kept[k], i * DMA)
                settle(core, pool)
                for t in range(C):
                    nc.gpsimd.indirect_dma_start(
                        out=xd_rows[:, k, t, :], out_offset=None, in_=io["x"][:, :],
                        in_offset=bass.IndirectOffsetOnAxis(ap=xd_idx[:, k, t:t + 1], axis=0)).then_inc(xd_got[k], DMA)

            def scatter(c, i, k):
                pool.wait_ge(endi_in, c + 1)
                pool.wait_ge(rows_in, 2 * c + 2)
                settle(core, pool)
                for t in range(C):
                    nc.gpsimd.indirect_dma_start(
                        out=d["a0"][:, :], out_offset=bass.IndirectOffsetOnAxis(ap=end_idx[:, k, t:t + 1], axis=0),
                        in_=rows[:, k, t, :], in_offset=None, bounds_check=NP - 1,
                        oob_is_err=False).then_inc(scattered[k], DMA)

            gather_sources(0, 0, 0)
            gather_sources(1, 0, 1)
            for at in steps(pool):
                gather_targets(*at(0))
                if at(-2):
                    scatter(*at(-2))
                if at(2):
                    gather_sources(*at(2))
            scatter(NCH - 2, LOOP - 1, 0)
            scatter(NCH - 1, LOOP - 1, 1)
            for k in range(2):
                pool.wait_ge(scattered[k], LOOP * C * DMA)

        @block.tensor
        def _(pe):
            def spread(c, i, k):
                pe.wait_ge(hs_in, c + 1)
                for u in range(2):
                    since(pe, hb_in, 2 * c + u - 1)
                    for t in range(C):
                        mm = nc.tensor.transpose(p_hb[u][:, t * P:(t + 1) * P], hs[:, k, t, u * P:(u + 1) * P],
                                                 m["ident"][:])
                    mm.then_inc(hb_out, 1)

            def project(c, i, k, u):
                pe.wait_ge(ef_in[k], (i + 1) * DMA)
                since(pe, x_done, 2 * c + u - 1)
                for q in range(2):
                    mm = nc.tensor.matmul(p_w[u][:, q, :], weights[:, (2 * q + u) * P:(2 * q + u + 1) * P], ef[:, k, :],
                                          start=True, stop=True)
                mm.then_inc(w_out, 1)

            def sum_inputs(c, i, k):
                since(pe, rows_in, 2 * c)
                pe.wait_ge(ratio_in, 2 * c + 2)
                for t in range(C):
                    for u in range(2):
                        mm = nc.tensor.matmul(p_out[:, t, :], ratio[:, u, t * P:(t + 1) * P], sel[:],
                                              start=(u == 0), stop=(u == 1))
                mm.then_inc(out_in, 1)

            pe.wait_ge(consts, 2 * DMA)
            spread(0, 0, 0)
            project(0, 0, 0, 0)
            project(0, 0, 0, 1)
            for at in steps(pe):
                if at(1):
                    project(*at(1), 0)
                    project(*at(1), 1)
                    spread(*at(1))
                if at(-1):
                    sum_inputs(*at(-1))
            sum_inputs(NCH - 1, LOOP - 1, 1)

        @block.scalar
        def _(act):
            def place_sources(c, i, k):
                act.wait_ge(xs_got[k], (i + 1) * (C * DMA))
                since(act, hb_out, 2 * c - 2)
                for t in range(C):
                    ins = nc.scalar.copy(hs[:, k, t].rearrange("p (w o) -> p w o", o=D), over(xs_rows[:, k, t, D:2 * D], D))
                ins.then_inc(hs_in, 1)

            def take_spread(c, i, k, u):
                act.wait_ge(hb_out, 2 * c + u + 1)
                since(act, x_done, 2 * c + u - 1)
                nc.scalar.copy(hb[:, u], p_hb[u][:]).then_inc(hb_in, 1)

            def exponentials(c, u):
                act.wait_ge(args_in, 2 * c + u + 1)
                nc.scalar.activation(ab[:, u], arg[:, u], ACT.Exp).then_inc(exp_done, 1)

            def inverse(c, k, u):
                act.wait_ge(den_in, 2 * c + u + 1)
                nc.scalar.activation(logd[:, u], den[:, u, k], ACT.Ln).then_inc(log_in, 1)
                act.wait_ge(log_in, 2 * c + u + 1)
                nc.scalar.activation(inv[:, u], logd[:, u], ACT.Exp, scale=-1.0).then_inc(inv_in, 1)

            def place_rows(c, i, k):
                since(act, scattered[k], i * (C * DMA))
                since(act, t_kept[k], i * DMA)
                nc.scalar.copy(end_idx[:, k], m["end_s"][:, cols(c * C, C)]).then_inc(endi_in, 1)
                nc.scalar.copy(rows[:, k, :, D:A0W], m["cntpos_s"][:, cols(c * C, C), :]).then_inc(rows_in, 1)
                act.wait_ge(out_in, c + 1)
                nc.scalar.copy(rows[:, k, :, 0:D], p_out[:]).then_inc(rows_in, 1)
                act.wait_ge(rows_in, 2 * c + 2)
                act.dma_start(t0[:, cols(c * C, C), :], rows[:, k, :, 0:D]).then_inc(t_kept[k], DMA)

            nc.scalar.add_instruction(mybir.InstLoadActFuncSet(name=nc.get_next_instruction_name(),
                                                               act_func_set_id=LN_EXP_SET))
            place_sources(0, 0, 0)
            take_spread(0, 0, 0, 0)
            take_spread(0, 0, 0, 1)
            for at in steps(act):
                c, i, k = at(0)
                if at(1):
                    place_sources(*at(1))
                exponentials(c, 0)
                exponentials(c, 1)
                if at(1):
                    take_spread(*at(1), 0)
                    take_spread(*at(1), 1)
                inverse(c, k, 0)
                inverse(c, k, 1)
                if at(-1):
                    place_rows(*at(-1))
            place_rows(NCH - 1, LOOP - 1, 1)
            for k in range(2):
                act.wait_ge(t_kept[k], LOOP * DMA)

        @block.vector
        def _(v):
            tt, scan = nc.vector.tensor_tensor, nc.vector.tensor_tensor_scan

            def ratios(c, i, k):
                since(v, out_in, c)
                for u in range(2):
                    v.wait_ge(inv_in, 2 * c + u + 1)
                    tt(ratio[:, u], num[:, u, k], inv[:, u], ALU.mult).then_inc(ratio_in, 1)

            nc.vector.memset(zeros[:], 0.0).then_inc(zeros_in, 1)
            for u in range(2):
                nc.vector.memset(top[:, u, 1, W:W + 1], 0.0).then_inc(state_in, 1)
                nc.vector.memset(den[:, u, 1, W - 1:W], 0.0).then_inc(state_in, 1)
                nc.vector.memset(num[:, u, 1, W - 1:W], 0.0).then_inc(state_in, 1)
            v.wait_ge(state_in, 6)
            st = Steps(v, own, STEPS_AT)
            for at in steps(v):
                c, i, k = at(0)
                if k == 0:
                    st.start_pass(i)
                was = [top[:, u, 1 - k, W:W + 1] for u in range(2)]
                now = [top[:, u, k] for u in range(2)]
                for u in range(2):
                    v.wait_ge(hb_in, 2 * c + u + 1)
                    v.wait_ge(w_out, 2 * c + u + 1)
                    tt(mxv[:, u, 1:3], p_w[u][:], hb[:, u:u + 1].to_broadcast([P, 2, W]), ALU.mult).then_inc(x_done, 1)
                    st.did(nc.vector.tensor_copy(now[u][:, 0:1], was[u]))
                v.wait_ge(pen_in[k], (i + 1) * DMA)
                for u in range(2):
                    v.wait_ge(x_done, 2 * c + u + 1)
                    st.did(scan(now[u][:, 1:W + 1], pen[:, k], mxv[:, u, 1], was[u], ALU.add, ALU.max))
                st.wait()
                st.did(tt(mxv[:, 0, 0], now[0][:, 0:W], pen[:, k], ALU.add))
                tt(mxv[:, 1, 0], now[1][:, 0:W], pen[:, k], ALU.add).then_inc(pen_read, 1)
                st.wait()
                tt(arg[:, 0], mxv[:, 0, 0:2], now[0][:, 1:W + 1].rearrange("p (o x) -> p o x", o=1).to_broadcast([P, 2, W]),
                   ALU.subtract).then_inc(args_in, 1)
                v.wait_ge(pen_read, c + 1)
                tt(arg[:, 1], mxv[:, 1, 0:2], now[1][:, 1:W + 1].rearrange("p (o x) -> p o x", o=1).to_broadcast([P, 2, W]),
                   ALU.subtract).then_inc(args_in, 1)
                if at(-1):
                    ratios(*at(-1))
                for u in range(2):
                    v.wait_ge(exp_done, 2 * c + u + 1)
                    tt(part[:, u], mxv[:, u, 2], ab[:, u, 1], ALU.mult).then_inc(part_in, 1)
                    scan(den[:, u, k], ab[:, u, 0], ab[:, u, 1], den[:, u, 1 - k, W - 1:W],
                         ALU.mult, ALU.add).then_inc(den_in, 1)
                    v.wait_ge(part_in, 2 * c + u + 1)
                    st.did(scan(num[:, u, k], ab[:, u, 0], part[:, u], num[:, u, 1 - k, W - 1:W], ALU.mult, ALU.add))
                st.wait()
                if k == 1:
                    st.end_pass()
            ratios(NCH - 1, LOOP - 1, 1)


def message_sum(core, io, d, m, lanes, base, qf, dinv, own_sum):
    nc, sem = core.nc, core.sem
    ctx, sb, ps = stage(core)
    GW = HG * P
    M = 3 * D + 1
    wgt, before, dump = sb("wgt", [P, ET]), sb("before", [P, HG, P], BF16), sb("dump", [P, HG])
    one_only = sb("one_only", [P, M], BF16)
    idx, a0r = sb("ms_idx", [P, 2, G], I32), sb("ms_a0", [P, 2, G, A0W])
    xs, xd, s_row = sb("ms_xs", [P, 2, G, D]), sb("ms_xd", [P, 2, G, D]), sb("ms_srow", [P, 2, G * P], I32)
    s_int, s_col = sb("ms_sint", [P, 2, G], I32), sb("ms_scol", [P, 2, G])
    xa, xb, ca, cb, sq = (sb(f"ms_{n}", [P, G, D]) for n in ("xa", "xb", "ca", "cb", "sq"))
    ha, hb, t1, t2, t3, msg = (sb(f"ms_{n}", [P, G, D]) for n in ("ha", "hb", "t1", "t2", "t3", "msg"))
    s = sb("ms_s", [P, G])
    var, root, rs = sb("ms_var", [P, 3, G]), sb("ms_root", [P, 3, G]), sb("ms_rs", [P, G])
    after, before_i = sb("ms_with_one", [P, 2, G, M], BF16), sb("ms_with_zero", [P, 2, G, M], BF16)
    same = sb("ms_same", [P, 2, HG * (GW + P)], BF16)
    same_before = sb("ms_same_before", [P, 2, HG, P], BF16)
    sums, total, to_idx = sb("ms_sums", [P, 2, HG, M]), sb("ms_total", [P, 2, HG, D]), sb("ms_to", [P, 2, HG], I32)
    u1, u2 = sb("ms_u1", [P, HG]), sb("ms_u2", [P, HG])
    p_sum, p_lane = [ps(f"p_ms{g}", [P, HG, M]) for g in range(2)], ps("p_lane_ms", [P, 512])
    two = lambda name: [sem(f"{name}{k}") for k in range(2)]
    consts, lanes_ready, lanes_turned, own_in = sem("ms_consts"), sem("ms_lanes_in"), sem("ms_lanes_turned"), sem("ms_own_in")
    idx_in, rows_in, got, added = two("ms_idx_in"), two("ms_rows_in"), two("ms_got"), sem("ms_added")
    used, var_in, root_in, own, once = sem("ms_used"), sem("ms_var_in"), sem("ms_root_in"), sem("ms_own"), sem("ms_once")
    same_in, summed, copied, total_in = sem("ms_same_in"), sem("ms_summed"), sem("ms_copied"), sem("ms_total_in")
    landed, a0_read = sem("ms_landed"), sem("ms_a0_read")
    LOOP = EC // 2
    blk = lambda name: d[name].rearrange("(p t) w -> p t w", p=P)
    loads = ((own_sum[:], blk("t0")), (wgt[:], io["wgt"]), (before[:], io["before"]), (dump[:], io["dump"]), (one_only[:], io["one_only"]))

    with ctx, nc.Block() as block:
        @block.sync
        def _(sp):
            for dst, src in loads:
                sp.dma_start(dst, src).then_inc(consts, DMA)
            for i, _ in passes(sp, LOOP):
                for k in range(2):
                    a = i * (2 * G) + k * G
                    sp.wait_ge(got[k], i * (G * DMA))
                    sp.dma_start(idx[:, k, :], io["src_b"][:, cols(a, G)]).then_inc(idx_in[k], DMA)
                    sp.wait_ge(used, 2 * i + k + 1)
                    sp.dma_start(xs[:, k], blk("xs")[:, cols(a, G), :]).then_inc(rows_in[k], DMA)
                    sp.dma_start(xd[:, k], blk("xd")[:, cols(a, G), :]).then_inc(rows_in[k], DMA)
                    sp.dma_start(s_int[:, k], io["src_b"][:, cols(a, G)]).then_inc(rows_in[k], DMA)
                    sp.dma_start(s_row[:, k], io["src_rows"][:, cols(i * (2 * G * P) + k * G * P, G * P)]
                                 .to_broadcast([P, G * P])).then_inc(rows_in[k], DMA)

        @block.gpsimd
        def _(pool):
            def gather(i, k, c, half):
                pool.wait_ge(idx_in[k], (i + 1) * DMA)
                pool.wait_ge(a0_read, c + 1)
                settle(core, pool)
                for t in range(half * HG, (half + 1) * HG):
                    nc.gpsimd.indirect_dma_start(
                        out=a0r[:, k, t, :], out_offset=None, in_=d["a0"][:, :],
                        in_offset=bass.IndirectOffsetOnAxis(ap=idx[:, k, t:t + 1], axis=0)).then_inc(got[k], DMA)

            for k in range(2):
                gather(0, k, k, 0)
                gather(0, k, k, 1)
            for i, last in passes(pool, LOOP, last_apart=True):
                for k in range(2):
                    for g in range(2):
                        n = 4 * i + 2 * k + g
                        pool.wait_ge(total_in, n + 1)
                        since(pool, added, n * (HG * DMA))
                        pool.sem_inc(landed, 1)
                        for t in range(HG):
                            nc.gpsimd.indirect_dma_start(
                                out=d["a1"][:, :], out_offset=bass.IndirectOffsetOnAxis(ap=to_idx[:, g, t:t + 1], axis=0),
                                in_=total[:, g, t, :], in_offset=None, compute_op=ALU.add).then_inc(added, DMA)
                        if not last:
                            gather(i + 1, k, 2 * i + 2 + k, g)
            pool.wait_ge(added, 2 * EC * HG * DMA)

        @block.scalar
        def _(act):
            for i, _ in passes(act, LOOP):
                for k in range(2):
                    for r in range(3):
                        act.wait_ge(var_in, 3 * (2 * i + k) + r + 1)
                        nc.scalar.activation(root[:, r], var[:, r], ACT.Sqrt).then_inc(root_in, 1)
                    for g in range(2):
                        n = 4 * i + 2 * k + g
                        act.wait_ge(summed, n + 1)
                        nc.scalar.copy(sums[:, g], p_sum[g][:]).then_inc(copied, 1)

        @block.tensor
        def _(pe):
            lanes.tensor(pe, D, False, p_lane, lanes_ready, lanes_turned)
            for i, _ in passes(pe, LOOP):
                for k in range(2):
                    for g in range(2):
                        n = 4 * i + 2 * k + g
                        pe.wait_ge(same_in, n + 1)
                        for t in range(HG):
                            o = p_sum[g][:, t, :]
                            nc.tensor.matmul(o, same_before[:, g, t, :], one_only[:], start=True, stop=False)
                            for j in range(HG):
                                parts = after if j < t else before_i
                                mm = nc.tensor.matmul(o, same[:, g, j * GW + t * P:j * GW + (t + 1) * P],
                                                      parts[:, k, g * HG + j, :], start=False, stop=(j == HG - 1))
                        mm.then_inc(summed, 1)

        @block.vector
        def _(v):
            tt, ts, stt = nc.vector.tensor_tensor, nc.vector.tensor_scalar, nc.vector.scalar_tensor_tensor
            first = Steps(v, once)
            v.sem_inc(used, 2)
            v.sem_inc(a0_read, 2)
            v.wait_ge(consts, len(loads) * DMA)
            first.did(nc.vector.memset(after[:], 1.0))
            first.did(nc.vector.memset(before_i[:], 0.0))
            first.did(tt(own_sum[:], own_sum[:], over(m["ends"][:], D), ALU.mult))
            first.wait()
            for w in range(D):
                first.did(nc.vector.tensor_tensor_scan(own_sum[:, ::-1, w], m["ends_not"][:, ::-1],
                                                       own_sum[:, ::-1, w], 0.0, ALU.mult, ALU.add))
            lanes.vector(first, own_sum, D, False, p_lane, lanes_ready, lanes_turned, own_in)
            v.wait_ge(own_in, D)
            st = Steps(v, own, STEPS_MS)
            for i, _ in passes(v, LOOP):
                st.start_pass(i)
                for k in range(2):
                    c, at = 2 * i + k, cols(i * (2 * G) + k * G, G)
                    v.wait_ge(got[k], (i + 1) * (G * DMA))
                    v.wait_ge(rows_in[k], (i + 1) * (4 * DMA))
                    st.did(nc.vector.tensor_copy(s_col[:, k], s_int[:, k]))
                    st.did(tt(xa[:], xs[:, k], a0r[:, k, :, 0:D], ALU.add))
                    st.did(tt(xb[:], xd[:, k], own_sum[:, at, :], ALU.add))
                    st.wait()
                    centre(nc, st, xa[:], ca[:], sq[:], s[:], var[:, 0], var_in)
                    v.wait_ge(var_in, 3 * c + 1)
                    centre(nc, st, xb[:], cb[:], sq[:], s[:], var[:, 1], var_in)
                    ts(var[:, 2], a0r[:, k, :, D], 1.0, None, ALU.add).then_inc(var_in, 1)
                    st.did(nc.vector.tensor_copy(qf[:, at], a0r[:, k, :, D + 1]))
                    v.wait_ge(root_in, 3 * c + 1)
                    scale_relu(nc, st, root[:, 0], rs[:], ca[:], ha[:])
                    v.wait_ge(var_in, 3 * c + 3)
                    st.wait()
                    v.sem_inc(a0_read, 1)
                    v.wait_ge(root_in, 3 * c + 2)
                    scale_relu(nc, st, root[:, 1], rs[:], cb[:], hb[:])
                    v.wait_ge(root_in, 3 * c + 3)
                    st.did(nc.vector.reciprocal(dinv[:, at], root[:, 2]))
                    st.did(ts(t1[:], ha[:], -0.2, 1.0, ALU.mult, ALU.add))
                    st.did(stt(t2[:], ha[:], -1.0, ha[:], ALU.add, ALU.mult))
                    st.wait()
                    st.did(tt(t3[:], t1[:], t2[:], ALU.mult))
                    st.wait()
                    st.did(stt(base[:, at, :], t3[:], 0.1, xa[:], ALU.add, ALU.add))
                    st.did(ts(t2[:], hb[:], 0.1, 5.0, ALU.mult, ALU.add))
                    st.did(tt(msg[:], ha[:], hb[:], ALU.mult))
                    st.wait()
                    st.did(stt(t1[:], ha[:], 0.9, t2[:], ALU.mult, ALU.add))
                    st.did(tt(t3[:], msg[:], over(wgt[:, at], D), ALU.mult))
                    st.wait()
                    st.did(nc.vector.reciprocal(t2[:], t1[:]))
                    st.wait()
                    st.did(tt(msg[:], t3[:], t2[:], ALU.mult))
                    st.wait()
                    v.wait_ge(summed, 4 * i + 2 * k)
                    hi, mid, lo = (after[:, k, :, 1 + D * q:1 + D * (q + 1)] for q in range(3))
                    st.did(nc.vector.tensor_copy(hi, msg[:]))
                    st.wait()
                    st.did(tt(t1[:], msg[:], hi, ALU.subtract))
                    st.wait()
                    st.did(nc.vector.tensor_copy(mid, t1[:]))
                    st.wait()
                    st.did(tt(t2[:], t1[:], mid, ALU.subtract))
                    st.wait()
                    st.did(nc.vector.tensor_copy(lo, t2[:]))
                    st.wait()
                    st.did(nc.vector.tensor_copy(before_i[:, k, :, 1:M], after[:, k, :, 1:M]))
                    for g in range(2):
                        n = 4 * i + 2 * k + g
                        for j in range(HG):
                            st.did(ts(same[:, g, j * GW:(j + 1) * GW], s_row[:, k, g * GW:(g + 1) * GW],
                                      s_col[:, k, g * HG + j:g * HG + j + 1], None, ALU.is_equal))
                        st.wait()
                        diagonal = same[:, g].rearrange("p (j x) -> p j x", x=GW + P)[:, :, 0:P]
                        tt(same_before[:, g], diagonal, before[:], ALU.mult).then_inc(same_in, 1)
                    for g in range(2):
                        n = 4 * i + 2 * k + g
                        v.wait_ge(copied, n + 1)
                        v.wait_ge(landed, n)
                        st.did(ts(u1[:], sums[:, g, :, 0], 0.0, None, ALU.is_equal))
                        st.did(tt(u2[:], s_col[:, k, g * HG:(g + 1) * HG], dump[:], ALU.subtract))
                        st.did(tt(total[:, g], sums[:, g, :, 1:1 + D], sums[:, g, :, 1 + D:1 + 2 * D], ALU.add))
                        st.wait()
                        st.did(tt(u2[:], u2[:], u1[:], ALU.mult))
                        st.did(tt(total[:, g], total[:, g], sums[:, g, :, 1 + 2 * D:M], ALU.add))
                        st.wait()
                        tt(to_idx[:, g], u2[:], dump[:], ALU.add).then_inc(total_in, 1)
                    v.wait_ge(total_in, 4 * i + 2 * k + 2)
                    v.sem_inc(used, 1)
                st.end_pass()


def edge_layer(core, io, d, m, lanes, base):
    nc, sem = core.nc, core.sem
    ctx, sb, ps = stage(core)
    WE = 2 * D * D
    msg = sb("el_msg", [P, ET, D])
    sums = sb("el_sums", [P, ET, D])
    idx, rows = sb("el_idx", [P, 2, G], I32), sb("el_rows", [P, 2, G, D])
    ea = sb("el_ea", [9, 2, G, P])
    edge_w, root_w = sb("el_edge_w", [9, D * D]), sb("el_root_w", [KB, TG * D])
    x2, xc, sq, h = sb("el_x2", [P, 2, G, D]), sb("el_xc", [P, G, D]), sb("el_sq", [P, G, D]), sb("el_h", [P, 2, G, D])
    s, var, root, rs = sb("el_s", [P, G]), sb("el_var", [P, 2, G]), sb("el_root", [P, 2, G]), sb("el_rs", [P, G])
    turned = sb("el_turned", [KB, 2, 2, P])
    prod = sb("el_prod", [P, 2, WE])
    p_turn, p_lin = ps("p_el_turn", [TG * D, 2, P]), ps("p_el_lin", [P, 2, TG * D])
    p_w = [ps(f"p_el_w{k}", [P, WE]) for k in range(3)]
    p_lane = ps("p_el_lane", [P, 512])
    two = lambda name: [sem(f"{name}{k}") for k in range(2)]
    consts, lanes_ready, lanes_turned, sums_in, stored = sem("el_consts"), sem("el_lanes_in"), sem("el_lanes_turned"), sem("el_sums_in"), sem("el_stored")
    idx_in, got, ea_in, used = two("el_idx_in"), two("el_got"), two("el_ea_in"), sem("el_used")
    var_in, root_in, own, h_in, turn_in, turned_in, lin_in = sem("el_var_in"), sem("el_root_in"), sem("el_own"), sem("el_h_in"), sem("el_turn_in"), sem("el_turned_in"), sem("el_lin_in")
    msg_own = sem("el_msg_own")
    w_in, w_used, ones_in, end_own = sem("el_w_in"), sem("el_w_used"), sem("el_ones_in"), sem("el_end_own")
    LOOP = EC // 2
    NW = G // 2

    with ctx, nc.Block() as block:
        @block.sync
        def _(sp):
            sp.dma_start(edge_w[:], io["edge_w"]).then_inc(consts, DMA)
            sp.dma_start(root_w[:], io["root_w"]).then_inc(consts, DMA)
            for i, _ in passes(sp, LOOP):
                for k in range(2):
                    a = i * (2 * G) + k * G
                    sp.wait_ge(got[k], i * (G * DMA))
                    sp.dma_start(idx[:, k, :], io["src_b"][:, cols(a, G)]).then_inc(idx_in[k], DMA)
                    sp.wait_ge(w_in, (2 * i + k) * NW)
                    sp.dma_start(ea[:, k], io["ea_t"][:, cols(a, G), :]).then_inc(ea_in[k], DMA)
            sp.wait_ge(sums_in, D)
            sp.dma_start(d["t2"][1:EP + 1, :].rearrange("(p t) w -> p t w", p=P), sums[:]).then_inc(stored, DMA)
            sp.wait_ge(stored, DMA)

        @block.gpsimd
        def _(pool):
            for i, _ in passes(pool, LOOP):
                for k in range(2):
                    pool.wait_ge(idx_in[k], (i + 1) * DMA)
                    pool.wait_ge(used, 2 * i + k + 1)
                    settle(core, pool)
                    for t in range(G):
                        nc.gpsimd.indirect_dma_start(
                            out=rows[:, k, t, :], out_offset=None, in_=d["a1"][:, :],
                            in_offset=bass.IndirectOffsetOnAxis(ap=idx[:, k, t:t + 1], axis=0)).then_inc(got[k], DMA)

        @block.scalar
        def _(act):
            act.wait_ge(ones_in, 1)
            for i, _ in passes(act, LOOP):
                for k in range(2):
                    c = 2 * i + k
                    act.wait_ge(var_in, c + 1)
                    nc.scalar.activation(root[:, k], var[:, k], ACT.Sqrt).then_inc(root_in, 1)
                    act.wait_ge(turn_in, c + 1)
                    nc.scalar.copy(turned[0:TG * D, k], p_turn[:]).then_inc(turned_in, 1)

        @block.tensor
        def _(pe):
            pe.wait_ge(consts, 2 * DMA)
            pe.sem_inc(w_in, NW)
            for i, _ in passes(pe, LOOP):
                for k in range(2):
                    c = 2 * i + k
                    pe.wait_ge(h_in, c + 1)
                    for q in range(2):
                        mm = nc.tensor.transpose(p_turn[:, q, :], h[:, k, q * TG:(q + 1) * TG, :].rearrange("p t w -> p (t w)"), m["ident"][:])
                    mm.then_inc(turn_in, 1)
                    pe.wait_ge(ea_in[k], (i + 1) * DMA)
                    for q in range(NW):
                        n = c * NW + q
                        pe.wait_ge(w_used, n + (2 if k == 0 and q < 2 else 1))
                        for j in range(2):
                            mm = nc.tensor.matmul(p_w[(k * NW + q) % 3][:, j * D * D:(j + 1) * D * D], ea[:, k, 2 * q + j, :], edge_w[:],
                                                  start=True, stop=True)
                        mm.then_inc(w_in, 1)
                    pe.wait_ge(turned_in, c + 1)
                    for q in range(2):
                        mm = nc.tensor.matmul(p_lin[:, q, :], turned[:, k, q, :], root_w[:], start=True, stop=True)
                    mm.then_inc(lin_in, 1)
            lanes.tensor(pe, D, True, p_lane, lanes_ready, lanes_turned)

        @block.vector
        def _(v):
            tt, stt = nc.vector.tensor_tensor, nc.vector.scalar_tensor_tensor
            nc.vector.memset(turned[:], 1.0).then_inc(ones_in, 1)
            v.sem_inc(used, 2)
            v.sem_inc(w_used, 3)
            ahead, st = Steps(v, own, 5), Steps(v, msg_own, NW + 1)

            def prepare(i, k, c):
                ahead.start_pass(c)
                v.wait_ge(got[k], (i + 1) * (G * DMA))
                tt(x2[:, k], base[:, cols(i * (2 * G) + k * G, G), :], rows[:, k], ALU.add).then_inc(used, 1)
                v.wait_ge(used, c + 3)
                centre(nc, ahead, x2[:, k], xc[:], sq[:], s[:], var[:, k], var_in)
                v.wait_ge(root_in, c + 1)
                ahead.did(nc.vector.reciprocal(rs[:], root[:, k]))
                ahead.wait()
                stt(h[:, k], xc[:], 0.0, over(rs[:], D), ALU.max, ALU.mult).then_inc(h_in, 1)
                v.wait_ge(h_in, c + 1)
                ahead.end_pass()

            def messages(i, k, c):
                st.start_pass(c)
                for q in range(NW):
                    n = c * NW + q
                    at = cols(i * (2 * G) + k * G + 2 * q, 2)
                    four = lambda ap: ap.rearrange("p (t o w) -> p t o w", t=2, o=D)
                    v.wait_ge(w_in, n + 1 + NW)
                    hh = h[:, k, 2 * q:2 * q + 2, :].rearrange("p t (o w) -> p t o w", o=1).to_broadcast([P, 2, D, D])
                    tt(four(prod[:, q % 2]), four(p_w[(k * NW + q) % 3][:]), hh, ALU.mult).then_inc(w_used, 1)
                    v.wait_ge(w_used, n + 4)
                    st.did(nc.vector.tensor_reduce(msg[:, at, :], four(prod[:, q % 2]), AX.X, ALU.add))
                v.wait_ge(lin_in, c + 1)
                st.did(tt(base[:, cols(i * (2 * G) + k * G, G), :], x2[:, k],
                          p_lin[:].rearrange("p q (t w) -> p (q t) w", w=D), ALU.add))
                st.wait()
                st.end_pass()

            prepare(0, 0, 0)
            for i, final in passes(v, LOOP, last_apart=True):
                prepare(i, 1, 2 * i + 1)
                messages(i, 0, 2 * i)
                if not final:
                    prepare(i + 1, 0, 2 * i + 2)
                messages(i, 1, 2 * i + 1)
            last = Steps(v, end_own)
            for w in range(D):
                last.did(nc.vector.tensor_tensor_scan(sums[:, :, w], m["starts_not"][:], msg[:, :, w], 0.0, ALU.mult, ALU.add))
            lanes.vector(last, sums, D, True, p_lane, lanes_ready, lanes_turned, sums_in)


def gcn_first(core, io, d, m, lanes, base, qf, dinv, y0):
    nc, sem = core.nc, core.sem
    ctx, sb, ps = stage(core)
    sums = sb("gf_sums", [P, ET, D])
    idx, rows = sb("gf_idx", [P, 2, G], I32), sb("gf_rows", [P, 2, G, D])
    x3, xc, sq, h = (sb(f"gf_{n}", [P, G, D]) for n in ("x3", "xc", "sq", "h"))
    s, var, root, rs = sb("gf_s", [P, G]), sb("gf_var", [P, 2, G]), sb("gf_root", [P, 2, G]), sb("gf_rs", [P, G])
    p_lane = ps("p_gf_lane", [P, 512])
    two = lambda name: [sem(f"{name}{k}") for k in range(2)]
    lanes_ready, lanes_turned, sums_in, stored = sem("gf_lanes_in"), sem("gf_lanes_turned"), sem("gf_sums_in"), sem("gf_stored")
    idx_in, got, used = sem("gf_idx_in"), two("gf_got"), sem("gf_used")
    var_in, root_in, own, end_own = sem("gf_var_in"), sem("gf_root_in"), sem("gf_own"), sem("gf_end_own")
    LOOP = EC // 2
    with ctx, nc.Block() as block:
        @block.sync
        def _(sp):
            sp.wait_ge(sums_in, D)
            sp.dma_start(d["t3a"][1:EP + 1, :].rearrange("(p t) w -> p t w", p=P), sums[:]).then_inc(stored, DMA)
            sp.wait_ge(stored, DMA)

        @block.gpsimd
        def _(pool):
            gather_rows(core, pool, d["t2"], idx, rows, idx_in, used, got)

        @block.scalar
        def _(act):
            for k in range(2):
                place_indices(nc, act, 0, k, qf, idx, idx_in, got)
            for i, last in passes(act, LOOP, last_apart=True):
                for k in range(2):
                    act.wait_ge(var_in, 2 * i + k + 1)
                    nc.scalar.activation(root[:, k], var[:, k], ACT.Sqrt).then_inc(root_in, 1)
                    if not last:
                        place_indices(nc, act, i + 1, k, qf, idx, idx_in, got)

        @block.tensor
        def _(pe):
            lanes.tensor(pe, D, True, p_lane, lanes_ready, lanes_turned)

        @block.vector
        def _(v):
            tt = nc.vector.tensor_tensor
            v.sem_inc(used, 2)
            st = Steps(v, own, STEPS_GF)
            for i, _ in passes(v, LOOP):
                st.start_pass(i)
                for k in range(2):
                    c, at = 2 * i + k, cols(i * (2 * G) + k * G, G)
                    v.wait_ge(got[k], (i + 1) * (G * DMA))
                    tt(x3[:], base[:, at, :], rows[:, k], ALU.add).then_inc(used, 1)
                    v.wait_ge(used, c + 3)
                    centre(nc, st, x3[:], xc[:], sq[:], s[:], var[:, k], var_in)
                    v.wait_ge(root_in, c + 1)
                    scale_relu(nc, st, root[:, k], rs[:], xc[:], h[:])
                    st.wait()
                    st.did(tt(y0[:, at, :], h[:], over(dinv[:, at], D), ALU.mult))
                    st.wait()
                st.end_pass()
            last = Steps(v, end_own)
            for w in range(D):
                last.did(nc.vector.tensor_tensor_scan(sums[:, :, w], m["starts_not"][:], y0[:, :, w], 0.0, ALU.mult, ALU.add))
            lanes.vector(last, sums, D, True, p_lane, lanes_ready, lanes_turned, sums_in)


def gather_rows(core, pool, table, idx, rows, idx_in, used, got):
    nc = core.nc
    for i, _ in passes(pool, EC // 2):
        for k in range(2):
            pool.wait_ge(idx_in, 2 * i + k + 1)
            pool.wait_ge(used, 2 * i + k + 1)
            settle(core, pool)
            for t in range(G):
                nc.gpsimd.indirect_dma_start(
                    out=rows[:, k, t, :], out_offset=None, in_=table[:, :],
                    in_offset=bass.IndirectOffsetOnAxis(ap=idx[:, k, t:t + 1], axis=0)).then_inc(got[k], DMA)


def place_indices(nc, act, i, k, qf, idx, idx_in, got):
    since(act, got[k], i * (G * DMA))
    nc.scalar.copy(idx[:, k, :], qf[:, cols(i * (2 * G) + k * G, G)]).then_inc(idx_in, 1)


def turn_groups(W):
    n = P // W if P // W < TG else TG
    return [(a, min(n, G - a)) for a in range(0, G, n)]


def gcn_next(core, io, d, m, lanes, W, weights, bias, table, sums_d, y, y_out, sums, qf, dinv):
    nc, sem = core.nc, core.sem
    ctx, sb, ps = stage(core)
    n_ = f"g{W}_"
    groups = turn_groups(W)
    n0 = groups[0][1]
    W2 = 2 * W
    idx, rows = sb(n_ + "idx", [P, 2, G], I32), sb(n_ + "rows", [P, 2, G, W])
    a, agg = sb(n_ + "a", [P, G, W]), sb(n_ + "agg", [P, 2, G, W])
    wt, bs, ones = sb(n_ + "w", [n0 * W, n0 * W2]), sb(n_ + "b", [1, n0 * W2]), sb(n_ + "ones", [1, P])
    turned = sb(n_ + "turned", [n0 * W, 2, len(groups), P])
    p_turn = ps(n_ + "p_turn", [n0 * W, len(groups), P])
    p_out = [ps(n_ + f"p_out{q}", [P, n0 * W2]) for q in range(len(groups))]
    p_lane = ps(n_ + "p_lane", [P, 512])
    two = lambda name: [sem(n_ + f"{name}{k}") for k in range(2)]
    consts, lanes_ready, lanes_turned, sums_in, stored = sem(n_ + "consts"), sem(n_ + "lanes_in"), sem(n_ + "lanes_turned"), sem(n_ + "sums_in"), sem(n_ + "stored")
    idx_in, got, used, own, end_own, ones_in = sem(n_ + "idx_in"), two("got"), sem(n_ + "used"), sem(n_ + "own"), sem(n_ + "end_own"), sem(n_ + "ones_in")
    agg_in, turn_in, turned_in, out_in, out_read = sem(n_ + "agg_in"), sem(n_ + "turn_in"), sem(n_ + "turned_in"), sem(n_ + "out_in"), sem(n_ + "out_read")
    LOOP = EC // 2
    NG = len(groups)
    with ctx, nc.Block() as block:
        @block.sync
        def _(sp):
            sp.dma_start(wt[:], weights).then_inc(consts, DMA)
            sp.dma_start(bs[:], bias).then_inc(consts, DMA)
            sp.wait_ge(sums_in, W2)
            sp.dma_start(sums_d[1:EP + 1, :].rearrange("(p t) w -> p t w", p=P), sums[:]).then_inc(stored, DMA)
            sp.wait_ge(stored, DMA)

        @block.gpsimd
        def _(pool):
            gather_rows(core, pool, table, idx, rows, idx_in, used, got)

        @block.scalar
        def _(act):
            for k in range(2):
                place_indices(nc, act, 0, k, qf, idx, idx_in, got)
            for i, last in passes(act, LOOP, last_apart=True):
                for k in range(2):
                    act.wait_ge(turn_in, 2 * i + k + 1)
                    n_last = groups[-1][1]
                    if n_last == n0:
                        nc.scalar.copy(turned[:, k], p_turn[:]).then_inc(turned_in, 1)
                    else:
                        nc.scalar.copy(turned[:, k, 0:NG - 1], p_turn[:, 0:NG - 1, :])
                        nc.scalar.copy(turned[0:n_last * W, k, NG - 1], p_turn[0:n_last * W, NG - 1, :]).then_inc(turned_in, 1)
                    if not last:
                        place_indices(nc, act, i + 1, k, qf, idx, idx_in, got)

        @block.tensor
        def _(pe):
            pe.wait_ge(consts, 2 * DMA)
            pe.wait_ge(ones_in, 1)
            for i, _ in passes(pe, LOOP):
                for k in range(2):
                    c = 2 * i + k
                    pe.wait_ge(agg_in, c + 1)
                    for q, (t, n) in enumerate(groups):
                        mm = nc.tensor.transpose(p_turn[0:n * W, q, :], agg[:, k, t:t + n, :].rearrange("p t w -> p (t w)"), m["ident"][:])
                    mm.then_inc(turn_in, 1)
                    pe.wait_ge(out_read, c * NG)
                    pe.wait_ge(turned_in, c + 1)
                    for q, (t, n) in enumerate(groups):
                        nc.tensor.matmul(p_out[q][:, 0:n * W2], ones[:], bs[:, 0:n * W2], start=True, stop=False)
                        mm = nc.tensor.matmul(p_out[q][:, 0:n * W2], turned[0:n * W, k, q, :], wt[0:n * W, 0:n * W2],
                                              start=False, stop=True)
                    mm.then_inc(out_in, 1)
            lanes.tensor(pe, W2, True, p_lane, lanes_ready, lanes_turned)

        @block.vector
        def _(v):
            tt, stt = nc.vector.tensor_tensor, nc.vector.scalar_tensor_tensor
            nc.vector.memset(ones[:], 1.0).then_inc(ones_in, 1)
            v.sem_inc(used, 2)
            apart = sums is not y_out
            st = Steps(v, own, W2 + apart)

            def aggregate(i, k, c):
                at = cols(i * (2 * G) + k * G, G)
                v.wait_ge(got[k], (i + 1) * (G * DMA))
                since(v, agg_in, c)
                tt(a[:], rows[:, k], y[:, at, :], ALU.add).then_inc(used, 1)
                v.wait_ge(used, c + 3)
                tt(agg[:, k], a[:], over(dinv[:, at], W), ALU.mult).then_inc(agg_in, 1)

            def finish(i, k, c):
                v.wait_ge(out_in, c + 1)
                for q, (t, n) in enumerate(groups):
                    at = cols(i * (2 * G) + k * G + t, n)
                    stt(y_out[:, at, :], p_out[q][:, 0:n * W2].rearrange("p (t w) -> p t w", w=W2), 0.0,
                        over(dinv[:, at], W2), ALU.max, ALU.mult).then_inc(out_read, 1)
                v.wait_ge(out_read, (c + 1) * NG)
                st.start_pass(c)
                if apart:
                    at = cols(c * G, G)
                    st.did(nc.vector.tensor_copy(sums[:, at, :], y_out[:, at, :]))
                    st.wait()
                run_on(nc, st, sums, m["starts_not"], c, W2)
                st.wait()
                st.end_pass()

            aggregate(0, 0, 0)
            for i, last in passes(v, LOOP, last_apart=True):
                aggregate(i, 1, 2 * i + 1)
                finish(i, 0, 2 * i)
                if not last:
                    aggregate(i + 1, 0, 2 * i + 2)
                finish(i, 1, 2 * i + 1)
            last = Steps(v, end_own)
            lanes.vector(last, sums, W2, True, p_lane, lanes_ready, lanes_turned, sums_in)


def node_base(core, io, d, m, nbase, ndinv):
    nc, sem = core.nc, core.sem
    ctx, sb, ps = stage(core)
    GN = NT // EC
    NQ = GN // TG
    x, a0, a1 = sb("nb_x", [P, 2, GN, D]), sb("nb_a0", [P, 2, GN, A0W]), sb("nb_a1", [P, 2, GN, D])
    x1, xc, sq, h, t1, t2, t3 = (sb(f"nb_{n}", [P, GN, D]) for n in ("x1", "xc", "sq", "h", "t1", "t2", "t3"))
    x2, h2 = sb("nb_x2", [P, 2, GN, D]), sb("nb_h2", [P, 2, GN, D])
    s, rs = sb("nb_s", [P, GN]), sb("nb_rs", [P, GN])
    var, root = sb("nb_var", [P, 3, GN]), sb("nb_root", [P, 3, GN])
    root_w, turned = sb("nb_root_w", [KB, TG * D]), sb("nb_turned", [KB, 2, NQ, P])
    p_turn = [ps(f"nb_p_turn{k}", [TG * D, NQ, P]) for k in range(2)]
    p_lin = [ps(f"nb_p_lin{k}", [P, NQ, TG * D]) for k in range(2)]
    two = lambda name: [sem(f"{name}{k}") for k in range(2)]
    consts, rows_in, used, var_in, root_in, own = sem("nb_consts"), two("nb_rows_in"), sem("nb_used"), sem("nb_var_in"), sem("nb_root_in"), sem("nb_own")
    h_in, turn_in, turned_in, lin_in, ones_in = sem("nb_h_in"), sem("nb_turn_in"), sem("nb_turned_in"), sem("nb_lin_in"), sem("nb_ones_in")
    base_in = sem("nb_base_in")
    rows, idx = sb("fs_rows", [P, 2, G, FW]), sb("fs_idx", [P, 2, G], I32)
    row_in, idx_in, sent = two("fs_rows_in"), sem("fs_idx_in"), two("fs_sent")
    LOOP = EC // 2
    parts, start = [], 0
    for name in ("t2", "t3a", "t3b", "t3c"):
        w = d[name].shape[1]
        parts.append((d[name][1:EP + 1, :].rearrange("(p t) w -> p t w", p=P), start, w))
        start += w
    blk = lambda ap: ap[0:NP, :].rearrange("(p t) w -> p t w", p=P)
    with ctx, nc.Block() as block:
        @block.sync
        def _(sp):
            sp.dma_start(root_w[:], io["root_w"]).then_inc(consts, DMA)
            for i, _ in passes(sp, LOOP):
                for k in range(2):
                    at = cols(i * (2 * GN) + k * GN, GN)
                    since(sp, sent[k], i * (G * DMA))
                    for src, a, w in parts:
                        sp.dma_start(rows[:, k, :, a:a + w], src[:, cols(i * (2 * G) + k * G, G), :]).then_inc(row_in[k], DMA)
                    sp.wait_ge(used, 2 * i + k + 1)
                    for dst, src in ((x, io["x"]), (a0, d["a0"]), (a1, d["a1"])):
                        sp.dma_start(dst[:, k], blk(src)[:, at, :]).then_inc(rows_in[k], DMA)

        @block.gpsimd
        def _(pool):
            for i, _ in passes(pool, LOOP):
                for k in range(2):
                    pool.wait_ge(idx_in, 2 * i + k + 1)
                    pool.wait_ge(row_in[k], (i + 1) * (4 * DMA))
                    settle(core, pool)
                    for t in range(G):
                        nc.gpsimd.indirect_dma_start(
                            out=d["f"][:, :], out_offset=bass.IndirectOffsetOnAxis(ap=idx[:, k, t:t + 1], axis=0),
                            in_=rows[:, k, t, :], in_offset=None, bounds_check=NP - 1, oob_is_err=False).then_inc(sent[k], DMA)
            for k in range(2):
                pool.wait_ge(sent[k], LOOP * G * DMA)

        @block.scalar
        def _(act):
            def place_ends(i, k):
                since(act, sent[k], i * (G * DMA))
                nc.scalar.copy(idx[:, k, :], m["end_b"][:, cols(i * (2 * G) + k * G, G)]).then_inc(idx_in, 1)

            for k in range(2):
                place_ends(0, k)
            act.wait_ge(ones_in, 1)
            for i, last in passes(act, LOOP, last_apart=True):
                for k in range(2):
                    c = 2 * i + k
                    for r in range(3):
                        act.wait_ge(var_in, 3 * c + r + 1)
                        nc.scalar.activation(root[:, r], var[:, r], ACT.Sqrt).then_inc(root_in, 1)
                    act.wait_ge(turn_in, c + 1)
                    nc.scalar.copy(turned[0:TG * D, k], p_turn[k][:]).then_inc(turned_in, 1)
                    if not last:
                        place_ends(i + 1, k)

        @block.tensor
        def _(pe):
            pe.wait_ge(consts, DMA)
            for i, _ in passes(pe, LOOP):
                for k in range(2):
                    c = 2 * i + k
                    pe.wait_ge(h_in, c + 1)
                    for q in range(NQ):
                        mm = nc.tensor.transpose(p_turn[k][:, q, :], h2[:, k, q * TG:(q + 1) * TG, :].rearrange("p t w -> p (t w)"), m["ident"][:])
                    mm.then_inc(turn_in, 1)
                    pe.wait_ge(turned_in, c + 1)
                    for q in range(NQ):
                        mm = nc.tensor.matmul(p_lin[k][:, q, :], turned[:, k, q, :], root_w[:], start=True, stop=True)
                    mm.then_inc(lin_in, 1)

        @block.vector
        def _(v):
            tt, ts, stt = nc.vector.tensor_tensor, nc.vector.tensor_scalar, nc.vector.scalar_tensor_tensor
            nc.vector.memset(turned[:], 1.0).then_inc(ones_in, 1)
            v.sem_inc(used, 2)
            st = Steps(v, own, STEPS_NB)

            def finish(i, k, c):
                v.wait_ge(lin_in, c + 1)
                tt(nbase[:, cols(c * GN, GN), :], x2[:, k], p_lin[k][:].rearrange("p q (t w) -> p (q t) w", w=D),
                   ALU.add).then_inc(base_in, 1)

            for i, _ in passes(v, LOOP):
                st.start_pass(i)
                for k in range(2):
                    c, at = 2 * i + k, cols(i * (2 * GN) + k * GN, GN)
                    v.wait_ge(rows_in[k], (i + 1) * (3 * DMA))
                    st.did(tt(x1[:], x[:, k], a0[:, k, :, 0:D], ALU.add))
                    ts(var[:, 0], a0[:, k, :, D], 1.0, None, ALU.add).then_inc(var_in, 1)
                    st.wait()
                    centre(nc, st, x1[:], xc[:], sq[:], s[:], var[:, 1], var_in)
                    if k or not isinstance(i, int):
                        finish(i if k else i - 1, 1 - k, c - 1)
                    v.wait_ge(root_in, 3 * c + 1)
                    st.did(nc.vector.reciprocal(ndinv[:, at], root[:, 0]))
                    v.wait_ge(root_in, 3 * c + 2)
                    scale_relu(nc, st, root[:, 1], rs[:], xc[:], h[:])
                    st.wait()
                    st.did(ts(t1[:], h[:], -0.2, 1.0, ALU.mult, ALU.add))
                    st.did(stt(t2[:], h[:], -1.0, h[:], ALU.add, ALU.mult))
                    since(v, base_in, c)
                    st.did(stt(x2[:, k], x1[:], 0.1, a1[:, k], ALU.add, ALU.add))
                    st.wait()
                    st.did(tt(t3[:], t1[:], t2[:], ALU.mult))
                    st.wait()
                    tt(x2[:, k], x2[:, k], t3[:], ALU.add).then_inc(used, 1)
                    v.wait_ge(used, c + 3)
                    centre(nc, st, x2[:, k], xc[:], sq[:], s[:], var[:, 2], var_in)
                    v.wait_ge(root_in, 3 * c + 3)
                    st.did(nc.vector.reciprocal(rs[:], root[:, 2]))
                    st.wait()
                    stt(h2[:, k], xc[:], 0.0, over(rs[:], D), ALU.max, ALU.mult).then_inc(h_in, 1)
                    v.wait_ge(h_in, c + 1)
                st.end_pass()
            finish(LOOP - 1, 1, EC - 1)


class Turn:

    def __init__(self, i, kk, whole):
        self.i, self.kk, self.whole = i, kk, whole

    def chunk(self, lag, n):
        o = self.kk - lag
        if not self.whole and not 0 <= 4 * self.i + o < n:
            return None
        return 4 * self.i + o, self.i + o // 4, o % 4, 2 * self.i + o // 2, o % 2


def pipeline(eng, n, lags, steps=None):
    total, first = n + lags, -(-lags // 4) + 1
    begun = 0
    for i in range(first):
        for kk in range(4):
            yield Turn(i, kk, False)
    if steps:
        begun = steps.k
    with eng.Fori(first, n // 4) as i:
        if steps:
            steps.base, steps.k = begun + (i - first) * steps.per_pass, 0
        for kk in range(4):
            yield Turn(i, kk, True)
        if steps:
            steps.end_pass()
    if steps:
        steps.base, steps.k = begun + (n // 4 - first) * steps.per_pass, 0
    for j in range(n, total):
        yield Turn(n // 4, j - n, False)


def node_gcn(core, io, d, m, nbase, ndinv, out):
    nc, sem = core.nc, core.sem
    ctx, sb, ps = stage(core)
    NC = NT // G
    D2, D4, D8 = 2 * D, 4 * D, 8 * D
    HALF = G * P // 4
    LB, LC, LT, LM, LO, LS = 1, 2, 2, 3, 4, 6
    n1 = (P - 1) // D2
    groups1 = [(t, min(n1, G - t)) for t in range(0, G, n1)]
    K2 = n1 * D2 + 1
    f = sb("ng_f", [P, 4, G, FW])
    xc, sq, h, y0, a0 = (sb(f"ng_{n}", [P, G, D]) for n in ("xc", "sq", "h", "y0", "a0"))
    s, var, root, rs = sb("ng_s", [P, G]), sb("ng_var", [P, G]), sb("ng_root", [P, G]), sb("ng_rs", [P, G])
    agg0, y1, a1, agg1 = sb("ng_agg0", [P, G, D]), sb("ng_y1", [P, G, D2]), sb("ng_a1", [P, G, D2]), sb("ng_agg1", [P, G, D2])
    y2, a2, agg2 = sb("ng_y2", [P, G, D4]), sb("ng_a2", [P, G, D4]), sb("ng_agg2", [P, G, D4])
    tu0, tu1, tu2 = sb("ng_tu0", [KB, 2, P]), sb("ng_tu1", [K2, len(groups1), P]), sb("ng_tu2", [P, 2, HG * P])
    h3, h4, h5 = sb("ng_h3", [P, 2, 2, HALF]), sb("ng_h4", [P, 2, HALF]), sb("ng_h5", [D4 + 1, 2 * HALF])
    res = sb("ng_res", [P, 2, G, D])
    w1, w2 = sb("ng_w1", [KB, TG * D2]), sb("ng_w2", [K2, n1 * D4])
    w3, b3 = sb("ng_w3", [P, D8]), sb("ng_b3", [P, 1])
    wl1, bl1, wl2, bl2, wl3 = sb("ng_wl1", [P, D4]), sb("ng_bl1", [P, 1]), sb("ng_wl2", [P, D4]), sb("ng_bl2", [D4, 1]), sb("ng_wl3", [D4 + 1, D2])
    p_ao = ps("ng_p_ao", [P, 512])
    p_t0, p_o = p_ao[0:TG * D, 0:2 * P].rearrange("p (q x) -> p q x", q=2), p_ao[:, 2 * P:2 * P + G * D]
    p_l1, p_t = ps("ng_p_l1", [P, 512]), ps("ng_p_t", [P, 4, P])
    p_l2 = [ps(f"ng_p_l2{q}", [P, 512]) for q in range(2)]
    l2_at = lambda q, n: p_l2[q // 2 if q < 4 else 0][:, (q % 2 if q < 4 else 2) * n1 * D4:][:, 0:n * D4]
    t1_last = p_l2[1][0:groups1[-1][1] * D2, 2 * n1 * D4:2 * n1 * D4 + P]
    p_c, p_d, p_e = ps("ng_p_c", [P, 512]), ps("ng_p_d", [P, 512]), ps("ng_p_e", [D4, 512])
    consts, f_in, res_out, used = sem("ng_consts"), [sem(f"ng_f_in{k}") for k in range(4)], [sem(f"ng_res_out{k}") for k in range(2)], sem("ng_used")
    var_in, root_in, own, ready = sem("ng_var_in"), sem("ng_root_in"), sem("ng_own"), sem("ng_ready")
    agg0_in, agg1_in, agg2_in, res_in, l1_read, l2_read = (sem(f"ng_{n}") for n in ("agg0_in", "agg1_in", "agg2_in", "res_in", "l1_read", "l2_read"))
    t0_in, t1_in, t2_in, l1_in, l2_in, c_in, d_in, e_in, o_in = (sem(f"ng_{n}") for n in ("t0_in", "t1_in", "t2_in", "l1_in", "l2_in", "c_in", "d_in", "e_in", "o_in"))
    tu0_in, tu1_in, tu2_in, h3_in, h4_in, h5_in = (sem(f"ng_{n}") for n in ("tu0_in", "tu1_in", "tu2_in", "h3_in", "h4_in", "h5_in"))
    loads = [(w1, "w1b"), (w2, "w2b"), (w3, "w3"), (b3, "b3"), (wl1, "wl1"), (bl1, "bl1"), (wl2, "wl2"), (bl2, "bl2"), (wl3, "wl3")]
    f_rows, out_rows = d["f"].rearrange("(p t) w -> p t w", p=P), out.rearrange("(p t) w -> p t w", p=P)
    tiles = lambda c: cols(c * G, G)

    with ctx, nc.Block() as block:
        @block.sync
        def _(sp):
            for dst, name in loads:
                sp.dma_start(dst[:], io[name]).then_inc(consts, DMA)
            for turn in pipeline(sp, NC, LS):
                if ch := turn.chunk(0, NC):
                    c, m4, k4, m2, k2 = ch
                    sp.wait_ge(used, c + 1)
                    sp.dma_start(f[:, k4], f_rows[:, tiles(c), :]).then_inc(f_in[k4], DMA)
                if ch := turn.chunk(LS, NC):
                    c, m4, k4, m2, k2 = ch
                    sp.wait_ge(res_in, c + 1)
                    sp.dma_start(out_rows[:, tiles(c), :], res[:, k2]).then_inc(res_out[k2], DMA)
            for k in range(2):
                sp.wait_ge(res_out[k], NC // 2 * DMA)

        @block.tensor
        def _(pe):
            mmul = nc.tensor.matmul
            pe.wait_ge(consts, len(loads) * DMA)
            pe.wait_ge(ready, 3)

            def first(g, par, half):
                c, m4, k4, m2, k2 = g
                n = 4 * c + 2 * half + par
                pe.wait_ge(h3_in, n)
                if par == 0 and half == 0:
                    pe.wait_ge(tu2_in, 2 * c + 2)
                r = slice(par * D4, (par + 1) * D4)
                mmul(p_c[:, 0:HALF], w3[r, :], tu2[r, k2, half * HALF:(half + 1) * HALF], start=True, stop=True).then_inc(c_in, 1)

            def second(g, par, half):
                c = g[0]
                if par == 0:
                    pe.wait_ge(h4_in, 2 * c + half)
                pe.wait_ge(h3_in, 4 * c + 2 * half + par + 1)
                mm = mmul(p_d[par * D4:(par + 1) * D4, 0:HALF], wl1[:], h3[:, par, half], start=True, stop=True)
                if par == 1:
                    mm.then_inc(d_in, 1)

            def third(g, half):
                c = g[0]
                pe.wait_ge(h4_in, 2 * c + half + 1)
                pe.wait_ge(h5_in, 2 * c + half)
                mmul(p_e[:, 0:HALF], wl2[:], h4[:, half], start=True, stop=True).then_inc(e_in, 1)

            def turn2(g, q):
                c = g[0]
                if q == 0:
                    pe.wait_ge(agg2_in, c + 1)
                    pe.wait_ge(tu1_in, c + 1)
                else:
                    pe.wait_ge(tu2_in, 2 * c + 1)
                for j in range(4 if q == 0 else 3):
                    t = 2 * (4 * q + j)
                    mm = nc.tensor.transpose(p_t[:, j, :], agg2[:, t:t + 2, :].rearrange("p t w -> p (t w)"), m["ident"][:])
                mm.then_inc(t2_in, 1)

            for turn in pipeline(pe, NC, LO):
                a, b, g2, g, o = (turn.chunk(lag, NC) for lag in (0, LB, LT, LM, LO))
                if g:
                    first(g, 0, 0)
                if o:
                    pe.wait_ge(h5_in, 2 * o[0] + 2)
                    since(pe, res_in, o[0])
                    pe.wait_ge(tu0_in, b[0] + 1 if b else NC)
                    for j in range(HG):
                        mm = mmul(p_o[:, j * D2:(j + 1) * D2], h5[:, j * P:(j + 1) * P], wl3[:], start=True, stop=True)
                    mm.then_inc(o_in, 1)
                if g2:
                    turn2(g2, 0)
                if g:
                    first(g, 1, 0)
                    second(g, 0, 0)
                if g2:
                    turn2(g2, 1)
                if g:
                    second(g, 1, 0)
                    first(g, 0, 1)
                if b:
                    pe.wait_ge(agg1_in, b[0] + 1)
                    since(pe, tu2_in, 2 * b[0])
                    since(pe, l2_read, len(groups1) * b[0])
                    for q, (t, n) in enumerate(groups1):
                        mm = nc.tensor.transpose(p_t[0:n * D2, q, :] if q < 4 else t1_last, agg1[:, t:t + n, :].rearrange("p t w -> p (t w)"), m["ident"][:])
                    mm.then_inc(t1_in, 1)
                if g:
                    third(g, 0)
                    first(g, 1, 1)
                    second(g, 0, 1)
                if b:
                    pe.wait_ge(tu1_in, b[0] + 1)
                    for q, (t, n) in enumerate(groups1):
                        mm = mmul(l2_at(q, n), tu1[:, q, :], w2[:, 0:n * D4], start=True, stop=True)
                    mm.then_inc(l2_in, 1)
                if g:
                    second(g, 1, 1)
                if a:
                    pe.wait_ge(agg0_in, a[0] + 1)
                    pe.wait_ge(tu0_in, a[0])
                    if o:
                        pe.wait_ge(res_in, o[0] + 1)
                    for q in range(2):
                        mm = nc.tensor.transpose(p_t0[:, q, :], agg0[:, q * TG:(q + 1) * TG, :].rearrange("p t w -> p (t w)"), m["ident"][:])
                    mm.then_inc(t0_in, 1)
                if g:
                    third(g, 1)
                if a:
                    pe.wait_ge(tu0_in, a[0] + 1)
                    pe.wait_ge(l1_read, a[0])
                    for q in range(2):
                        mm = mmul(p_l1[:, q * TG * D2:(q + 1) * TG * D2], tu0[:, q, :], w1[:], start=True, stop=True)
                    mm.then_inc(l1_in, 1)

        @block.scalar
        def _(act):
            relu = lambda o, i, bias: nc.scalar.activation(o, i, ACT.Relu, bias=bias)
            act.wait_ge(consts, len(loads) * DMA)
            act.wait_ge(ready, 3)

            def out3(g, par, half):
                act.wait_ge(c_in, 4 * g[0] + 2 * half + par + 1)
                relu(h3[:, par, half], p_c[:, 0:HALF], b3[:]).then_inc(h3_in, 1)

            def out4(g, half):
                act.wait_ge(d_in, 2 * g[0] + half + 1)
                relu(h4[:, half], p_d[:, 0:HALF], bl1[:]).then_inc(h4_in, 1)

            def out5(g, half):
                act.wait_ge(e_in, 2 * g[0] + half + 1)
                relu(h5[0:D4, half * HALF:(half + 1) * HALF], p_e[:, 0:HALF], bl2[:]).then_inc(h5_in, 1)

            def copy2(g, q):
                c, m4, k4, m2, k2 = g
                n = 4 if q == 0 else 3
                act.wait_ge(t2_in, 2 * c + q + 1)
                nc.scalar.copy(tu2[:, k2, q * 4 * P:(q * 4 + n) * P], p_t[:, 0:n, :].rearrange("p j x -> p (j x)")).then_inc(tu2_in, 1)

            for turn in pipeline(act, NC, LM):
                a, b, g2, g = turn.chunk(0, NC), turn.chunk(LB, NC), turn.chunk(LT, NC), turn.chunk(LM, NC)
                if g:
                    out3(g, 0, 0)
                if g2:
                    copy2(g2, 0)
                if g:
                    out3(g, 1, 0)
                if g2:
                    copy2(g2, 1)
                if g:
                    out3(g, 0, 1)
                    out4(g, 0)
                if b:
                    act.wait_ge(t1_in, b[0] + 1)
                    nl = groups1[-1][1]
                    nc.scalar.copy(tu1[0:n1 * D2, 0:4, :], p_t[0:n1 * D2])
                    nc.scalar.copy(tu1[0:nl * D2, 4, :], t1_last).then_inc(tu1_in, 1)
                if a:
                    act.wait_ge(var_in, a[0] + 1)
                    nc.scalar.activation(root[:], var[:], ACT.Sqrt).then_inc(root_in, 1)
                if g:
                    out3(g, 1, 1)
                    out5(g, 0)
                    out4(g, 1)
                if a:
                    act.wait_ge(t0_in, a[0] + 1)
                    nc.scalar.copy(tu0[0:TG * D], p_t0).then_inc(tu0_in, 1)
                if g:
                    out5(g, 1)

        @block.vector
        def _(v):
            tt, stt = nc.vector.tensor_tensor, nc.vector.scalar_tensor_tensor
            nc.vector.memset(tu0[:], 1.0).then_inc(ready, 1)
            nc.vector.memset(tu1[:], 1.0).then_inc(ready, 1)
            nc.vector.memset(h5[:], 1.0).then_inc(ready, 1)
            v.sem_inc(used, 4)
            st = Steps(v, own, STEPS_NG)
            for turn in pipeline(v, NC, LO, st):
                if ch := turn.chunk(LC, NC):
                    c, m4, k4, m2, k2 = ch
                    v.wait_ge(l2_in, c + 1)
                    for q, (t, n) in enumerate(groups1):
                        o = l2_at(q, n).rearrange("p (t w) -> p t w", w=D4)
                        stt(y2[:, t:t + n, :], o, 0.0, over(ndinv[:, cols(c * G + t, n)], D4), ALU.max, ALU.mult).then_inc(l2_read, 1)
                    v.wait_ge(l2_read, len(groups1) * (c + 1))
                    tt(a2[:], y2[:], f[:, k4, :, 4 * D:8 * D], ALU.add).then_inc(used, 1)
                    v.wait_ge(used, c + 5)
                    tt(agg2[:], a2[:], over(ndinv[:, tiles(c)], D4), ALU.mult).then_inc(agg2_in, 1)
                if ch := turn.chunk(LO, NC):
                    c, m4, k4, m2, k2 = ch
                    v.wait_ge(o_in, c + 1)
                    v.wait_ge(res_out[k2], m2 * DMA)
                    stt(res[:, k2], p_o.rearrange("p (t w) -> p t w", w=D), 0.0, nbase[:, tiles(c), :], ALU.max, ALU.add).then_inc(res_in, 1)
                if ch := turn.chunk(LB, NC):
                    c, m4, k4, m2, k2 = ch
                    v.wait_ge(l1_in, c + 1)
                    stt(y1[:], p_l1[:, 0:G * D2].rearrange("p (t w) -> p t w", w=D2), 0.0, over(ndinv[:, tiles(c)], D2),
                        ALU.max, ALU.mult).then_inc(l1_read, 1)
                    v.wait_ge(l1_read, c + 1)
                    st.did(tt(a1[:], y1[:], f[:, k4, :, 2 * D:4 * D], ALU.add))
                    st.wait()
                    tt(agg1[:], a1[:], over(ndinv[:, tiles(c)], D2), ALU.mult).then_inc(agg1_in, 1)
                if ch := turn.chunk(0, NC):
                    c, m4, k4, m2, k2 = ch
                    x3 = nbase[:, tiles(c), :]
                    v.wait_ge(f_in[k4], (m4 + 1) * DMA)
                    st.did(tt(x3, nbase[:, tiles(c), :], f[:, k4, :, 0:D], ALU.add))
                    st.wait()
                    settle(core, v)
                    centre(nc, st, x3, xc[:], sq[:], s[:], var[:], var_in)
                    v.wait_ge(root_in, c + 1)
                    scale_relu(nc, st, root[:], rs[:], xc[:], h[:])
                    st.wait()
                    st.did(tt(y0[:], h[:], over(ndinv[:, tiles(c)], D), ALU.mult))
                    st.wait()
                    st.did(tt(a0[:], y0[:], f[:, k4, :, D:2 * D], ALU.add))
                    st.wait()
                    tt(agg0[:], a0[:], over(ndinv[:, tiles(c)], D), ALU.mult).then_inc(agg0_in, 1)


STEPS_FT, STEPS_AT, STEPS_MS, STEPS_GF, STEPS_NB, STEPS_NG = 6, 14, 114, 14, 34, 40

INPUTS = ("x", "src_s", "dst_s", "next_s", "src_b", "dst_ext", "src_rows", "ef_t", "ea_t", "wgt", "w_att", "root_w",
          "edge_w", "w1", "b1", "w2", "b2", "w1b", "w2b", "w3", "b3", "wl1", "bl1", "wl2", "bl2", "wl3", "ident", "sel", "before",
          "one_only", "pos_b", "pos1_s", "dump")


def gnn(nc, io, out):
    dram = lambda name, shape, dt=F32: nc.dram_tensor(name, shape, dt).ap()
    d = dict(xh=dram("x_and_h", [NP, 2 * D]), xs=dram("xs_rows", [EP, D]), xd=dram("xd_rows", [EP, D]), t0=dram("t0_rows", [EP, D]),
             pen=dram("pen_row", [EP], BF16), cnt=dram("cnt_row", [EP]),
             a0=dram("att_nodes", [NP, A0W]), a1=dram("l1_nodes", [NP + HG * P, D]), f=dram("final_nodes", [NP, FW]),
             t2=dram("t2_rows", [EP + 1, D]), t3a=dram("t3a_rows", [EP + 1, D]),
             t3b=dram("t3b_rows", [EP + 1, 2 * D]), t3c=dram("t3c_rows", [EP + 1, 4 * D]))
    with ExitStack() as top:
        core = Core(nc)
        sb = lambda name, shape, dt=F32, ctx=top: ctx.enter_context(nc.sbuf_tensor(name, shape, dt))
        m = dict(ident=sb("ident", [P, P]), starts_not=sb("starts_not", [P, ET]), ends=sb("ends", [P, ET]),
                 ends_not=sb("ends_not", [P, ET]), cntpos_s=sb("cntpos_s", [P, ET, 2]),
                 end_s=sb("end_s", [P, ET], I32), end_b=sb("end_b", [P, ET], I32))
        lanes = Lanes(nc, sb, m["ident"])
        setup(core, io, d, lanes, m)
        core.end_stage()
        features(core, io, d)
        core.end_stage()
        attention(core, io, d, m)
        core.end_stage()
        with ExitStack() as edge:
            qf, dinv = sb("qf", [P, ET], ctx=edge), sb("dinv", [P, ET], ctx=edge)
            y1 = sb("y1", [P, ET, 2 * D], ctx=edge)
            with ExitStack() as c0:
                y0 = sb("y0", [P, ET, D], ctx=c0)
                with ExitStack() as c1:
                    base = sb("base", [P, ET, D], ctx=c1)
                    message_sum(core, io, d, m, lanes, base, qf, dinv, y0)
                    core.end_stage()
                    edge_layer(core, io, d, m, lanes, base)
                    core.end_stage()
                    gcn_first(core, io, d, m, lanes, base, qf, dinv, y0)
                    core.end_stage()
                with ExitStack() as c2:
                    sums = sb("y1_sums", [P, ET, 2 * D], ctx=c2)
                    gcn_next(core, io, d, m, lanes, D, io["w1"], io["b1"], d["t3a"], d["t3b"], y0, y1, sums, qf, dinv)
                    core.end_stage()
            with ExitStack() as c3:
                y2 = sb("y2", [P, ET, 4 * D], ctx=c3)
                gcn_next(core, io, d, m, lanes, 2 * D, io["w2"], io["b2"], d["t3b"], d["t3c"], y1, y2, y2, qf, dinv)
                core.end_stage()
        with ExitStack() as ctx:
            nbase, ndinv = sb("node_base", [P, NT, D], ctx=ctx), sb("node_dinv", [P, NT], ctx=ctx)
            node_base(core, io, d, m, nbase, ndinv)
            core.end_stage()
            node_gcn(core, io, d, m, nbase, ndinv, out)
            core.end_stage()


def kernel(**inputs):
    import numpy as _np
    import ml_dtypes as _ml
    import concourse.bacc as _bacc
    from concourse import mybir as _mybir
    from concourse.bass_utils import run_bass_kernel_spmd as _run

    a = {k: _np.asarray(v) for k, v in inputs.items()}

    def padded(x, n, value=0):
        out = _np.full((n,) + x.shape[1:], value, x.dtype)
        out[:x.shape[0]] = x
        return out

    def diagonal(w, n):
        out = _np.zeros((n * w.shape[0], n * w.shape[1]), w.dtype)
        for q in range(n):
            out[q * w.shape[0]:(q + 1) * w.shape[0], q * w.shape[1]:(q + 1) * w.shape[1]] = w
        return out

    strided = lambda x: x.reshape(ET, P).T
    blocked = lambda x: x.reshape((P, ET) + x.shape[1:])
    row = lambda x: x[None, :]
    src = padded(a["src"].astype(_np.int32), EP, N + 1)
    dst = padded(a["dst"].astype(_np.int32), EP, N)
    dst_ext = _np.concatenate([_np.full(1, -1, _np.int32), dst, _np.full(1, -1, _np.int32)])
    ones = _np.ones((1, EP), _np.float32)
    pos = _np.arange(EP, dtype=_np.float32)
    io = dict(
        x=padded(a["x"], NP), src_s=strided(src), dst_s=strided(dst), next_s=strided(dst_ext[2:]), src_b=blocked(src),
        dst_ext=dst_ext, src_rows=row(blocked(src).T.reshape(-1)), 
        ef_t=_np.concatenate([padded(a["edge_attr_16"], EP).T, ones]),
        ea_t=_np.concatenate([blocked(padded(a["edge_attr_8"], EP)).transpose(2, 1, 0), _np.ones((1, ET, P), _np.float32)]),
        wgt=blocked(padded(a["edge_weight"], EP)),
        w_att=_np.concatenate([_np.concatenate([a["L0_gnn_W_attn"], a["L0_gnn_W_msg"]], 1),
                               row(_np.concatenate([a["L0_gnn_b_attn"], a["L0_gnn_b_msg"]]))]),
        root_w=_np.concatenate([diagonal(a["L2_gnn_root_w"], TG), row(_np.tile(a["L2_gnn_root_b"], TG))]),
        edge_w=_np.concatenate([a["L2_gnn_edge_w"], row(a["L2_gnn_edge_b"])]),
        w1=diagonal(a["L3_gnn_W1"], TG), b1=row(_np.tile(a["L3_gnn_b1"], TG)),
        w2=diagonal(a["L3_gnn_W2"], 4), b2=row(_np.tile(a["L3_gnn_b2"], 4)),
        w1b=_np.concatenate([diagonal(a["L3_gnn_W1"], TG), row(_np.tile(a["L3_gnn_b1"], TG))]),
        w2b=_np.concatenate([diagonal(a["L3_gnn_W2"], 3), row(_np.tile(a["L3_gnn_b2"], 3))]),
        w3=_np.tile(a["L3_gnn_W3"], (2, 1)), b3=a["L3_gnn_b3"][:, None],
        wl1=a["L3_gnn_Wl1"], bl1=_np.tile(a["L3_gnn_bl1"], 2)[:, None],
        wl2=diagonal(a["L3_gnn_Wl2"], 2), bl2=_np.tile(a["L3_gnn_bl2"], 2)[:, None],
        wl3=_np.concatenate([diagonal(a["L3_gnn_Wl3"], 2), row(_np.tile(a["L3_gnn_bl3"], 2))]),
        ident=_np.eye(P, dtype=_np.float32), sel=_np.tile(_np.eye(D, dtype=_np.float32), (P // D, 1)),
        before=_np.repeat(_np.triu(_np.ones((P, P)), 1).astype(_ml.bfloat16)[:, None, :], HG, 1),
        one_only=_np.repeat(_np.eye(1, 3 * D + 1).astype(_ml.bfloat16), P, 0),
        pos_b=blocked(pos), pos1_s=strided(pos + 1),
        dump=(NP + _np.arange(HG)[None, :] * P + _np.arange(P)[:, None]).astype(_np.float32))
    nc = _bacc.Bacc("TRN2", target_bir_lowering=False, num_devices=1)
    arrays, aps = {}, {}
    for name in INPUTS:
        arr = _np.ascontiguousarray(io[name])
        arrays[f"in_{name}"] = arr
        aps[name] = nc.dram_tensor(f"in_{name}", arr.shape, _mybir.dt.from_np(arr.dtype), kind="ExternalInput").ap()
    out = nc.dram_tensor("out_rows", (NP, D), F32, kind="ExternalOutput").ap()
    gnn(nc, aps, out)
    r = _run(nc, [arrays], core_ids=[0])
    return r.results[0]["out_rows"][:N]
```
